# Optimizing a Trainium2 kernel written in Bass

```python
import numpy as np
import jax
import jax.numpy as jnp

def _softmax(x, axis=-1):
    return jax.nn.softmax(x, axis=axis)

def _gelu(x):
    return jax.nn.gelu(x, approximate=True)

def _silu(x):
    return jax.nn.silu(x)

def _sigmoid(x):
    return jax.nn.sigmoid(x)

def _layernorm(x, axis=-1, eps=1e-05):
    m = jnp.mean(x, axis=axis, keepdims=True)
    v = jnp.var(x, axis=axis, keepdims=True)
    return (x - m) / jnp.sqrt(v + eps)

def _scatter_add(tgt, idx, src, axis=0):
    return tgt.at[idx].add(src)

def _segment_sum(src, seg, n):
    return jax.ops.segment_sum(src, seg, n)
kernel_name = 'mk_flamingo_gated_d2_seqx_r4_7cd9c4'

def setup_inputs(seed: int=0):
    np.random.seed(seed)
    _w = jnp.asarray

    def _rec_inputs():
        import jax
        import jax.numpy as jnp
        _rk = jax.random.key(seed)
        x = 4.136e-05 + 0.9999 * jax.random.normal(jax.random.fold_in(_rk, 1), (8, 256, 256), jnp.float32)
        _lenS = 256 - jax.random.randint(jax.random.fold_in(_rk, 7), (8,), 0, max(1, 256 // 4) + 1, jnp.int32)
        _lenS2 = 256 - jax.random.randint(jax.random.fold_in(_rk, 8), (8,), 0, max(1, 256 // 4) + 1, jnp.int32)
        _ctx_2048P = jax.random.normal(jax.random.fold_in(_rk, 11), (8, 16, 512), jnp.float32)
        _ctx_2048c = jax.random.dirichlet(jax.random.fold_in(_rk, 511), 0.3 * jnp.ones((16,), jnp.float32), (8, 256))
        _ctx_2048t = jnp.einsum('bsk,bkd->bsd', _ctx_2048c, _ctx_2048P)
        _ctx_2048t = _ctx_2048t * jax.lax.rsqrt(jnp.mean(jnp.square(_ctx_2048t)) + 1e-12) * 0.953939
        ctx_2048 = -0.000392918 + 0.999932 * (_ctx_2048t + 0.3 * jax.random.normal(jax.random.fold_in(_rk, 611), (8, 256, 512), jnp.float32))
        itok_Bx1_68_817 = jax.random.randint(jax.random.fold_in(_rk, 12), (8, 1), 68, 818, jnp.int32)
        _validS = jnp.arange(256)[None, :] < _lenS[:, None]
        _validS2 = jnp.arange(256)[None, :] < _lenS2[:, None]
        _causal = jnp.tril(jnp.ones((256, 256), dtype=bool))
        mask_BxS2_fk1 = jnp.where(jnp.broadcast_to(_validS2[:, :], (8, 256)), 1.0, 0.0).astype(jnp.float32)
        _g = jax.random.normal(jax.random.fold_in(_rk, 9001), (2, 2), jnp.float32)
        _g = jnp.sign(_g) * jnp.maximum(jnp.abs(_g), 1.0) + (_g == 0) * 1.0
        g_xattn = _g[0]
        g_ffn = _g[1]
        return (x, ctx_2048, itok_Bx1_68_817, mask_BxS2_fk1, g_xattn, g_ffn)
    x, ctx_2048, itok_Bx1_68_817, mask_BxS2_fk1, g_xattn, g_ffn = _rec_inputs()

    def _L0_xattn_setup():
        import jax, jax.numpy as jnp
        import numpy as np
        UNITS = 256
        NUM_HEADS = 16
        MASK_VALUE = -1000000000000.0

        def _split_heads(x, n):
            B, S, D = x.shape
            return x.reshape(B, S, n, D // n).transpose(0, 2, 1, 3)
        key = jax.random.key(seed)
        k1, k2, k3, k4 = jax.random.split(key, 4)
        B, S = (8, 256)
        memory = jax.random.normal(k1, (B, S, 2 * UNITS), dtype=jnp.float32)
        query = jax.random.normal(k2, (B, S, UNITS), dtype=jnp.float32)
        b = jax.random.normal(k3, (S,), dtype=jnp.float32)
        seq_len = jax.random.randint(k4, (B, 1), 0, S, dtype=jnp.int32)
        return {'memory': memory, 'query': query, 'b': b, 'seq_len': seq_len}
    _L0_xattn_all = _L0_xattn_setup()
    _L0_xattn_in = {k: v for k, v in _L0_xattn_all.items() if k in ('b',)}
    del _L0_xattn_all

    def _L0_ffn_setup():
        import jax, jax.numpy as jnp
        import numpy as np
        B, S, H, E = (4, 512, 256, 8)
        key = jax.random.key(seed)
        k1, k2, k3 = jax.random.split(key, 3)
        scale_w = 1.0 / np.sqrt(H)
        return {'x': jax.random.normal(k1, (B, S, H), dtype=jnp.float32), 'router_w': jax.random.normal(k2, (H, E), dtype=jnp.float32) * scale_w, 'router_b': jnp.zeros((E,), dtype=jnp.float32), 'expert_w': jax.random.normal(k3, (E, H, H), dtype=jnp.float32) * scale_w, 'expert_b': jnp.zeros((E, H), dtype=jnp.float32)}
    _L0_ffn_all = _L0_ffn_setup()
    _L0_ffn_in = {k: v for k, v in _L0_ffn_all.items() if k in ('router_w', 'router_b', 'expert_w', 'expert_b')}
    del _L0_ffn_all

    def _L1_xattn_setup():
        import jax, jax.numpy as jnp
        import numpy as np
        B, S, T = (32, 128, 128)
        SRC_SIZE, TGT_SIZE, OUT_SIZE, NUM_HEAD = (512, 256, 256, 8)
        HEAD_DIM = OUT_SIZE // NUM_HEAD
        key = jax.random.key(seed)
        ks = jax.random.split(key, 12)
        src = jax.random.normal(ks[0], (B, S, SRC_SIZE), dtype=jnp.float32)
        tgt = jax.random.normal(ks[1], (B, T, TGT_SIZE), dtype=jnp.float32)
        src_mask = (jax.random.uniform(ks[2], (B, S)) > 0.3).astype(jnp.float32)
        src_mask = src_mask.at[:, 0].set(1.0)
        tgt_mask = (jax.random.uniform(ks[3], (B, T)) > 0.3).astype(jnp.float32)
        tgt_mask = tgt_mask.at[:, 0].set(1.0)

        def lin(k, out_f, in_f):
            return jax.random.normal(k, (out_f, in_f), dtype=jnp.float32) / np.sqrt(in_f)
        W_src = lin(ks[4], 2 * OUT_SIZE, SRC_SIZE)
        b_src = jnp.zeros((2 * OUT_SIZE,), jnp.float32)
        W_tgt = lin(ks[5], OUT_SIZE, TGT_SIZE)
        b_tgt = jnp.zeros((OUT_SIZE,), jnp.float32)
        W_out = lin(ks[6], OUT_SIZE, OUT_SIZE + TGT_SIZE)
        b_out = jnp.zeros((OUT_SIZE,), jnp.float32)
        return {'src': src, 'tgt': tgt, 'src_mask': src_mask, 'tgt_mask': tgt_mask, 'W_src': W_src, 'b_src': b_src, 'W_tgt': W_tgt, 'b_tgt': b_tgt, 'W_out': W_out, 'b_out': b_out}
    _L1_xattn_all = _L1_xattn_setup()
    _L1_xattn_in = {k: v for k, v in _L1_xattn_all.items() if k in ('W_src', 'b_src', 'W_tgt', 'b_tgt', 'W_out', 'b_out')}
    del _L1_xattn_all

    def _L1_ffn_setup():
        import jax, jax.numpy as jnp
        import numpy as np
        TOPK = 8
        NUM_EXPERTS = 64
        FFN = 768
        CAPACITY = 160

        def _swiglu(x, w1, w2):
            h = x @ w1.T
            x1, x2 = jnp.split(h, 2, axis=-1)
            return x1 * jax.nn.silu(x2) @ w2.T
        key = jax.random.key(seed)
        ks = jax.random.split(key, 6)
        B, S, H = (1, 128, 256)
        scale = 0.02
        return {'hidden_states': jax.random.normal(ks[0], (B, S, H), jnp.float32), 'wg': jax.random.normal(ks[1], (NUM_EXPERTS, H), jnp.float32) * scale, 'shared_w1': jax.random.normal(ks[2], (2 * FFN, H), jnp.float32) * scale, 'shared_w2': jax.random.normal(ks[3], (H, FFN), jnp.float32) * scale, 'expert_w1': jax.random.normal(ks[4], (NUM_EXPERTS, 2 * FFN, H), jnp.float32) * scale, 'expert_w2': jax.random.normal(ks[5], (NUM_EXPERTS, H, FFN), jnp.float32) * scale}
    _L1_ffn_all = _L1_ffn_setup()
    _L1_ffn_in = {k: v for k, v in _L1_ffn_all.items() if k in ('wg', 'shared_w1', 'shared_w2', 'expert_w1', 'expert_w2')}
    del _L1_ffn_all
    return {'x': x, 'ctx_2048': ctx_2048, 'itok_Bx1_68_817': itok_Bx1_68_817, 'mask_BxS2_fk1': mask_BxS2_fk1, 'g_xattn': g_xattn, 'g_ffn': g_ffn, 'L0_xattn_b': _L0_xattn_in['b'], 'L0_ffn_router_w': _L0_ffn_in['router_w'], 'L0_ffn_router_b': _L0_ffn_in['router_b'], 'L0_ffn_expert_w': _L0_ffn_in['expert_w'], 'L0_ffn_expert_b': _L0_ffn_in['expert_b'], 'L1_xattn_W_src': _L1_xattn_in['W_src'], 'L1_xattn_b_src': _L1_xattn_in['b_src'], 'L1_xattn_W_tgt': _L1_xattn_in['W_tgt'], 'L1_xattn_b_tgt': _L1_xattn_in['b_tgt'], 'L1_xattn_W_out': _L1_xattn_in['W_out'], 'L1_xattn_b_out': _L1_xattn_in['b_out'], 'L1_ffn_wg': _L1_ffn_in['wg'], 'L1_ffn_shared_w1': _L1_ffn_in['shared_w1'], 'L1_ffn_shared_w2': _L1_ffn_in['shared_w2'], 'L1_ffn_expert_w1': _L1_ffn_in['expert_w1'], 'L1_ffn_expert_w2': _L1_ffn_in['expert_w2']}

def reference(x, ctx_2048, itok_Bx1_68_817, mask_BxS2_fk1, g_xattn, g_ffn, L0_xattn_b, L0_ffn_router_w, L0_ffn_router_b, L0_ffn_expert_w, L0_ffn_expert_b, L1_xattn_W_src, L1_xattn_b_src, L1_xattn_W_tgt, L1_xattn_b_tgt, L1_xattn_W_out, L1_xattn_b_out, L1_ffn_wg, L1_ffn_shared_w1, L1_ffn_shared_w2, L1_ffn_expert_w1, L1_ffn_expert_w2):
    import jax
    import jax.numpy as jnp

    def _L0_xattn_ref(memory, query, b, seq_len):
        import jax, jax.numpy as jnp
        import numpy as np
        UNITS = 256
        NUM_HEADS = 16
        MASK_VALUE = -1000000000000.0

        def _split_heads(x, n):
            B, S, D = x.shape
            return x.reshape(B, S, n, D // n).transpose(0, 2, 1, 3)
        B, S, _ = query.shape
        dh = UNITS // NUM_HEADS
        k_mem, v_mem = jnp.split(memory, 2, axis=2)
        Q = _split_heads(query, NUM_HEADS) * dh ** (-0.5)
        Kh = _split_heads(k_mem, NUM_HEADS)
        Vh = _split_heads(v_mem, NUM_HEADS)
        logits = jnp.einsum('bhqd,bhkd->bhqk', Q, Kh) + b
        valid = (jnp.arange(S)[None, :] < seq_len[:, 0:1]).astype(jnp.float32)
        logits = logits + MASK_VALUE * (1.0 - valid)[:, None, None, :]
        weights = jax.nn.softmax(logits, axis=-1)
        out = jnp.einsum('bhqk,bhkd->bhqd', weights, Vh)
        return out.transpose(0, 2, 1, 3).reshape(B, S, UNITS)

    def _L0_ffn_ref(x, router_w, router_b, expert_w, expert_b):
        import jax, jax.numpy as jnp
        import numpy as np
        B, S, H, E = (4, 512, 256, 8)
        b, s, h = x.shape
        xt = x.reshape(b * s, h)
        logits = xt @ router_w + router_b
        probs = jax.nn.softmax(logits, axis=-1)
        gate = jnp.max(probs, axis=-1)
        idx = jnp.argmax(probs, axis=-1)
        out_all = jnp.einsum('th,ehd->ted', xt, expert_w) + expert_b[None, :, :]
        e_out = jnp.take_along_axis(out_all, idx[:, None, None], axis=1)[:, 0, :]
        y = gate[:, None] * e_out
        return y.reshape(b, s, h)

    def _L1_xattn_ref(src, tgt, src_mask, tgt_mask, W_src, b_src, W_tgt, b_tgt, W_out, b_out):
        import jax, jax.numpy as jnp
        import numpy as np
        B, S, T = (32, 128, 128)
        SRC_SIZE, TGT_SIZE, OUT_SIZE, NUM_HEAD = (512, 256, 256, 8)
        HEAD_DIM = OUT_SIZE // NUM_HEAD
        b, s, _ = src.shape
        t = tgt.shape[1]
        src_trans = jnp.einsum('bsf,of->bso', src, W_src) + b_src
        tgt_trans = jnp.einsum('btf,of->bto', tgt, W_tgt) + b_tgt
        src_trans = src_trans * src_mask[:, :, None]
        tgt_trans = tgt_trans * tgt_mask[:, :, None]
        src_key, src_val = jnp.split(src_trans, 2, axis=2)
        k = src_key.reshape(b, s, NUM_HEAD, HEAD_DIM)
        v = src_val.reshape(b, s, NUM_HEAD, HEAD_DIM)
        q = tgt_trans.reshape(b, t, NUM_HEAD, HEAD_DIM)
        scores = jnp.einsum('bthd,bshd->bhts', q, k) / np.sqrt(HEAD_DIM)
        scores = jnp.where(src_mask[:, None, None, :] == 0, -jnp.inf, scores)
        attn = jax.nn.softmax(scores, axis=-1)
        tgt_update = jnp.einsum('bhts,bshd->bthd', attn, v).reshape(b, t, OUT_SIZE)
        cat_tgt = jnp.concatenate([tgt, tgt_update], axis=2)
        return jnp.einsum('btf,of->bto', cat_tgt, W_out) + b_out

    def _L1_ffn_ref(hidden_states, wg, shared_w1, shared_w2, expert_w1, expert_w2):
        import jax, jax.numpy as jnp
        import numpy as np
        TOPK = 8
        NUM_EXPERTS = 64
        FFN = 768
        CAPACITY = 160

        def _swiglu(x, w1, w2):
            h = x @ w1.T
            x1, x2 = jnp.split(h, 2, axis=-1)
            return x1 * jax.nn.silu(x2) @ w2.T
        B, S, H = hidden_states.shape
        T = B * S
        x = hidden_states.reshape(T, H)
        shared_out = _swiglu(x, shared_w1, shared_w2)
        logits = x.astype(jnp.float32) @ wg.T
        gates = jax.nn.softmax(logits, axis=-1)
        w_topk, idx_topk = jax.lax.top_k(gates, TOPK)
        denom = jnp.maximum(w_topk.sum(-1, keepdims=True), jnp.finfo(jnp.float32).eps)
        w_topk = w_topk / denom
        A = T * TOPK
        flat_e = idx_topk.reshape(A)
        flat_w = w_topk.reshape(A)
        flat_t = jnp.repeat(jnp.arange(T), TOPK)
        order = jnp.argsort(flat_e)
        se, st, sw = (flat_e[order], flat_t[order], flat_w[order])
        counts = jnp.zeros(NUM_EXPERTS, jnp.int32).at[flat_e].add(1)
        starts = jnp.cumsum(counts) - counts
        rank = jnp.arange(A) - starts[se]
        valid = rank < CAPACITY
        buf = jnp.zeros((NUM_EXPERTS, CAPACITY, H), x.dtype).at[se, rank].set(x[st], mode='drop')
        h = jnp.einsum('ech,efh->ecf', buf, expert_w1)
        x1, x2 = jnp.split(h, 2, axis=-1)
        out = jnp.einsum('ecf,ehf->ech', x1 * jax.nn.silu(x2), expert_w2)
        y = out[se, jnp.clip(rank, 0, CAPACITY - 1)]
        y = jnp.where(valid[:, None], y * sw[:, None].astype(y.dtype), 0.0)
        combined = jnp.zeros((T, H), x.dtype).at[st].add(y)
        return (shared_out + combined).reshape(B, S, H)
    x = x + jnp.tanh(g_xattn[0]) * _L0_xattn_ref(ctx_2048, _layernorm(x, axis=-1), L0_xattn_b, itok_Bx1_68_817)
    x = x + jnp.tanh(g_ffn[0]) * _L0_ffn_ref(_layernorm(x, axis=-1), L0_ffn_router_w, L0_ffn_router_b, L0_ffn_expert_w, L0_ffn_expert_b)
    x = x + jnp.tanh(g_xattn[1]) * _L1_xattn_ref(ctx_2048, _layernorm(x, axis=-1), mask_BxS2_fk1, mask_BxS2_fk1, L1_xattn_W_src, L1_xattn_b_src, L1_xattn_W_tgt, L1_xattn_b_tgt, L1_xattn_W_out, L1_xattn_b_out)
    x = x + jnp.tanh(g_ffn[1]) * _L1_ffn_ref(_layernorm(x, axis=-1), L1_ffn_wg, L1_ffn_shared_w1, L1_ffn_shared_w2, L1_ffn_expert_w1, L1_ffn_expert_w2)
    return x

_drawn_inputs = setup_inputs


def setup_inputs(seed=0):
    import zlib

    import numpy as np

    out = dict(_drawn_inputs(seed))
    spreads = {'g_ffn': (-1.0, 0.6),
     'L0_ffn_router_b': (0.0, 0.1),
     'L0_ffn_expert_b': (0.0, 0.321),
     'L1_xattn_b_src': (0.0, 0.1),
     'L1_xattn_b_tgt': (0.0, 0.8),
     'L1_xattn_b_out': (0.0, 0.1)}
    factors = {'L1_ffn_wg': 8.0,
     'L1_ffn_shared_w1': 3.179,
     'L1_ffn_shared_w2': 3.165,
     'L1_ffn_expert_w1': 8.0,
     'L1_ffn_expert_w2': 8.0}
    for name, (base, spread) in spreads.items():
        noise = np.random.default_rng([zlib.crc32(name.encode()), seed]).standard_normal(out[name].shape)
        drawn = base * np.exp(spread * noise) if base else spread * noise
        out[name] = jnp.asarray(drawn.astype(out[name].dtype))
    for name, factor in factors.items():
        out[name] = (out[name] * factor).astype(out[name].dtype)
    return out
```

```python
from contextlib import ExitStack

import concourse.bass as bass
from concourse import mybir

F32 = mybir.dt.float32
BF16 = mybir.dt.bfloat16
I32 = mybir.dt.int32
U32 = mybir.dt.uint32
ALU = mybir.AluOpType
ACT = mybir.ActivationFunctionType
AX = mybir.AxisListType
ds = bass.ds

P = 128
B, S, D = 8, 256, 256
CTX = 512
T = B * S // P
NT = B * S
QT = S // P
EPS = 1e-5
H0, DH0 = 16, 16
E0 = 8
H1, DH1 = 8, 32
E1, TOPK, FF, CAP = 64, 8, 768, 160
KF = FF // P
RA, RB = CAP // 16, 16
CAPX = CAP - P
ROW = D + E1
MASKED0 = -1e12
MASKED1 = -1e30
NEG = -3.0e38
WCOLS = 2 * 2 * FF + KF * D
RING = 4


class Shared:
    pass


class Chain:

    def __init__(self, eng, sem, per_step):
        self.eng, self.sem, self.per_step = eng, sem, per_step
        self.base = self.k = 0

    def step(self, n):
        self.base, self.k = n * self.per_step, 0

    def end(self):
        assert self.k == self.per_step, self.k

    def link(self, ins):
        ins.then_inc(self.sem, 1)
        self.k += 1
        self.eng.wait_ge(self.sem, self.base + self.k)


def steps(eng, n, body, slots=2):
    for k in range(slots):
        body(k, 0, k)
    with eng.Fori(1, n // slots - 1) as i:
        for k in range(slots):
            body(slots * i + k, i, k)
    for k in range(n - slots, n):
        body(k, n // slots - 1, k % slots)


def apart(eng):
    eng.nop(nofuse=True)


def setup(nc, g, a):
    with ExitStack() as ctx:
        def sb(name, shape, dt=F32):
            return ctx.enter_context(nc.sbuf_tensor(name, shape, dt))

        def sem(name):
            return ctx.enter_context(nc.semaphore(name))

        seq = sb("seq", [P, B], I32)
        seqf = sb("seqf", [P, B])
        bcol = sb("bcol", [P, QT])
        kpos = sb("kpos", [P, QT])
        valid = sb("valid", [P, QT, B])
        gates = sb("gates", [P, 4])
        bmrow = sb("bmrow", [B, S])
        st = sb("st_setup", [P, T, 6])
        maskrow = sb("maskrow", [1, B * S])
        x_in, small_in, iotas, masks_made, mask_turned, row_made, row_out, chain, rows_in = [
            sem(n) for n in ("x_in", "small_in", "iotas", "masks_made", "mask_turned", "row_made",
                             "row_out", "su_chain", "rows_in")]
        zeroed, consts = sem("zeroed"), sem("consts")
        aggr, var_eps, rooted, tanhs = sem("aggr"), sem("su_var_eps"), sem("su_rooted"), sem("tanhs")
        block = ctx.enter_context(nc.Block())

        @block.sync
        def _(sp):
            sp.dma_start(g.x[:, :, :], a["x"].rearrange("(t p) d -> p t d", p=P)).then_inc(x_in, 16)
            sp.dma_start(seq[:, :], a["seq"]).then_inc(small_in, 16)
            sp.dma_start(bcol[:, :], a["b"]).then_inc(small_in, 16)
            sp.dma_start(gates[:, :], a["gates"]).then_inc(small_in, 16)
            sp.dma_start(g.maskcol[:, :, :], a["maskcol"]).then_inc(small_in, 16)
            sp.wait_ge(row_made, QT)
            for r in range(4):
                sp.dma_start(g.bm_dram[:, r, :], bmrow[:, :]).then_inc(row_out, 16)
            for e in range(RING):
                sp.dma_start(g.wring[:, e, :], a["experts"][e]).then_inc(g.w_loaded[e], 16)
            sp.wait_ge(row_out, 64)

        @block.gpsimd
        def _(pool):
            nc.gpsimd.memset(g.ident[:, :], 0.0).then_inc(zeroed, 1)
            nc.gpsimd.memset(g.tri[:, :], 1.0).then_inc(zeroed, 1)
            nc.gpsimd.memset(g.ones_bf[:, :], 1.0).then_inc(zeroed, 1)
            nc.gpsimd.memset(g.esel[:, :, :], 1.0).then_inc(zeroed, 1)
            nc.gpsimd.memset(g.ones_f[:, :], 1.0).then_inc(zeroed, 1)
            nc.gpsimd.memset(g.row0_bf[:, :], 0.0).then_inc(zeroed, 1)
            nc.gpsimd.iota(kpos[:, :], [[P, QT]], 0, 1, allow_small_or_imprecise_dtypes=True).then_inc(iotas, 1)
            nc.gpsimd.iota(g.iota8[:, :], [[1, E0]], 0, 0, allow_small_or_imprecise_dtypes=True).then_inc(iotas, 1)
            nc.gpsimd.iota(g.iota_b[:, :], [[1, RB]], 0, 0, allow_small_or_imprecise_dtypes=True).then_inc(iotas, 1)
            nc.gpsimd.iota(g.iota_p[:, :], [[1, 1]], 0, 1, allow_small_or_imprecise_dtypes=True).then_inc(iotas, 1)
            nc.gpsimd.iota(g.iota_t[:, :], [[1, T]], 1, 0, allow_small_or_imprecise_dtypes=True).then_inc(iotas, 1)
            nc.gpsimd.iota(g.iota_slot[:, :], [[1, CAP]], NT, 0, allow_small_or_imprecise_dtypes=True).then_inc(iotas, 1)
            pool.wait_ge(zeroed, 6)
            nc.gpsimd.affine_select(out=g.ident[:, :], in_=g.ident[:, :], compare_op=ALU.not_equal, fill=1.0,
                                    base=0, pattern=[[-1, P]], channel_multiplier=1).then_inc(consts, 1)
            nc.gpsimd.affine_select(out=g.tri[:, :], in_=g.tri[:, :], compare_op=ALU.is_ge, fill=0.0,
                                    base=-1, pattern=[[1, P]], channel_multiplier=-1).then_inc(consts, 1)
            nc.gpsimd.affine_select(out=g.esel[:, :, :], in_=g.esel[:, :, :], compare_op=ALU.is_equal, fill=0.0,
                                    base=0, pattern=[[-1, H1], [0, P]], channel_multiplier=1).then_inc(consts, 1)
            nc.gpsimd.memset(g.row0_bf[0:1, :], 1.0).then_inc(consts, 1)
            pool.wait_ge(consts, 4)

        @block.vector
        def _(dve):
            ch = Chain(dve, chain, 4)
            dve.wait_ge(small_in, 64)
            dve.wait_ge(iotas, 6)
            ch.link(dve.tensor_copy(seqf[:, :], seq[:, :]))
            for k in range(QT):
                ins = dve.tensor_scalar(valid[:, k, :], seqf[:, :], kpos[:, k:k + 1], None, ALU.is_gt)
            ch.link(ins)
            ch.link(dve.tensor_scalar(valid[:, :, :], valid[:, :, :], -1.0, -MASKED0, ALU.add, ALU.mult))
            for k in range(QT):
                ins = dve.tensor_scalar(g.bm0[:, k, :], valid[:, k, :], bcol[:, k:k + 1], None, ALU.add)
            ins.then_inc(masks_made, 1)
            ch.link(dve.tensor_scalar(g.bm1[:, :, :], g.maskcol[:, :, :], 0.0, MASKED1, ALU.is_equal, ALU.mult))
            for k in range(QT):
                dve.wait_ge(mask_turned, k + 1)
                dve.tensor_copy(bmrow[:, k * P:(k + 1) * P], g.ps[0:B, k, 0:P]).then_inc(row_made, 1)
            dve.wait_ge(x_in, 16)
            for t in range(T):
                ins = dve.bn_stats(st[:, t, :], g.x[:, t, :])
            ins.then_inc(aggr, 1)
            dve.wait_ge(aggr, 1)
            for t in range(T):
                ins = dve.bn_aggr(g.mv[:, t, :], st[:, t, :])
            ins.then_inc(aggr, 1)
            dve.wait_ge(aggr, 2)
            ch.end()

        @block.tensor
        def _(pe):
            pe.wait_ge(consts, 1)
            pe.wait_ge(masks_made, 1)
            for k in range(QT):
                pe.transpose(g.ps[0:B, k, 0:P], g.bm0[:, k, :], g.ident[:, :]).then_inc(mask_turned, 1)

        @block.scalar
        def _(act):
            act.wait_ge(small_in, 64)
            act.activation(g.tg[:, :], gates[:, :], ACT.Tanh).then_inc(tanhs, 1)
            act.wait_ge(tanhs, 1)


def attn0(nc, g, a):
    G = H0 // 4
    with ExitStack() as ctx:
        def sb(name, shape, dt=F32):
            return ctx.enter_context(nc.sbuf_tensor(name, shape, dt))

        def sem(name):
            return ctx.enter_context(nc.semaphore(name))

        qpad = sb("qpad", [P, QT, H0, 32])
        kz = sb("kz", [P, 2, H0, S])
        kzb = sb("kzb", [P, 2, H0, S], BF16)
        vraw = sb("vraw", [P, 2, QT, D])
        vaug = sb("vaug", [P, 2, QT, H0, 32])
        qtb = sb("qtb", [P, G, S], BF16)
        qt = sb("qt", [P, 2, G, S])
        pt = sb("pt", [P, 2, QT, 2, S])
        ot = sb("ot", [P, G, S])
        rec = sb("rec", [P, QT, H0])
        upd = sb("upd", [P, QT, H0, DH0])
        st = sb("st0", [P, QT, 6])
        mvb = sb("mvb0", [P, QT, 2])
        kv_loaded = [sem(f"kv_loaded{s}") for s in (0, 1)]
        kb_loaded = [sem(f"kb_loaded{s}") for s in (0, 1)]
        padded, var_eps, rooted, scale_ready = sem("padded"), sem("a_var_eps"), sem("a_rooted"), sem("a_scale_ready")
        v_padded, q_ready, t1_done, qtb_ready = sem("v_padded"), sem("q_ready"), sem("t1_done"), sem("qtb_ready")
        max_ready, max_used, q2_ready, t2_done = sem("max_ready"), sem("max_used"), sem("q2_ready"), sem("t2_done")
        qt_ready, sc_ready, pt_ready, pv_done = sem("qt_ready"), sem("sc_ready"), sem("pt_ready"), sem("pv_done")
        ot_used, outt_done, fin_done, chain = sem("ot_used"), sem("outt_done"), sem("fin_done"), sem("a_chain")
        ps = g.ps
        TB, MB, SB, OB = 0, 2, 4, 7
        LOADS = 9
        block = ctx.enter_context(nc.Block())

        @block.sync
        def _(sp):
            def load(b, i, s):
                if not (isinstance(b, int) and b < 2):
                    sp.wait_ge(sc_ready, 16 * (b - 1))
                    sp.wait_ge(v_padded, b - 1)
                apart(sp)
                kt = a["ctx_t"][ds(b, 1), 0:D, :].rearrange("o (g j d) k -> j d (o g) k", j=4, d=DH0)
                bm = g.bm_dram[ds(b, 1), :, :]
                for j in range(4):
                    sp.dma_start(kz[32 * j + 2:32 * j + 2 + DH0, s, j:H0:4, :], kt[j]).then_inc(kv_loaded[s], 16)
                    sp.dma_start(kz[32 * j + 1:32 * j + 2, s, j:H0:4, :], bm).then_inc(kv_loaded[s], 16)
                sp.dma_start(vraw[:, s, :, :],
                             a["ctx"][ds(b, 1), :, D:2 * D].rearrange("o (k p) d -> p (o k) d", p=P)
                             ).then_inc(kv_loaded[s], 16)

            sp.wait_ge(padded, 10)
            steps(sp, B, load)

        @block.gpsimd
        def _(pool):
            nc.gpsimd.memset(qpad[:, :, :, :], 0.0).then_inc(padded, 1)
            nc.gpsimd.memset(vaug[:, :, :, :, :], 0.0).then_inc(padded, 1)
            nc.gpsimd.memset(kz[:, 0, :, :], 0.0).then_inc(padded, 1)
            nc.gpsimd.memset(kz[:, 1, :, :], 0.0).then_inc(padded, 1)
            nc.gpsimd.memset(kzb[:, :, :, :], 0.0).then_inc(padded, 1)
            pool.wait_ge(padded, 5)
            nc.gpsimd.memset(vaug[:, :, :, :, DH0], 1.0).then_inc(padded, 1)
            pool.wait_ge(padded, 6)
            for j in range(4):
                nc.gpsimd.memset(kz[32 * j:32 * j + 1, :, j:H0:4, :], 1.0).then_inc(padded, 1)
                pool.wait_ge(padded, 7 + j)

            def prepare(b, i, s):
                if not (isinstance(b, int) and b < 2):
                    pool.wait_ge(max_ready, 16 * (b - 1))
                    apart(pool)
                kt = a["ctx_t"][ds(b, 1), 0:D, :].rearrange("o (g j d) k -> j d (o g) k", j=4, d=DH0)
                bm = g.bm_dram[ds(b, 1), :, :]
                for j in range(4):
                    pool.dma_start(kzb[32 * j + 2:32 * j + 2 + DH0, s, j:H0:4, :], kt[j]).then_inc(kb_loaded[s], 16)
                    pool.dma_start(kzb[32 * j + 1:32 * j + 2, s, j:H0:4, :], bm).then_inc(kb_loaded[s], 16)
                pool.wait_ge(kv_loaded[s], 16 * LOADS * (i + 1))
                if not (isinstance(b, int) and b < 2):
                    pool.wait_ge(pv_done, 8 * (b - 1))
                apart(pool)
                nc.gpsimd.tensor_copy(vaug[:, s, :, :, 0:DH0],
                                      vraw[:, s, :, :].rearrange("p k (h d) -> p k h d", d=DH0)).then_inc(v_padded, 1)

            steps(pool, B, prepare)

        @block.vector
        def _(dve):
            ch = Chain(dve, chain, 6)
            dve.tensor_scalar(g.rstd[:, :], g.mv[:, :, 1], EPS, None, ALU.add).then_inc(var_eps, 1)
            dve.wait_ge(rooted, 1)
            dve.reciprocal(g.rstd[:, :], g.rstd[:, :]).then_inc(scale_ready, 1)
            dve.wait_ge(scale_ready, 1)
            dve.tensor_scalar(g.rstd[:, :], g.rstd[:, :], DH0 ** -0.5, None, ALU.mult).then_inc(scale_ready, 1)
            dve.wait_ge(scale_ready, 2)
            dve.wait_ge(padded, 10)

            def queries(b):
                if not (isinstance(b, int) and b < 1):
                    dve.wait_ge(t2_done, b)
                for k in range(QT):
                    dve.tensor_scalar(qpad[:, k, :, 2:2 + DH0],
                                      g.x[:, ds(2 * b + k, 1), :].rearrange("p o (h d) -> p (o h) d", d=DH0),
                                      g.mv[:, ds(2 * b + k, 1), 0], g.rstd[:, ds(2 * b + k, 1)],
                                      ALU.subtract, ALU.mult)
                dve.memset(qpad[:, :, :, 1], 1.0)
                dve.memset(qpad[:, :, :, 0], 0.0).then_inc(q_ready, 1)

            def maxima(b, u):
                j, k = u // 2, u % 2
                dve.wait_ge(max_ready, 16 * b + u + 1)
                dve.tensor_reduce(qpad[:, k, 2 * j:2 * j + 2, 0],
                                  ps[:, MB + u % 2, :].rearrange("p (h k) -> p h k", h=2), AX.X, ALU.max,
                                  negate=True).then_inc(max_used, 1)

            def mask_off(b):
                dve.memset(qpad[:, :, :, 1], 0.0).then_inc(q2_ready, 1)

            def keep_ot(b, q):
                dve.wait_ge(pv_done, 8 * b + 4 * q + 4)
                if q == 0 and not (isinstance(b, int) and b < 1):
                    dve.wait_ge(outt_done, b)
                dve.tensor_copy(ot[:, 2 * q:2 * q + 2, :], ps[:, OB, :].rearrange("p (g q) -> p g q", g=2)).then_inc(ot_used, 1)

            def finish(b):
                ch.step(b)
                dve.wait_ge(outt_done, b + 1)
                o = ps[:, TB:TB + 2, :].rearrange("p k (h d) -> p k h d", d=32)
                ch.link(dve.reciprocal(rec[:, :, :], o[:, :, :, DH0]))
                ch.link(dve.tensor_scalar(rec[:, :, :], rec[:, :, :], g.tg[:, 0:1], None, ALU.mult))
                ch.link(dve.tensor_tensor(upd[:, :, :, :], o[:, :, :, 0:DH0],
                                          rec[:, :, :].unsqueeze(3).broadcast_to([P, QT, H0, DH0]), ALU.mult))
                xb = g.x[:, ds(2 * b, 2), :]
                dve.tensor_tensor(xb, xb, upd[:, :, :, :].rearrange("p k h d -> p k (h d)"), ALU.add).then_inc(fin_done, 1)
                dve.wait_ge(fin_done, b + 1)
                apart(dve)
                for k in range(QT):
                    ins = dve.bn_stats(st[:, k, :], g.x[:, ds(2 * b + k, 1), :].rearrange("p o d -> p (o d)"))
                ch.link(ins)
                apart(dve)
                for k in range(QT):
                    ins = dve.bn_aggr(mvb[:, k, :], st[:, k, :])
                ch.link(ins)
                apart(dve)
                ch.link(dve.tensor_copy(g.mv[:, ds(2 * b, 2), :], mvb[:, :, :]))
                ch.end()

            queries(0)
            for u in range(16):
                maxima(0, u)
            mask_off(0)
            queries(1)

            def body(b, i, s):
                last, last2 = isinstance(b, int) and b == B - 1, isinstance(b, int) and b >= B - 2
                if not last:
                    for u in range(16):
                        maxima(b + 1, u)
                    mask_off(b + 1)
                keep_ot(b, 0)
                if not last2:
                    queries(b + 2)
                keep_ot(b, 1)
                finish(b)

            steps(dve, B, body)

        @block.scalar
        def _(act):
            act.wait_ge(var_eps, 1)
            act.activation(g.rstd[:, :], g.rstd[:, :], ACT.Sqrt).then_inc(rooted, 1)

            def keep_qtb(b):
                act.wait_ge(t1_done, b + 1)
                for k in range(QT):
                    act.activation(qtb[:, :, k * P:(k + 1) * P],
                                   ps[:, TB + k, :].rearrange("p (g q) -> p g q", q=P), ACT.Copy).then_inc(qtb_ready, 1)

            def keep_qt(b, s):
                act.wait_ge(t2_done, b + 1)
                for k in range(QT):
                    act.activation(qt[:, s, :, k * P:(k + 1) * P],
                                   ps[:, TB + k, :].rearrange("p (g q) -> p g q", q=P), ACT.Copy).then_inc(qt_ready, 1)

            def exps(b, j):
                for k in range(QT):
                    v = 2 * j + k
                    act.wait_ge(sc_ready, 16 * b + v + 1)
                    if k == 0 and not (isinstance(b, int) and b == 0 and j < 2):
                        act.wait_ge(pv_done, 8 * b + j - 1)
                    apart(act)
                    act.activation(pt[:, j % 2, k, :, :], ps[:, SB + v % 3, :].rearrange("p (h q) -> p h q", h=2),
                                   ACT.Exp, bias=g.bm0[:, k, ds(b, 1)]).then_inc(pt_ready, 1)

            keep_qtb(0)
            keep_qt(0, 0)
            keep_qtb(1)

            def body(b, i, s):
                last, last2 = isinstance(b, int) and b == B - 1, isinstance(b, int) and b >= B - 2
                for j in range(8):
                    exps(b, j)
                    if j == 6 and not last:
                        keep_qt(b + 1, 1 - s)
                if not last2:
                    keep_qtb(b + 2)

            steps(act, B, body)

        @block.tensor
        def _(pe):
            def turn(done):
                for k in range(QT):
                    for q in range(G):
                        ins = pe.transpose(ps[:, TB + k, q * P:(q + 1) * P],
                                           qpad[:, k, 4 * q:4 * q + 4, :].rearrange("p h d -> p (h d)"), g.ident[:, :])
                ins.then_inc(done, 1)

            def turn1(b):
                pe.wait_ge(q_ready, b + 1)
                if isinstance(b, int) and b == 1:
                    pe.wait_ge(qt_ready, 2)
                elif not isinstance(b, int) or b > 1:
                    pe.wait_ge(fin_done, b - 1)
                turn(t1_done)

            def turn2(b):
                pe.wait_ge(q2_ready, b + 1)
                pe.wait_ge(qtb_ready, 2 * b + 2)
                turn(t2_done)

            def max_pass(b, i, s, u):
                j, k = u // 2, u % 2
                if u == 0:
                    pe.wait_ge(qtb_ready, 2 * b + 2)
                    pe.wait_ge(kb_loaded[s], 128 * (i + 1))
                    pe.wait_ge(kv_loaded[s], 16 * LOADS * (i + 1))
                if not (isinstance(b, int) and b == 0 and u < 2):
                    pe.wait_ge(max_used, 16 * b + u - 1)
                pe.matmul(ps[:, MB + u % 2, :], qtb[:, j // 2, k * P:(k + 1) * P], kzb[:, s, 2 * j:2 * j + 2, :],
                          start=True, stop=True).then_inc(max_ready, 1)

            def scores(b, s, j):
                if j == 0:
                    pe.wait_ge(qt_ready, 2 * b + 2)
                for k in range(QT):
                    v = 2 * j + k
                    if not (isinstance(b, int) and b == 0 and v < 3):
                        pe.wait_ge(pt_ready, 16 * b + v - 2)
                    for h in (2 * j, 2 * j + 1):
                        ins = pe.matmul(ps[:, SB + v % 3, (h % 2) * S:(h % 2 + 1) * S],
                                        kz[:, s, h, k * P:(k + 1) * P], qt[:, s, h // 4, :], start=True, stop=True)
                    ins.then_inc(sc_ready, 1)

            def values(b, s, j):
                q = j // 2
                if j == 0:
                    pe.wait_ge(v_padded, b + 1)
                pe.wait_ge(pt_ready, 16 * b + 2 * j + 2)
                if j % 4 == 0 and not (isinstance(b, int) and b == 0 and j == 0):
                    pe.wait_ge(ot_used, 2 * b + j // 4)
                for k in range(QT):
                    for h in (2 * j, 2 * j + 1):
                        r = 32 * (h % 4)
                        ins = pe.matmul(ps[r:r + 32, OB, (q % 2) * S:(q % 2 + 1) * S], vaug[:, s, k, h, :],
                                        pt[:, j % 2, k, h % 2, :], start=(k == 0), stop=(k == QT - 1),
                                        tile_position=(0, r))
                ins.then_inc(pv_done, 1)

            def turn_out(b, last):
                pe.wait_ge(ot_used, 2 * b + 2)
                pe.wait_ge(qt_ready, 2 * b + (2 if last else 4))
                for k in range(QT):
                    for q in range(G):
                        ins = pe.transpose(ps[:, TB + k, q * P:(q + 1) * P], ot[:, q, k * P:(k + 1) * P], g.ident[:, :])
                ins.then_inc(outt_done, 1)

            turn1(0)
            for u in range(16):
                max_pass(0, 0, 0, u)
            turn2(0)
            turn1(1)

            def body(b, i, s):
                last, last2 = isinstance(b, int) and b == B - 1, isinstance(b, int) and b >= B - 2
                for j in range(8):
                    scores(b, s, j)
                    if j < 4 and not last:
                        for u in range(4 * j, 4 * j + 4):
                            max_pass(b + 1, i + s, 1 - s, u)
                    if j >= 1:
                        values(b, s, j - 1)
                    if j == 6 and not last:
                        turn2(b + 1)
                values(b, s, 7)
                turn_out(b, last)
                if not last2:
                    turn1(b + 2)

            steps(pe, B, body)


def ffn0(nc, g, a):
    with ExitStack() as ctx:
        def sb(name, shape, dt=F32):
            return ctx.enter_context(nc.sbuf_tensor(name, shape, dt))

        def sem(name):
            return ctx.enter_context(nc.semaphore(name))

        ew = sb("ew", [P, 2, E0, D])
        eb = sb("eb", [E0, D])
        rw = sb("rw", [P, 2, E0])
        rb = sb("rb", [1, E0])
        y = sb("y0", [P, D])
        yt = sb("yt0", [P, 2, 2, P])
        lg = sb("lg0", [P, E0])
        top = sb("top0", [P, 8])
        neg = sb("neg0", [P, 1])
        at = sb("at0", [P, 8], U32)
        atf = sb("atf0", [P, 1])
        hot = sb("hot0", [P, E0])
        ex = sb("ex0", [P, E0])
        total = sb("total0", [P, 1])
        inv = sb("inv0", [P, 1])
        gm = sb("gm0", [P, 2, E0])
        gmt = sb("gmt0", [E0, P])
        st = sb("stf", [P, 6])
        mvb = sb("mvf", [P, 2])
        loaded, var_eps, rooted, scale_ready = sem("f_loaded"), sem("f_var_eps"), sem("f_rooted"), sem("f_scale")
        y_ready, yt_turned, yt_ready, lg_ready = sem("f_y"), sem("f_yt_turned"), sem("f_yt"), sem("f_lg")
        neg_ready, ex_ready, gm_ready, gmt_turned = sem("f_neg"), sem("f_ex"), sem("f_gm"), sem("f_gmt_turned")
        gmt_ready, bias_ready, mm_ready, acc_done = sem("f_gmt"), sem("f_bias"), sem("f_mm"), sem("f_acc")
        route_chain, stat_chain = sem("f_route_chain"), sem("f_stat_chain")
        ps = g.ps
        TURN, LOGIT, EXP, GATE, BIAS = 0, 1, 2, 6, 7
        block = ctx.enter_context(nc.Block())

        @block.sync
        def _(sp):
            sp.dma_start(ew[:, :, :, :], a["ew0"].rearrange("p (k e d) -> p k e d", k=2, e=E0)).then_inc(loaded, 16)
            sp.dma_start(eb[:, :], a["eb0"]).then_inc(loaded, 16)
            sp.dma_start(rw[:, :, :], a["router_w"].rearrange("p (k e) -> p k e", k=2)).then_inc(loaded, 16)
            sp.dma_start(rb[:, :], a["router_b"]).then_inc(loaded, 16)

        @block.vector
        def _(dve):
            route, stat = Chain(dve, route_chain, 6), Chain(dve, stat_chain, 3)
            dve.tensor_scalar(g.rstd[:, :], g.mv[:, :, 1], EPS, None, ALU.add).then_inc(var_eps, 1)
            dve.wait_ge(rooted, 1)
            dve.reciprocal(g.rstd[:, :], g.rstd[:, :]).then_inc(scale_ready, 1)
            dve.wait_ge(scale_ready, 1)

            def normalise(t):
                if not (isinstance(t, int) and t == 0):
                    dve.wait_ge(yt_turned, t)
                dve.tensor_scalar(y[:, :], g.x[:, ds(t, 1), :].rearrange("p o d -> p (o d)"),
                                  g.mv[:, ds(t, 1), 0], g.rstd[:, ds(t, 1)], ALU.subtract, ALU.mult).then_inc(y_ready, 1)

            def pick(t):
                route.step(t)
                dve.wait_ge(lg_ready, t + 1)
                route.link(dve.tensor_copy(lg[:, :], ps[:, LOGIT, 0:E0]))
                apart(dve)
                route.link(dve.max(top[:, :], lg[:, :]))
                if not (isinstance(t, int) and t == 0):
                    dve.wait_ge(ex_ready, t)
                dve.tensor_scalar(neg[:, :], top[:, 0:1], -1.0, None, ALU.mult).then_inc(neg_ready, 1)
                route.link(dve.max_index(at[:, :], top[:, :], lg[:, :]))
                route.link(dve.tensor_copy(atf[:, :], at[:, 0:1]))
                route.link(dve.tensor_scalar(hot[:, :], g.iota8[:, :], atf[:, 0:1], None, ALU.is_equal))

            def weigh(t, s):
                dve.wait_ge(ex_ready, t + 1)
                route.link(dve.reciprocal(inv[:, :], total[:, :]))
                route.end()
                if not (isinstance(t, int) and t < 2):
                    dve.wait_ge(gmt_turned, t - 1)
                dve.tensor_scalar(gm[:, s, :], hot[:, :], inv[:, 0:1], g.tg[:, 1:2], ALU.mult, ALU.mult).then_inc(gm_ready, 1)
                dve.wait_ge(gm_ready, t + 1)

            def add_bias(t):
                dve.wait_ge(bias_ready, t + 1)
                xt = g.x[:, ds(t, 1), :].rearrange("p o d -> p (o d)")
                dve.tensor_tensor(xt, xt, ps[:, BIAS, 0:D], ALU.add).then_inc(acc_done, 1)
                dve.wait_ge(acc_done, 9 * t + 1)

            def add_experts(t, s, q):
                dve.wait_ge(mm_ready, 4 * t + q + 1)
                xt = g.x[:, ds(t, 1), :].rearrange("p o d -> p (o d)")
                for e in range(2):
                    dve.scalar_tensor_tensor(xt, ps[:, EXP + q, e * D:(e + 1) * D], gm[:, s, 2 * q + e:2 * q + e + 1], xt,
                                             ALU.mult, ALU.add).then_inc(acc_done, 1)
                    dve.wait_ge(acc_done, 9 * t + 2 + 2 * q + e)

            def statistics(t):
                stat.step(t)
                apart(dve)
                stat.link(dve.bn_stats(st[:, :], g.x[:, ds(t, 1), :].rearrange("p o d -> p (o d)")))
                apart(dve)
                stat.link(dve.bn_aggr(mvb[:, :], st[:, :]))
                apart(dve)
                stat.link(dve.tensor_copy(g.mv[:, ds(t, 1), :].rearrange("p o d -> p (o d)"), mvb[:, :]))
                stat.end()

            normalise(0)
            pick(0)
            weigh(0, 0)

            def body(t, i, s):
                last = isinstance(t, int) and t == T - 1
                if not last:
                    normalise(t + 1)
                add_bias(t)
                add_experts(t, s, 0)
                add_experts(t, s, 1)
                if not last:
                    pick(t + 1)
                add_experts(t, s, 2)
                if not last:
                    weigh(t + 1, 1 - s)
                add_experts(t, s, 3)
                statistics(t)

            steps(dve, T, body)

        @block.scalar
        def _(act):
            act.wait_ge(var_eps, 1)
            act.activation(g.rstd[:, :], g.rstd[:, :], ACT.Sqrt).then_inc(rooted, 1)

            def keep_yt(t, s):
                act.wait_ge(yt_turned, t + 1)
                if not (isinstance(t, int) and t < 2):
                    act.wait_ge(mm_ready, 4 * (t - 1))
                act.activation(yt[:, s, :, :], ps[:, TURN, 0:2 * P].rearrange("p (k q) -> p k q", k=2), ACT.Copy).then_inc(yt_ready, 1)

            def route(t, s):
                act.wait_ge(neg_ready, t + 1)
                if not (isinstance(t, int) and t < 1):
                    act.wait_ge(gm_ready, t)
                act.activation(ex[:, :], lg[:, :], ACT.Exp, bias=neg[:, 0:1], accum_out=total[:, :]).then_inc(ex_ready, 1)
                act.wait_ge(gmt_turned, t + 1)
                if not (isinstance(t, int) and t < 1):
                    act.wait_ge(bias_ready, t)
                act.activation(gmt[:, :], ps[0:E0, GATE, 0:P], ACT.Copy).then_inc(gmt_ready, 1)

            keep_yt(0, 0)
            route(0, 0)

            def body(t, i, s):
                if not (isinstance(t, int) and t == T - 1):
                    keep_yt(t + 1, 1 - s)
                    route(t + 1, 1 - s)

            steps(act, T, body)

        @block.tensor
        def _(pe):
            pe.wait_ge(loaded, 64)

            def turn(t):
                pe.wait_ge(y_ready, t + 1)
                if not (isinstance(t, int) and t == 0):
                    pe.wait_ge(yt_ready, t)
                for k in range(2):
                    ins = pe.transpose(ps[:, TURN, k * P:(k + 1) * P], y[:, k * P:(k + 1) * P], g.ident[:, :])
                ins.then_inc(yt_turned, 1)

            def logits(t, s):
                pe.wait_ge(yt_ready, t + 1)
                if not (isinstance(t, int) and t == 0):
                    pe.wait_ge(neg_ready, t)
                for k in range(2):
                    pe.matmul(ps[:, LOGIT, 0:E0], yt[:, s, k, :], rw[:, k, :], start=(k == 0), stop=False)
                pe.matmul(ps[:, LOGIT, 0:E0], g.ones_f[:, :], rb[:, :], start=False, stop=True).then_inc(lg_ready, 1)

            def turn_gates(t, s):
                pe.wait_ge(gm_ready, t + 1)
                if not (isinstance(t, int) and t == 0):
                    pe.wait_ge(gmt_ready, t)
                pe.transpose(ps[0:E0, GATE, 0:P], gm[:, s, :], g.ident[:, :]).then_inc(gmt_turned, 1)

            def bias(t):
                pe.wait_ge(gmt_ready, t + 1)
                if not (isinstance(t, int) and t == 0):
                    pe.wait_ge(acc_done, 9 * t - 8)
                pe.matmul(ps[:, BIAS, 0:D], gmt[:, :], eb[:, :], start=True, stop=True).then_inc(bias_ready, 1)

            def experts(t, s, q):
                if not (isinstance(t, int) and t == 0):
                    pe.wait_ge(acc_done, 9 * t - 9 + 3 + 2 * q)
                for k in range(2):
                    ins = pe.matmul(ps[:, EXP + q, :], yt[:, s, k, :], ew[:, k, 2 * q:2 * q + 2, :],
                                    start=(k == 0), stop=(k == 1))
                ins.then_inc(mm_ready, 1)

            turn(0)
            logits(0, 0)
            turn_gates(0, 0)
            bias(0)

            def body(t, i, s):
                last = isinstance(t, int) and t == T - 1
                experts(t, s, 0)
                if not last:
                    turn(t + 1)
                experts(t, s, 1)
                if not last:
                    logits(t + 1, 1 - s)
                experts(t, s, 2)
                experts(t, s, 3)
                if not last:
                    turn_gates(t + 1, 1 - s)
                    bias(t + 1)

            steps(pe, T, body)


def attn1(nc, g, a):
    with ExitStack() as ctx:
        def sb(name, shape, dt=F32):
            return ctx.enter_context(nc.sbuf_tensor(name, shape, dt))

        def sem(name):
            return ctx.enter_context(nc.semaphore(name))

        w_tgt = sb("w_tgt", [P, 2, D])
        w_src = sb("w_src", [P, 4, 2 * D])
        w_out = sb("w_out", [P, 4, D])
        b_tgt = sb("b_tgt", [P, 2])
        b_key = sb("b_key", [P, 2])
        b_val = sb("b_val", [P, D])
        b_out = sb("b_out", [P, D])
        ctx_t = sb("ctx_t", [P, 2, 4, S])
        maskrow = sb("maskrow1", [P, 2, S])
        pen = sb("pen", [P, 2, 2, S], BF16)
        ones32 = sb("ones32", [P, 32])
        y = sb("y1", [P, QT, D])
        yt = sb("yt1", [P, 2, 2, S])
        qt = sb("qt1", [P, 2, 2, S])
        qtb = sb("qtb1", [P, 2, S], BF16)
        kz = sb("kz1", [P, 2, H1, S])
        kzb = sb("kzb1", [P, H1, S], BF16)
        vb = sb("vb1", [P, QT, D])
        v = sb("v1", [P, 2, QT, D])
        nm = sb("nm1", [P, QT, H1])
        nmt = sb("nmt1", [P, 2, S], BF16)
        pt = sb("pt1", [P, 2, QT, 2, S])
        rec = sb("rec1", [P, S])
        ut = sb("ut1", [P, 2, S])
        st = sb("st1", [P, QT, 6])
        mvb = sb("mvb1", [P, QT, 2])
        loaded, padded = sem("b_loaded"), sem("b_padded")
        ctx_loaded = [sem(f"b_ctx_loaded{s}") for s in (0, 1)]
        var_eps, rooted, scale_ready, bo_ready = sem("b_var_eps"), sem("b_rooted"), sem("b_scale"), sem("b_bo")
        y_ready, yt_turned, yt_ready = sem("b_y"), sem("b_yt_turned"), sem("b_yt")
        q_done, q_kept, qb_ready, k_done, k_kept, kb_ready = [sem("b_" + n) for n in (
            "q_done", "q_kept", "qb_ready", "k_done", "k_kept", "kb_ready")]
        v_done, v_kept, v_ready, pen_ready, max_ready, max_used = [sem("b_" + n) for n in (
            "v_done", "v_kept", "v_ready", "pen_ready", "max_ready", "max_used")]
        nm_turned, nmt_ready, sc_ready, pt_ready, pv_done, ut_ready = [sem("b_" + n) for n in (
            "nm_turned", "nmt_ready", "sc_ready", "pt_ready", "pv_done", "ut_ready")]
        o_done, x_done, rec_ready, chain = sem("b_o_done"), sem("b_x_done"), sem("b_rec"), sem("b_chain")
        ps = g.ps
        TURN, QO, KV, PV, MB, SB = 0, 1, 2, 3, 4, 6
        SCALE = DH1 ** -0.5
        block = ctx.enter_context(nc.Block())

        @block.sync
        def _(sp):
            for dst, name in ((w_tgt, "w_tgt"), (w_src, "w_src"), (w_out, "w_out")):
                sp.dma_start(dst[:, :, :], a[name].rearrange("p (k n) -> p k n", k=dst.shape[1])).then_inc(loaded, 16)
            for dst, name in ((b_tgt, "b_tgt"), (b_key, "b_key"), (b_val, "b_val"), (b_out, "b_out")):
                sp.dma_start(dst[:, :], a[name]).then_inc(loaded, 16)

            def load(b, i, s):
                if not (isinstance(b, int) and b < 2):
                    sp.wait_ge(v_done, b - 1)
                    apart(sp)
                    sp.wait_ge(k_kept, 8 * (b - 1))
                    apart(sp)
                    sp.wait_ge(pen_ready, b - 1)
                    apart(sp)
                sp.dma_start(ctx_t[:, s, :, :], a["ctx_t"][ds(b, 1), :, :].rearrange("o (k p) q -> p (o k) q", p=P)
                             ).then_inc(ctx_loaded[s], 16)
                sp.dma_start(maskrow[:, s, :], a["maskrow"][:, ds(b * S, S)].partition_broadcast(P)
                             ).then_inc(ctx_loaded[s], 16)

            steps(sp, B, load)

        @block.gpsimd
        def _(pool):
            nc.gpsimd.memset(kz[:, :, :, :], 0.0).then_inc(padded, 1)
            nc.gpsimd.memset(nmt[:, :, :], 0.0).then_inc(padded, 1)
            nc.gpsimd.memset(pen[:, :, :, :], 0.0).then_inc(padded, 1)
            nc.gpsimd.memset(ones32[:, :], 1.0).then_inc(padded, 1)

            def narrow(b, i, s):
                pool.wait_ge(q_kept, 2 * b + 2)
                if not (isinstance(b, int) and b < 1):
                    pool.wait_ge(max_ready, 8 * b)
                apart(pool)
                nc.gpsimd.tensor_copy(qtb[:, :, :], qt[:, s, :, :]).then_inc(qb_ready, 1)

            steps(pool, B, narrow)

        @block.vector
        def _(dve):
            ch = Chain(dve, chain, 4)
            dve.tensor_scalar(g.rstd[:, :], g.mv[:, :, 1], EPS, None, ALU.add).then_inc(var_eps, 1)
            dve.wait_ge(loaded, 112)
            dve.tensor_scalar(b_out[:, :], b_out[:, :], g.tg[:, 2:3], None, ALU.mult).then_inc(bo_ready, 1)
            dve.wait_ge(bo_ready, 1)
            dve.wait_ge(rooted, 1)
            dve.reciprocal(g.rstd[:, :], g.rstd[:, :]).then_inc(scale_ready, 1)
            dve.wait_ge(scale_ready, 1)
            dve.wait_ge(padded, 4)

            def normalise(b):
                if not (isinstance(b, int) and b == 0):
                    dve.wait_ge(yt_turned, b)
                for k in range(QT):
                    ins = dve.tensor_scalar(y[:, k, :], g.x[:, ds(2 * b + k, 1), :].rearrange("p o d -> p (o d)"),
                                            g.mv[:, ds(2 * b + k, 1), 0], g.rstd[:, ds(2 * b + k, 1)],
                                            ALU.subtract, ALU.mult)
                ins.then_inc(y_ready, 1)

            def mask_bias(b, i, s):
                dve.wait_ge(ctx_loaded[s], 32 * (i + 1))
                if not (isinstance(b, int) and b < 2):
                    dve.wait_ge(max_ready, 8 * (b - 1))
                dve.tensor_scalar(pen[0:1, s, :, :], maskrow[0:1, s, :].unsqueeze(1).broadcast_to([1, 2, S]), 0.0, MASKED1,
                                  ALU.is_equal, ALU.mult).then_inc(pen_ready, 1)

            def keep_qk(b, s):
                dve.wait_ge(q_done, b + 1)
                if not (isinstance(b, int) and b < 2):
                    dve.wait_ge(sc_ready, 8 * (b - 1))
                for m in range(2):
                    dve.scalar_tensor_tensor(qt[:, s, m, :], ps[:, QO, m * S:(m + 1) * S], b_tgt[:, m:m + 1],
                                             maskrow[:, s, :], ALU.add, ALU.mult).then_inc(q_kept, 1)
                dve.wait_ge(k_done, b + 1)
                for h in range(H1):
                    m, r = h // 4, 32 * (h % 4)
                    dve.scalar_tensor_tensor(kz[r:r + 32, s, h, :], ps[r:r + 32, KV, m * S:(m + 1) * S],
                                             b_key[r:r + 32, m:m + 1], maskrow[r:r + 32, s, :],
                                             ALU.add, ALU.mult).then_inc(k_kept, 1)

            def keep_v(b):
                dve.wait_ge(v_done, b + 1)
                if not (isinstance(b, int) and b < 1):
                    dve.wait_ge(v_ready, 2 * b)
                dve.tensor_tensor(vb[:, :, :], ps[:, KV, :].rearrange("p (k d) -> p k d", k=2),
                                  b_val[:, :].unsqueeze(1).broadcast_to([P, QT, D]), ALU.add).then_inc(v_kept, 1)

            def maxima(b, u):
                j, k = u // 2, u % 2
                dve.wait_ge(max_ready, 8 * b + u + 1)
                if u == 0 and not (isinstance(b, int) and b == 0):
                    dve.wait_ge(nm_turned, b)
                dve.tensor_reduce(nm[:, k, 2 * j:2 * j + 2], ps[:, MB + u % 2, :].rearrange("p (h k) -> p h k", h=2),
                                  AX.X, ALU.max, negate=True).then_inc(max_used, 1)

            def keep_ut(b, q):
                dve.wait_ge(pv_done, 4 * b + 2 * q + 2)
                if q == 0 and not (isinstance(b, int) and b == 0):
                    dve.wait_ge(o_done, b)
                dve.reciprocal(rec[:, :], ps[:, PV, S:2 * S]).then_inc(rec_ready, 1)
                dve.wait_ge(rec_ready, 2 * b + q + 1)
                dve.tensor_tensor(ut[:, q, :], ps[:, PV, 0:S], rec[:, :], ALU.mult).then_inc(ut_ready, 1)

            def finish(b):
                ch.step(b)
                dve.wait_ge(o_done, b + 1)
                xb = g.x[:, ds(2 * b, 2), :]
                dve.scalar_tensor_tensor(xb, ps[:, QO, :].rearrange("p (k d) -> p k d", k=2), g.tg[:, 2:3], xb,
                                         ALU.mult, ALU.add).then_inc(x_done, 1)
                dve.wait_ge(x_done, b + 1)
                ch.link(dve.tensor_tensor(xb, xb, b_out[:, :].unsqueeze(1).broadcast_to([P, QT, D]), ALU.add))
                apart(dve)
                for k in range(QT):
                    ins = dve.bn_stats(st[:, k, :], g.x[:, ds(2 * b + k, 1), :].rearrange("p o d -> p (o d)"))
                ch.link(ins)
                apart(dve)
                for k in range(QT):
                    ins = dve.bn_aggr(mvb[:, k, :], st[:, k, :])
                ch.link(ins)
                apart(dve)
                ch.link(dve.tensor_copy(g.mv[:, ds(2 * b, 2), :], mvb[:, :, :]))
                ch.end()

            normalise(0)
            mask_bias(0, 0, 0)
            keep_qk(0, 0)
            keep_v(0)
            for u in range(8):
                maxima(0, u)

            def body(b, i, s):
                last = isinstance(b, int) and b == B - 1
                if not last:
                    normalise(b + 1)
                    mask_bias(b + 1, i + s, 1 - s)
                    keep_qk(b + 1, 1 - s)
                    keep_ut(b, 0)
                    keep_v(b + 1)
                    for u in range(4):
                        maxima(b + 1, u)
                    keep_ut(b, 1)
                    for u in range(4, 8):
                        maxima(b + 1, u)
                else:
                    keep_ut(b, 0)
                    keep_ut(b, 1)
                finish(b)

            steps(dve, B, body)

        @block.scalar
        def _(act):
            act.wait_ge(var_eps, 1)
            act.activation(g.rstd[:, :], g.rstd[:, :], ACT.Sqrt).then_inc(rooted, 1)

            def keep_yt(b, s):
                act.wait_ge(yt_turned, b + 1)
                if not (isinstance(b, int) and b < 2):
                    act.wait_ge(o_done, b - 1)
                act.activation(yt[:, s, :, :], ps[:, TURN, :].rearrange("p (k q) -> p k q", k=2), ACT.Copy).then_inc(yt_ready, 1)

            def narrow(b, s):
                if not (isinstance(b, int) and b < 1):
                    act.wait_ge(max_ready, 8 * b)
                for m in range(2):
                    act.wait_ge(k_kept, 8 * b + 4 * m + 4)
                    act.activation(kzb[:, 4 * m:4 * m + 4, :], kz[:, s, 4 * m:4 * m + 4, :], ACT.Copy).then_inc(kb_ready, 1)

            def keep_v(b, s):
                act.wait_ge(v_kept, b + 1)
                if not (isinstance(b, int) and b < 2):
                    act.wait_ge(pv_done, 4 * (b - 1))
                apart(act)
                for k in range(QT):
                    act.activation(v[:, s, k, :], vb[:, k, :], ACT.Copy, scale=g.maskcol[:, k, ds(b, 1)]).then_inc(v_ready, 1)

            def keep_nmt(b, s):
                act.wait_ge(nm_turned, b + 1)
                if not (isinstance(b, int) and b < 2):
                    act.wait_ge(sc_ready, 8 * (b - 1))
                act.activation(nmt[0:H1, s, :], ps[0:H1, TURN, 0:S], ACT.Copy).then_inc(nmt_ready, 1)

            def exps(b, j):
                for k in range(QT):
                    u = 2 * j + k
                    act.wait_ge(sc_ready, 8 * b + u + 1)
                    if k == 0 and not (isinstance(b, int) and b == 0 and j < 2):
                        act.wait_ge(pv_done, 4 * b + j - 1)
                    apart(act)
                    act.activation(pt[:, j % 2, k, :, :], ps[:, SB + u % 2, :].rearrange("p (h q) -> p h q", h=2),
                                   ACT.Exp, bias=g.bm1[:, k, ds(b, 1)], scale=SCALE).then_inc(pt_ready, 1)

            act.wait_ge(padded, 4)
            keep_yt(0, 0)
            narrow(0, 0)
            keep_v(0, 0)
            keep_nmt(0, 0)

            def body(b, i, s):
                last = isinstance(b, int) and b == B - 1
                exps(b, 0)
                if not last:
                    keep_yt(b + 1, 1 - s)
                exps(b, 1)
                exps(b, 2)
                if not last:
                    narrow(b + 1, 1 - s)
                exps(b, 3)
                if not last:
                    keep_v(b + 1, 1 - s)
                    keep_nmt(b + 1, 1 - s)

            steps(act, B, body)

        @block.tensor
        def _(pe):
            pe.wait_ge(loaded, 112)
            pe.wait_ge(padded, 4)

            def turn(b):
                pe.wait_ge(y_ready, b + 1)
                if not (isinstance(b, int) and b == 0):
                    pe.wait_ge(nmt_ready, b)
                for d in range(2):
                    for k in range(QT):
                        ins = pe.transpose(ps[:, TURN, d * S + k * P:d * S + (k + 1) * P], y[:, k, d * P:(d + 1) * P],
                                           g.ident[:, :])
                ins.then_inc(yt_turned, 1)

            def project_q(b, s):
                pe.wait_ge(yt_ready, b + 1)
                if not (isinstance(b, int) and b < 2):
                    pe.wait_ge(x_done, b - 1)
                for m in range(2):
                    for d in range(2):
                        ins = pe.matmul(ps[:, QO, m * S:(m + 1) * S], w_tgt[:, d, m * P:(m + 1) * P], yt[:, s, d, :],
                                        start=(d == 0), stop=(d == 1))
                ins.then_inc(q_done, 1)

            def project_k(b, i, s):
                pe.wait_ge(ctx_loaded[s], 32 * (i + 1))
                if not (isinstance(b, int) and b == 0):
                    pe.wait_ge(v_kept, b)
                for m in range(2):
                    for d in range(4):
                        ins = pe.matmul(ps[:, KV, m * S:(m + 1) * S], w_src[:, d, m * P:(m + 1) * P], ctx_t[:, s, d, :],
                                        start=(d == 0), stop=(d == 3))
                ins.then_inc(k_done, 1)

            def project_v(b, s):
                pe.wait_ge(k_kept, 8 * b + 8)
                for k in range(QT):
                    for d in range(4):
                        ins = pe.matmul(ps[:, KV, k * D:(k + 1) * D], ctx_t[:, s, d, k * P:(k + 1) * P], w_src[:, d, D:2 * D],
                                        start=(d == 0), stop=(d == 3))
                ins.then_inc(v_done, 1)

            def max_pass(b, s, u):
                j, k = u // 2, u % 2
                if u == 0:
                    pe.wait_ge(qb_ready, b + 1)
                    pe.wait_ge(pen_ready, b + 1)
                if u % 4 == 0:
                    pe.wait_ge(kb_ready, 2 * b + u // 4 + 1)
                if not (isinstance(b, int) and b == 0 and u < 2):
                    pe.wait_ge(max_used, 8 * b + u - 1)
                pe.matmul(ps[:, MB + u % 2, :], qtb[:, j // 2, k * P:(k + 1) * P], kzb[:, 2 * j:2 * j + 2, :],
                          start=True, stop=False)
                pe.matmul(ps[:, MB + u % 2, :], g.row0_bf[:, :], pen[:, s, :, :], start=False, stop=True).then_inc(max_ready, 1)

            def turn_maxima(b):
                pe.wait_ge(max_used, 8 * b + 8)
                pe.wait_ge(yt_ready, b + 1)
                for k in range(QT):
                    ins = pe.transpose(ps[0:H1, TURN, k * P:(k + 1) * P], nm[:, k, :], g.ident[:, :])
                ins.then_inc(nm_turned, 1)

            def scores(b, s, j):
                if j == 0:
                    pe.wait_ge(nmt_ready, b + 1)
                    pe.wait_ge(k_kept, 8 * b + 8)
                for k in range(QT):
                    u = 2 * j + k
                    if not (isinstance(b, int) and b == 0 and u < 2):
                        pe.wait_ge(pt_ready, 8 * b + u - 1)
                    for h in (2 * j, 2 * j + 1):
                        o = ps[:, SB + u % 2, (h % 2) * S:(h % 2 + 1) * S]
                        pe.matmul(o, kz[:, s, h, k * P:(k + 1) * P], qt[:, s, h // 4, :], start=True, stop=False)
                        ins = pe.matmul(o, g.esel[:, h, :], nmt[:, s, :], start=False, stop=True)
                    ins.then_inc(sc_ready, 1)

            def values(b, s, j):
                if j == 0:
                    pe.wait_ge(v_ready, 2 * b + 2)
                pe.wait_ge(pt_ready, 8 * b + 2 * j + 2)
                if j % 2 == 0 and not (isinstance(b, int) and b == 0 and j == 0):
                    pe.wait_ge(ut_ready, 2 * b + j // 2)
                for lhs, c in ((v, 0), (ones32, S)):
                    for k in range(QT):
                        for h in (2 * j, 2 * j + 1):
                            r = 32 * (h % 4)
                            w = v[:, s, k, h * DH1:(h + 1) * DH1] if lhs is v else ones32[:, :]
                            ins = pe.matmul(ps[r:r + 32, PV, c:c + S], w, pt[:, j % 2, k, h % 2, :],
                                            start=(k == 0), stop=(k == QT - 1), tile_position=(0, r))
                ins.then_inc(pv_done, 1)

            def project_out(b, s, last):
                pe.wait_ge(ut_ready, 2 * b + 2)
                pe.wait_ge(q_kept, 2 * b + (2 if last else 4))
                for k in range(QT):
                    for d in range(4):
                        lhs = (yt[:, s, d, k * P:(k + 1) * P] if d < 2 else ut[:, d - 2, k * P:(k + 1) * P])
                        ins = pe.matmul(ps[:, QO, k * D:(k + 1) * D], lhs, w_out[:, d, :], start=(d == 0), stop=(d == 3))
                ins.then_inc(o_done, 1)

            turn(0)
            project_q(0, 0)
            project_k(0, 0, 0)
            project_v(0, 0)
            for u in range(8):
                max_pass(0, 0, u)
            turn_maxima(0)

            def body(b, i, s):
                last = isinstance(b, int) and b == B - 1
                scores(b, s, 0)
                if not last:
                    turn(b + 1)
                scores(b, s, 1)
                values(b, s, 0)
                if not last:
                    project_q(b + 1, 1 - s)
                    project_k(b + 1, i + s, 1 - s)
                scores(b, s, 2)
                values(b, s, 1)
                if not last:
                    project_v(b + 1, 1 - s)
                scores(b, s, 3)
                values(b, s, 2)
                if not last:
                    for u in range(4):
                        max_pass(b + 1, 1 - s, u)
                values(b, s, 3)
                if not last:
                    for u in range(4, 8):
                        max_pass(b + 1, 1 - s, u)
                project_out(b, s, last)
                if not last:
                    turn_maxima(b + 1)

            steps(pe, B, body)


def route(nc, g, a):
    with ExitStack() as ctx:
        def sb(name, shape, dt=F32):
            return ctx.enter_context(nc.sbuf_tensor(name, shape, dt))

        def sem(name):
            return ctx.enter_context(nc.semaphore(name))

        W1 = 2 * 2 * FF
        wg = sb("wg", [P, 2, E1])
        sw = sb("sw", [P, WCOLS])
        sw1 = sw[:, 0:W1].rearrange("p (k f) -> p k f", k=2)
        sw2 = sw[:, W1:WCOLS].rearrange("p (k d) -> p k d", k=KF)
        y = sb("y2", [P, 2, QT, D])
        yt = sb("yt2", [P, 2, 2, S])
        lg = sb("lg2", [P, QT, E1])
        top = sb("top2", [P, QT, 8])
        neg = sb("neg2", [P, QT])
        rest = sb("rest2", [P, QT, E1])
        mask = sb("mask2", [P, QT, E1])
        maskb = sb("maskb2", [P, QT, E1], BF16)
        seen = sb("seen2", [P, 2, E1], BF16)
        ex = sb("ex2", [P, QT, E1])
        total = sb("total2", [P, QT])
        picked = sb("picked2", [P, QT])
        coef = sb("coef2", [P, 3, QT])
        wrow = sb("wrow2", [P, 2, QT, E1])
        rank = sb("rank2", [P, QT, E1])
        ranki = sb("ranki2", [P, QT, E1], I32)
        hi = sb("hi2", [P, QT, E1], I32)
        lo = sb("lo2", [P, QT, E1], I32)
        hif = sb("hif2", [P, QT, E1], BF16)
        lof = sb("lof2", [P, QT, E1], BF16)
        hot_a = sb("hot_a", [P, QT, E1, RA], BF16)
        aa = sb("aa", [P, QT, E1, 32], BF16)
        bb = sb("bb", [P, QT, E1, RB], BF16)
        zero = sb("zero2", [P, 512], BF16)
        zrow = sb("zrow2", [32, CAP // 32 * ROW])
        sil = sb("sil2", [P, 2, S])
        gt = sb("gt2", [P, KF, S])
        base = sb("base2", [P, 2, QT, D])
        tt = sb("tt2", [P, E1 // 4, RB])
        pair = sb("pair2", [E1, 2, CAP])
        tok = sb("tok2", [E1, 3, CAP])
        names = ("r_loaded", "r_zeroed", "r_var_eps", "r_rooted", "r_scale", "r_y", "r_yt_turned", "r_yt", "r_lg",
                 "r_neg", "r_ex", "r_chain", "r_maskb", "r_rank", "r_wrow", "r_hot", "r_hot_used", "r_up", "r_sil",
                 "r_gt", "r_out", "r_base", "r_tt", "r_tt_out", "r_pair", "r_tok", "r_tok_turned", "r_fill")
        (loaded, zeroed, var_eps, rooted, scale_ready, y_ready, yt_turned, yt_ready, lg_ready, neg_ready, ex_ready,
         chain, maskb_ready, rank_ready, wrow_ready, hot_ready, hot_used, up_ready, sil_ready, gt_ready, out_ready,
         base_ready, tt_ready, tt_out, pair_in, tok_ready, tok_turned, filled) = [sem(n) for n in names]
        table_out = [sem(f"table_out{s}") for s in (0, 1)]
        base_out = [sem(f"base_out{s}") for s in (0, 1)]
        tchain = sem("r_tchain")
        ps = g.ps
        TURN, LOGIT, RANK, UP, OUT, LIST = 0, 1, 2, 3, 5, 6
        block = ctx.enter_context(nc.Block())

        @block.sync
        def _(sp):
            sp.dma_start(wg[:, :, :], a["wg"].rearrange("p (k e) -> p k e", k=2)).then_inc(loaded, 16)
            sp.dma_start(sw[:, :], a["shared"]).then_inc(loaded, 16)
            sp.wait_ge(zeroed, 4)
            sp.dma_start(g.table[NT:NT + CAP, :].rearrange("(p r) d -> p (r d)", p=32), zrow[:, :]).then_inc(filled, 16)
            sp.dma_start(a["out"][NT:NT + CAP, :].rearrange("(p r) d -> p (r d)", p=32), zrow[:, 0:CAP // 32 * D]
                         ).then_inc(filled, 16)

            def store_table(b, s):
                sp.wait_ge(wrow_ready, b + 1)
                apart(sp)
                rows = g.table[ds(b * S, S), :].rearrange("(k p) d -> p k d", p=P)
                sp.dma_start(rows[:, :, 0:D], y[:, s, :, :]).then_inc(table_out[s], 16)
                sp.dma_start(rows[:, :, D:ROW], wrow[:, s, :, :]).then_inc(table_out[s], 16)

            def store(b, i, s):
                if not (isinstance(b, int) and b == B - 1):
                    store_table(b + 1, 1 - s)
                sp.wait_ge(base_ready, b + 1)
                apart(sp)
                sp.dma_start(a["out"][ds(b * S, S), :].rearrange("(k p) d -> p k d", p=P), base[:, s, :, :]
                             ).then_inc(base_out[s], 16)

            store_table(0, 0)
            steps(sp, B, store)
            sp.wait_ge(tt_ready, 4)
            for i in range(4):
                for m in range(2):
                    r = 32 * i + m * RA
                    sp.dma_start(g.lists[i:E1:4, m, :].rearrange("g (a b) -> a g b", b=RB), tt[r:r + RA, :, :]
                                 ).then_inc(tt_out, 16)
            sp.wait_ge(tt_out, 128)
            sp.dma_start(pair[:, :, :], g.lists[:, :, :]).then_inc(pair_in, 16)
            for s in (0, 1):
                sp.wait_ge(base_out[s], 16 * (B // 2))
                sp.wait_ge(table_out[s], 32 * (B // 2))
            sp.wait_ge(filled, 32)
            sp.wait_ge(pair_in, 16)

        @block.gpsimd
        def _(pool):
            nc.gpsimd.memset(aa[:, :, :, :], 0.0).then_inc(zeroed, 1)
            nc.gpsimd.memset(zero[:, :], 0.0).then_inc(zeroed, 1)
            nc.gpsimd.memset(zrow[:, :], 0.0).then_inc(zeroed, 1)
            nc.gpsimd.memset(seen[:, :, :], 0.0).then_inc(zeroed, 1)

        @block.vector
        def _(dve):
            ch = Chain(dve, chain, 18)
            dve.tensor_scalar(g.rstd[:, :], g.mv[:, :, 1], EPS, None, ALU.add).then_inc(var_eps, 1)
            dve.wait_ge(rooted, 1)
            dve.reciprocal(g.rstd[:, :], g.rstd[:, :]).then_inc(scale_ready, 1)
            dve.wait_ge(scale_ready, 1)
            dve.wait_ge(zeroed, 4)

            def normalise(b, i, s):
                if not (isinstance(b, int) and b < 2):
                    dve.wait_ge(yt_turned, b - 1)
                    dve.wait_ge(table_out[s], 32 * i)
                    apart(dve)
                for k in range(QT):
                    ins = dve.tensor_scalar(y[:, s, k, :], g.x[:, ds(2 * b + k, 1), :].rearrange("p o d -> p (o d)"),
                                            g.mv[:, ds(2 * b + k, 1), 0], g.rstd[:, ds(2 * b + k, 1)],
                                            ALU.subtract, ALU.mult)
                ins.then_inc(y_ready, 1)

            def pick(b):
                ch.step(b)
                dve.wait_ge(lg_ready, b + 1)
                ch.link(dve.tensor_copy(lg[:, :, :], ps[:, LOGIT, 0:QT * E1].rearrange("p (k e) -> p k e", k=QT)))
                apart(dve)
                for k in range(QT):
                    ins = dve.max(top[:, k, :], lg[:, k, :])
                ch.link(ins)
                dve.tensor_scalar(neg[:, :], top[:, :, 0], -1.0, None, ALU.mult).then_inc(neg_ready, 1)
                apart(dve)
                for k in range(QT):
                    ins = dve.match_replace(rest[:, k, :], top[:, k, :], lg[:, k, :], NEG)
                ch.link(ins)
                if not (isinstance(b, int) and b == 0):
                    dve.wait_ge(rank_ready, b)
                ch.link(dve.tensor_tensor(mask[:, :, :], rest[:, :, :], lg[:, :, :], ALU.not_equal))
                dve.tensor_copy(maskb[:, :, :], mask[:, :, :]).then_inc(maskb_ready, 1)

            def weigh(b, i, s):
                dve.wait_ge(ex_ready, 2 * b + 2)
                ch.link(dve.tensor_tensor(ex[:, :, :], ex[:, :, :], mask[:, :, :], ALU.mult))
                dve.tensor_reduce(picked[:, :], ex[:, :, :], AX.X, ALU.add)
                ch.link(dve.reciprocal(coef[:, 0, :], total[:, :]))
                ch.link(dve.tensor_tensor(coef[:, 1, :], picked[:, :], coef[:, 0, :], ALU.mult))
                ch.link(dve.tensor_scalar(coef[:, 1, :], coef[:, 1, :], 1.1920929e-07, None, ALU.max))
                ch.link(dve.reciprocal(coef[:, 2, :], coef[:, 1, :]))
                ch.link(dve.tensor_tensor(coef[:, 2, :], coef[:, 2, :], coef[:, 0, :], ALU.mult))
                ch.link(dve.tensor_scalar(coef[:, 2, :], coef[:, 2, :], g.tg[:, 3:4], None, ALU.mult))
                if not (isinstance(b, int) and b < 2):
                    dve.wait_ge(table_out[s], 32 * i)
                dve.tensor_tensor(wrow[:, s, :, :], ex[:, :, :], coef[:, 2, :].unsqueeze(2).broadcast_to([P, QT, E1]),
                                  ALU.mult).then_inc(wrow_ready, 1)

            def slots(b, s):
                dve.wait_ge(rank_ready, b + 1)
                ch.link(dve.scalar_tensor_tensor(rank[:, :, :], mask[:, :, :], -4096.0,
                                                 ps[:, RANK, 0:QT * E1].rearrange("p (k e) -> p k e", k=QT),
                                                 ALU.mult, ALU.add))
                ch.link(dve.tensor_scalar(ranki[:, :, :], rank[:, :, :], 4096.0, None, ALU.add))
                dve.tensor_scalar(hi[:, :, :], ranki[:, :, :], 4, None, ALU.logical_shift_right)
                ch.link(dve.tensor_scalar(lo[:, :, :], ranki[:, :, :], 15, None, ALU.bitwise_and))
                dve.tensor_copy(hif[:, :, :], hi[:, :, :])
                ch.link(dve.tensor_copy(lof[:, :, :], lo[:, :, :]))
                ch.link(dve.tensor_tensor(seen[:, 1 - s, :], seen[:, s, :], maskb[:, 0, :], ALU.add))
                ch.link(dve.tensor_tensor(seen[:, 1 - s, :], seen[:, 1 - s, :], maskb[:, 1, :], ALU.add))
                if not (isinstance(b, int) and b == 0):
                    dve.wait_ge(hot_used, b)
                iota = g.iota_b[:, :].unsqueeze(1).broadcast_to([P, E1, RB])
                for k in range(QT):
                    dve.tensor_tensor(hot_a[:, k, :, :], hif[:, k, :].unsqueeze(2).broadcast_to([P, E1, RA]),
                                      iota[:, :, 0:RA], ALU.is_equal)
                    ins = dve.tensor_tensor(bb[:, k, :, :], lof[:, k, :].unsqueeze(2).broadcast_to([P, E1, RB]), iota,
                                            ALU.is_equal)
                ch.link(ins)
                for k in range(QT):
                    dve.tensor_scalar(aa[:, k, :, 0:RA], hot_a[:, k, :, :], g.iota_p[:, 0:1], None, ALU.mult)
                    ins = dve.tensor_scalar(aa[:, k, :, RA:2 * RA], hot_a[:, k, :, :], g.iota_t[:, ds(2 * b + k, 1)], None,
                                            ALU.mult)
                ins.then_inc(hot_ready, 1)

            def hidden(b, f):
                dve.wait_ge(sil_ready, KF * b + f + 1)
                if f == 0 and not (isinstance(b, int) and b == 0):
                    dve.wait_ge(out_ready, b)
                dve.tensor_tensor(gt[:, f, :], ps[:, UP + f % 2, S:2 * S], sil[:, f % 2, :], ALU.mult).then_inc(gt_ready, 1)

            def residual(b, i, s):
                dve.wait_ge(out_ready, b + 1)
                if not (isinstance(b, int) and b < 2):
                    dve.wait_ge(base_out[s], 16 * i)
                dve.scalar_tensor_tensor(base[:, s, :, :], ps[:, OUT, :].rearrange("p (k d) -> p k d", k=QT),
                                         g.tg[:, 3:4], g.x[:, ds(2 * b, 2), :], ALU.mult, ALU.add).then_inc(base_ready, 1)

            def front(b, i, s):
                pick(b)
                weigh(b, i, s)
                slots(b, s)
                ch.end()

            normalise(0, 0, 0)
            front(0, 0, 0)

            def body(b, i, s):
                last = isinstance(b, int) and b == B - 1
                if not last:
                    normalise(b + 1, i + s, 1 - s)
                hidden(b, 0)
                hidden(b, 1)
                if not last:
                    pick(b + 1)
                hidden(b, 2)
                hidden(b, 3)
                if not last:
                    weigh(b + 1, i + s, 1 - s)
                hidden(b, 4)
                hidden(b, 5)
                if not last:
                    slots(b + 1, 1 - s)
                    ch.end()
                residual(b, i, s)

            steps(dve, B, body)
            dve.wait_ge(hot_used, B)
            for i in range(4):
                dve.tensor_copy(tt[32 * i:32 * i + 32, :, :],
                                ps[32 * i:32 * i + 32, LIST:LIST + 2, :].rearrange("p n (g c) -> p (n g) c", c=4 * RB)[
                                    :, :, i * RB:(i + 1) * RB]).then_inc(tt_ready, 1)
            ct = Chain(dve, tchain, 4)
            dve.wait_ge(pair_in, 16)
            ct.link(dve.tensor_scalar(tok[:, 0, :], pair[:, 1, :], 0.0, float(P), ALU.is_equal, ALU.mult))
            dve.tensor_scalar(tok[:, 1, :], pair[:, 1, :], 0.0, None, ALU.is_equal)
            ct.link(dve.scalar_tensor_tensor(tok[:, 2, :], pair[:, 1, :], float(P), pair[:, 0, :], ALU.mult, ALU.add))
            dve.scalar_tensor_tensor(tok[:, 2, :], tok[:, 2, :], -float(P), tok[:, 0, :], ALU.add, ALU.add)
            ct.link(dve.tensor_tensor(tok[:, 1, :], tok[:, 1, :], g.iota_slot[0:E1, :], ALU.mult))
            ct.link(dve.tensor_tensor(tok[:, 2, :], tok[:, 2, :], tok[:, 1, :], ALU.add))
            ct.end()
            dve.tensor_copy(tok[:, 1, :], tok[:, 2, :]).then_inc(tok_ready, 1)
            dve.wait_ge(tok_turned, 1)
            dve.tensor_copy(g.list_a[:, :], ps[:, TURN, 0:E1])
            dve.tensor_copy(g.list_b[:, :], ps[0:CAPX, TURN, E1:2 * E1])

        @block.scalar
        def _(act):
            act.wait_ge(var_eps, 1)
            act.activation(g.rstd[:, :], g.rstd[:, :], ACT.Sqrt).then_inc(rooted, 1)

            def keep_yt(b, s):
                act.wait_ge(yt_turned, b + 1)
                if not (isinstance(b, int) and b < 2):
                    act.wait_ge(up_ready, KF * (b - 1))
                act.activation(yt[:, s, :, :], ps[:, TURN, :].rearrange("p (k q) -> p k q", k=2), ACT.Copy).then_inc(yt_ready, 1)

            def exps(b):
                act.wait_ge(neg_ready, b + 1)
                if not (isinstance(b, int) and b < 1):
                    act.wait_ge(wrow_ready, b)
                for k in range(QT):
                    act.activation(ex[:, k, :], lg[:, k, :], ACT.Exp, bias=neg[:, k:k + 1], accum_out=total[:, k:k + 1]
                                   ).then_inc(ex_ready, 1)

            def silu(b, f):
                act.wait_ge(up_ready, KF * b + f + 1)
                if not (isinstance(b, int) and b == 0 and f < 2):
                    act.wait_ge(gt_ready, KF * b + f - 1)
                act.activation(sil[:, f % 2, :], ps[:, UP + f % 2, 0:S], ACT.Silu).then_inc(sil_ready, 1)

            keep_yt(0, 0)
            exps(0)

            def body(b, i, s):
                last = isinstance(b, int) and b == B - 1
                silu(b, 0)
                if not last:
                    keep_yt(b + 1, 1 - s)
                silu(b, 1)
                silu(b, 2)
                if not last:
                    exps(b + 1)
                for f in (3, 4, 5):
                    silu(b, f)

            steps(act, B, body)

        @block.tensor
        def _(pe):
            pe.wait_ge(loaded, 32)
            pe.wait_ge(zeroed, 4)
            for n in range(2):
                pe.matmul(ps[:, LIST + n, :], g.ones_bf[:, :], zero[:, :], start=True, stop=False, skip_group_check=True)

            def turn(b, s):
                pe.wait_ge(y_ready, b + 1)
                if not (isinstance(b, int) and b == 0):
                    pe.wait_ge(yt_ready, b)
                for d in range(2):
                    for k in range(QT):
                        ins = pe.transpose(ps[:, TURN, d * S + k * P:d * S + (k + 1) * P], y[:, s, k, d * P:(d + 1) * P],
                                           g.ident[:, :])
                ins.then_inc(yt_turned, 1)

            def logits(b, s):
                pe.wait_ge(yt_ready, b + 1)
                if not (isinstance(b, int) and b == 0):
                    pe.wait_ge(neg_ready, b)
                for k in range(QT):
                    for d in range(2):
                        ins = pe.matmul(ps[:, LOGIT, k * E1:(k + 1) * E1], yt[:, s, d, k * P:(k + 1) * P], wg[:, d, :],
                                        start=(d == 0), stop=(d == 1))
                ins.then_inc(lg_ready, 1)

            def ranks(b, s):
                pe.wait_ge(maskb_ready, b + 1)
                if not (isinstance(b, int) and b == 0):
                    pe.wait_ge(hot_ready, b)
                for k in range(QT):
                    o = ps[:, RANK, k * E1:(k + 1) * E1]
                    pe.matmul(o, g.ones_bf[:, :], seen[:, s, :], start=True, stop=False)
                    if k == 1:
                        pe.matmul(o, g.ones_bf[:, :], maskb[:, 0, :], start=False, stop=False)
                    ins = pe.matmul(o, g.tri[:, :], maskb[:, k, :], start=False, stop=True)
                ins.then_inc(rank_ready, 1)

            def lists(b):
                pe.wait_ge(hot_ready, b + 1)
                for k in range(QT):
                    for q in range(E1 // 4):
                        ins = pe.matmul(ps[:, LIST + q // 8, (q % 8) * 4 * RB:(q % 8 + 1) * 4 * RB],
                                        aa[:, k, 4 * q:4 * q + 4, :], bb[:, k, 4 * q:4 * q + 4, :],
                                        start=False, stop=True, skip_group_check=True)
                ins.then_inc(hot_used, 1)

            def up(b, s, f):
                if not (isinstance(b, int) and b == 0 and f < 2):
                    pe.wait_ge(gt_ready, KF * b + f - 1)
                for c, m in ((0, KF + f), (S, f)):
                    for d in range(2):
                        ins = pe.matmul(ps[:, UP + f % 2, c:c + S], sw1[:, d, m * P:(m + 1) * P], yt[:, s, d, :],
                                        start=(d == 0), stop=(d == 1))
                ins.then_inc(up_ready, 1)

            def down(b):
                pe.wait_ge(gt_ready, KF * b + KF)
                if not (isinstance(b, int) and b == 0):
                    pe.wait_ge(base_ready, b)
                for k in range(QT):
                    for f in range(KF):
                        ins = pe.matmul(ps[:, OUT, k * D:(k + 1) * D], gt[:, f, k * P:(k + 1) * P], sw2[:, f, :],
                                        start=(f == 0), stop=(f == KF - 1))
                ins.then_inc(out_ready, 1)

            turn(0, 0)
            logits(0, 0)
            ranks(0, 0)

            def body(b, i, s):
                last = isinstance(b, int) and b == B - 1
                up(b, s, 0)
                if not last:
                    turn(b + 1, 1 - s)
                up(b, s, 1)
                if not last:
                    logits(b + 1, 1 - s)
                up(b, s, 2)
                lists(b)
                up(b, s, 3)
                if not last:
                    ranks(b + 1, 1 - s)
                up(b, s, 4)
                up(b, s, 5)
                down(b)

            steps(pe, B, body)
            pe.wait_ge(tok_ready, 1)
            pe.wait_ge(yt_ready, B)
            pe.transpose(ps[:, TURN, 0:E1], tok[:, 1, 0:P], g.ident[0:E1, 0:E1])
            pe.transpose(ps[0:CAPX, TURN, E1:2 * E1], tok[:, 1, P:CAP], g.ident[0:E1, 0:E1]).then_inc(tok_turned, 1)


def experts(nc, g, a):
    with ExitStack() as ctx:
        def sb(name, shape, dt=F32):
            return ctx.enter_context(nc.sbuf_tensor(name, shape, dt))

        def sem(name):
            return ctx.enter_context(nc.semaphore(name))

        W1 = 2 * 2 * FF
        HF = KF // 2
        w1 = [g.wring[:, s, 0:W1].rearrange("p (k f) -> p k f", k=2) for s in range(RING)]
        w2 = [g.wring[:, s, W1:WCOLS].rearrange("p (k d) -> p k d", k=KF) for s in range(RING)]
        rows_a = sb("rows_a", [P, RING], U32)
        rows_b = sb("rows_b", [CAPX, RING], U32)
        xa = sb("xa", [P, 2, ROW])
        xb = sb("xb", [CAPX, 2, ROW])
        wa = sb("wa", [P, RING])
        wb = sb("wb", [CAPX, RING])
        xt = sb("xt", [P, 2, 2, CAP])
        sil = sb("sil3", [P, 2, HF, CAP])
        gt = sb("gt3", [P, 2, KF, CAP])
        zt = sb("zt", [P, 2, 2, CAP])
        za = sb("za", [P, 2, D])
        zb = sb("zb", [CAPX, 2, D])
        names = ("x_rows", "x_turned", "x_ready", "x_weights", "x_up", "x_sil", "x_gt", "x_down", "x_zt", "x_zturned",
                 "x_z", "x_added")
        (rows_ready, turned, xt_ready, weights_kept, up_ready, sil_ready, gt_ready, down_ready, zt_ready, z_turned,
         z_ready, added) = [sem(n) for n in names]
        gathered = [sem(f"gathered{s}") for s in (0, 1)]
        ps = g.ps
        UP, DOWN, BACK, TURN = 0, 4, 5, 6
        block = ctx.enter_context(nc.Block())

        @block.sync
        def _(sp):
            def load(e, i, s):
                if isinstance(e, int) and e < RING:
                    return
                sp.wait_ge(down_ready, e - RING + 1)
                apart(sp)
                sp.dma_start(g.wring[:, s, :], a["experts"][ds(e, 1), :, :].rearrange("o p n -> p (o n)")
                             ).then_inc(g.w_loaded[s], 16)

            steps(sp, E1, load, RING)

        @block.gpsimd
        def _(pool):
            def gather(e, s):
                if not (isinstance(e, int) and e < RING):
                    pool.wait_ge(added, 32 * (e - RING + 1))
                apart(pool)
                nc.gpsimd.tensor_copy(rows_a[:, s:s + 1], g.list_a[:, ds(e, 1)]).then_inc(rows_ready, 1)
                nc.gpsimd.tensor_copy(rows_b[:, s:s + 1], g.list_b[:, ds(e, 1)]).then_inc(rows_ready, 1)
                pool.wait_ge(rows_ready, 2 * e + 2)
                if not (isinstance(e, int) and e < 2):
                    pool.wait_ge(turned, e - 1)
                    pool.wait_ge(weights_kept, e - 1)
                apart(pool)
                pool.indirect_dma_start(xa[:, s % 2, :], None, g.table,
                                        bass.IndirectOffsetOnAxis(ap=rows_a[:, s:s + 1], axis=0)).then_inc(gathered[s % 2], 16)
                pool.indirect_dma_start(xb[:, s % 2, :], None, g.table,
                                        bass.IndirectOffsetOnAxis(ap=rows_b[:, s:s + 1], axis=0)).then_inc(gathered[s % 2], 16)

            def add(e, s):
                pool.wait_ge(z_ready, e + 1)
                if not (isinstance(e, int) and e == 0):
                    pool.wait_ge(added, 32 * e)
                apart(pool)
                pool.indirect_dma_start(a["out"], bass.IndirectOffsetOnAxis(ap=rows_a[:, s:s + 1], axis=0),
                                        za[:, s % 2, :], None, compute_op=ALU.add).then_inc(added, 16)
                pool.indirect_dma_start(a["out"], bass.IndirectOffsetOnAxis(ap=rows_b[:, s:s + 1], axis=0),
                                        zb[:, s % 2, :], None, compute_op=ALU.add).then_inc(added, 16)

            gather(0, 0)
            gather(1, 1)

            def body(e, i, s):
                if not (isinstance(e, int) and e < 2):
                    add(e - 2, (s - 2) % RING)
                if not (isinstance(e, int) and e >= E1 - 2):
                    gather(e + 2, (s + 2) % RING)

            steps(pool, E1, body, RING)
            add(E1 - 2, (E1 - 2) % RING)
            add(E1 - 1, (E1 - 1) % RING)
            pool.wait_ge(added, 32 * E1)

        @block.vector
        def _(dve):
            def keep_weights(e, i2, s):
                dve.wait_ge(gathered[s % 2], 32 * (i2 + 1))
                if not (isinstance(e, int) and e < RING):
                    dve.wait_ge(z_ready, e - RING + 1)
                apart(dve)
                dve.tensor_copy(wa[:, s:s + 1], xa[:, s % 2, ds(e + D, 1)])
                dve.tensor_copy(wb[:, s:s + 1], xb[:, s % 2, ds(e + D, 1)]).then_inc(weights_kept, 1)

            def hidden(e, s, h):
                dve.wait_ge(sil_ready, 2 * e + h + 1)
                if h == 0 and not (isinstance(e, int) and e < 2):
                    dve.wait_ge(down_ready, e - 1)
                dve.tensor_tensor(gt[:, s % 2, h * HF:(h + 1) * HF, :],
                                  ps[:, UP + 2 * h + 1, 0:HF * CAP].rearrange("p (f c) -> p f c", c=CAP),
                                  sil[:, h, :, :], ALU.mult).then_inc(gt_ready, 1)

            def scale(e, s):
                dve.wait_ge(z_turned, e + 1)
                dve.wait_ge(weights_kept, e + 1)
                if not (isinstance(e, int) and e < 2):
                    dve.wait_ge(added, 32 * (e - 1))
                dve.tensor_scalar(za[:, s % 2, :], ps[:, BACK, 0:D], wa[:, s:s + 1], None, ALU.mult)
                dve.tensor_scalar(zb[:, s % 2, :], ps[0:CAPX, BACK, D:2 * D], wb[:, s:s + 1], None, ALU.mult).then_inc(z_ready, 1)

            def body(e, i, s):
                keep_weights(e, 2 * i + s // 2, s)
                hidden(e, s, 0)
                if not (isinstance(e, int) and e < 2):
                    scale(e - 2, (s - 2) % RING)
                hidden(e, s, 1)

            steps(dve, E1, body, RING)
            scale(E1 - 2, (E1 - 2) % RING)
            scale(E1 - 1, (E1 - 1) % RING)

        @block.scalar
        def _(act):
            def keep_xt(e, s):
                act.wait_ge(turned, e + 1)
                if not (isinstance(e, int) and e < 2):
                    act.wait_ge(up_ready, 2 * (e - 1))
                act.activation(xt[:, s % 2, :, :], ps[:, TURN, 0:2 * CAP].rearrange("p (k c) -> p k c", k=2), ACT.Copy
                               ).then_inc(xt_ready, 1)

            def silu(e, h):
                act.wait_ge(up_ready, 2 * e + h + 1)
                if not (isinstance(e, int) and e == 0):
                    act.wait_ge(gt_ready, 2 * e + h - 1)
                act.activation(sil[:, h, :, :], ps[:, UP + 2 * h, 0:HF * CAP].rearrange("p (f c) -> p f c", c=CAP), ACT.Silu
                               ).then_inc(sil_ready, 1)

            def keep_zt(e, s):
                act.wait_ge(down_ready, e + 1)
                if not (isinstance(e, int) and e < 2):
                    act.wait_ge(z_turned, e - 1)
                act.activation(zt[:, s % 2, :, :], ps[:, DOWN, 0:2 * CAP].rearrange("p (k c) -> p k c", k=2), ACT.Copy
                               ).then_inc(zt_ready, 1)

            keep_xt(0, 0)

            def body(e, i, s):
                silu(e, 0)
                if not (isinstance(e, int) and e == E1 - 1):
                    keep_xt(e + 1, (s + 1) % RING)
                silu(e, 1)
                if not (isinstance(e, int) and e == 0):
                    keep_zt(e - 1, (s - 1) % RING)

            steps(act, E1, body, RING)
            keep_zt(E1 - 1, (E1 - 1) % RING)

        @block.tensor
        def _(pe):
            def turn(e, i2, s):
                pe.wait_ge(gathered[s % 2], 32 * (i2 + 1))
                if not (isinstance(e, int) and e == 0):
                    pe.wait_ge(xt_ready, e)
                for k in range(2):
                    pe.transpose(ps[:, TURN, k * CAP:k * CAP + P], xa[:, s % 2, k * P:(k + 1) * P], g.ident[:, :])
                    ins = pe.transpose(ps[:, TURN, k * CAP + P:(k + 1) * CAP], xb[:, s % 2, k * P:(k + 1) * P],
                                       g.ident[0:CAPX, 0:CAPX])
                ins.then_inc(turned, 1)

            def up(e, i, s, h):
                if h == 0:
                    pe.wait_ge(xt_ready, e + 1)
                    pe.wait_ge(g.w_loaded[s], 16 * (i + 1))
                if not (isinstance(e, int) and e == 0):
                    pe.wait_ge(gt_ready, 2 * e + h - 1)
                for n, m in ((0, KF), (1, 0)):
                    for f in range(HF):
                        c = (m + h * HF + f) * P
                        for d in range(2):
                            ins = pe.matmul(ps[:, UP + 2 * h + n, f * CAP:(f + 1) * CAP], w1[s][:, d, c:c + P],
                                            xt[:, s % 2, d, :], start=(d == 0), stop=(d == 1))
                ins.then_inc(up_ready, 1)

            def down(e, s):
                pe.wait_ge(gt_ready, 2 * e + 2)
                if not (isinstance(e, int) and e == 0):
                    pe.wait_ge(zt_ready, e)
                for d in range(2):
                    for f in range(KF):
                        ins = pe.matmul(ps[:, DOWN, d * CAP:(d + 1) * CAP], w2[s][:, f, d * P:(d + 1) * P],
                                        gt[:, s % 2, f, :], start=(f == 0), stop=(f == KF - 1))
                ins.then_inc(down_ready, 1)

            def turn_back(e, s):
                pe.wait_ge(zt_ready, e + 1)
                if not (isinstance(e, int) and e == 0):
                    pe.wait_ge(z_ready, e)
                for d in range(2):
                    pe.transpose(ps[:, BACK, d * P:(d + 1) * P], zt[:, s % 2, d, 0:P], g.ident[:, :])
                    ins = pe.transpose(ps[0:CAPX, BACK, D + d * P:D + (d + 1) * P], zt[:, s % 2, d, P:CAP], g.ident[:, :])
                ins.then_inc(z_turned, 1)

            turn(0, 0, 0)

            def body(e, i, s):
                up(e, i, s, 0)
                if not (isinstance(e, int) and e < 2):
                    turn_back(e - 2, (s - 2) % RING)
                if not (isinstance(e, int) and e == E1 - 1):
                    turn(e + 1, 2 * i + (s + 1) // 2, (s + 1) % RING)
                up(e, i, s, 1)
                if not (isinstance(e, int) and e == 0):
                    down(e - 1, (s - 1) % RING)

            steps(pe, E1, body, RING)
            turn_back(E1 - 2, (E1 - 2) % RING)
            down(E1 - 1, (E1 - 1) % RING)
            turn_back(E1 - 1, (E1 - 1) % RING)


def program(nc, a):
    with ExitStack() as ctx:
        def sb(name, shape, dt=F32):
            return ctx.enter_context(nc.sbuf_tensor(name, shape, dt))

        g = Shared()
        g.ps = ctx.enter_context(nc.psum_tensor("ps", [P, 8, 512], F32))
        g.x = sb("x_state", [P, T, D])
        g.mv = sb("mv", [P, T, 2])
        g.rstd = sb("rstd", [P, T])
        g.ident = sb("ident", [P, P])
        g.tri = sb("tri", [P, P], BF16)
        g.ones_bf = sb("ones_bf", [P, P], BF16)
        g.row0_bf = sb("row0_bf", [P, P], BF16)
        g.ones_f = sb("ones_f", [1, P])
        g.esel = sb("esel", [P, H1, P], BF16)
        g.iota8 = sb("iota8", [P, E0])
        g.iota_b = sb("iota_b", [P, RB])
        g.iota_p = sb("iota_p", [P, 1])
        g.iota_t = sb("iota_t", [P, T])
        g.iota_slot = sb("iota_slot", [P, CAP])
        g.maskcol = sb("maskcol", [P, QT, B])
        g.bm0 = sb("bm0", [P, QT, B])
        g.bm1 = sb("bm1", [P, QT, B])
        g.tg = sb("tg", [P, 4])
        g.wring = sb("wring", [P, RING, WCOLS])
        g.w_loaded = [ctx.enter_context(nc.semaphore(f"w_loaded{k}")) for k in range(RING)]
        g.bm_dram = nc.dram_tensor("bm_dram", [B, 4, S], F32).ap()
        setup(nc, g, a)
        attn0(nc, g, a)
        ffn0(nc, g, a)
        attn1(nc, g, a)
        g.list_a = sb("list_a", [P, E1], U32)
        g.list_b = sb("list_b", [CAPX, E1], U32)
        g.table = nc.dram_tensor("table", [NT + CAP, ROW], F32).ap()
        g.lists = nc.dram_tensor("lists", [E1, 2, CAP], F32).ap()
        route(nc, g, a)
        experts(nc, g, a)

def lay_out(inputs):
    import numpy as np
    n = {k: np.asarray(v) for k, v in inputs.items()}
    E, F2, H = n["L1_ffn_expert_w1"].shape
    F = F2 // 2

    def rows(w):
        k = w.shape[-2] // 128
        return np.swapaxes(w.reshape(*w.shape[:-2], k, 128, w.shape[-1]), -3, -2).reshape(
            *w.shape[:-2], 128, k * w.shape[-1])

    def everywhere(v, shape):
        return np.broadcast_to(v, shape)

    out = {
        "x": n["x"].reshape(2048, 256),
        "ctx": n["ctx_2048"],
        "ctx_t": n["ctx_2048"].transpose(0, 2, 1),
        "seq": everywhere(n["itok_Bx1_68_817"].reshape(1, 8), (128, 8)),
        "b": n["L0_xattn_b"].reshape(2, 128).T,
        "gates": everywhere(np.stack([n["g_xattn"][0], n["g_ffn"][0], n["g_xattn"][1], n["g_ffn"][1]]).reshape(1, 4), (128, 4)),
        "maskcol": n["mask_BxS2_fk1"].reshape(8, 2, 128).transpose(2, 1, 0),
        "maskrow": n["mask_BxS2_fk1"].reshape(1, 2048),
        "router_w": rows(n["L0_ffn_router_w"]),
        "router_b": n["L0_ffn_router_b"].reshape(1, 8),
        "ew0": n["L0_ffn_expert_w"].reshape(8, 2, 128, 256).transpose(2, 1, 0, 3).reshape(128, 4096),
        "eb0": n["L0_ffn_expert_b"],
        "w_tgt": rows(n["L1_xattn_W_tgt"].T),
        "w_src": rows(n["L1_xattn_W_src"].T),
        "w_out": rows(n["L1_xattn_W_out"].T),
        "b_tgt": n["L1_xattn_b_tgt"].reshape(2, 128).T,
        "b_key": n["L1_xattn_b_src"][:256].reshape(2, 128).T,
        "b_val": everywhere(n["L1_xattn_b_src"][256:].reshape(1, 256), (128, 256)),
        "b_out": everywhere(n["L1_xattn_b_out"].reshape(1, 256), (128, 256)),
        "wg": rows(n["L1_ffn_wg"].T),
        "shared": np.concatenate([rows(n["L1_ffn_shared_w1"].T), rows(n["L1_ffn_shared_w2"].T)], axis=1),
        "experts": np.concatenate([rows(n["L1_ffn_expert_w1"].transpose(0, 2, 1)),
                                   rows(n["L1_ffn_expert_w2"].transpose(0, 2, 1))], axis=2),
    }
    return {k: np.ascontiguousarray(v) for k, v in out.items()}


def kernel(**inputs):
    import concourse.bacc as _bacc
    from concourse import mybir as _mybir
    from concourse.bass_utils import run_bass_kernel_spmd as _run

    nc = _bacc.Bacc("TRN2", target_bir_lowering=False, num_devices=1)
    arrays = lay_out(inputs)
    aps = {k: nc.dram_tensor("in_" + k, v.shape, _mybir.dt.from_np(v.dtype), kind="ExternalInput").ap()
           for k, v in arrays.items()}
    aps["out"] = nc.dram_tensor("out", (NT + CAP, D), F32, kind="ExternalOutput").ap()
    program(nc, aps)
    r = _run(nc, [{"in_" + k: v for k, v in arrays.items()}], core_ids=[0])
    return r.results[0]["out"][0:NT].reshape(B, S, D)
```

```python
from contextlib import ExitStack

import concourse.bass as bass
from concourse import mybir

F32 = mybir.dt.float32
BF16 = mybir.dt.bfloat16
I32 = mybir.dt.int32
U32 = mybir.dt.uint32
ALU = mybir.AluOpType
ACT = mybir.ActivationFunctionType
AX = mybir.AxisListType
ds = bass.ds

P = 128
B, S, D = 8, 256, 256
CTX = 512
T = B * S // P
NT = B * S
QT = S // P
EPS = 1e-5
H0, DH0 = 16, 16
E0 = 8
H1, DH1 = 8, 32
E1, TOPK, FF, CAP = 64, 8, 768, 160
KF = FF // P
RA, RB = CAP // 16, 16
CAPX = CAP - P
ROW = D + E1
MASKED0 = -1e12
MASKED1 = -1e30
NEG = -3.0e38
WCOLS = 2 * 2 * FF + KF * D
RING = 4
PARTS = 4
KV_LOADS = 9


class Shared:
    pass


class Chain:

    def __init__(self, eng, sem, per_step):
        self.eng, self.sem, self.per_step = eng, sem, per_step
        self.base = self.k = 0

    def step(self, n):
        self.base, self.k = n * self.per_step, 0

    def end(self):
        assert self.k == self.per_step, self.k

    def link(self, ins):
        ins.then_inc(self.sem, 1)
        self.k += 1
        self.eng.wait_ge(self.sem, self.base + self.k)


def steps(eng, n, body, slots=2):
    for k in range(slots):
        body(k, 0, k)
    with eng.Fori(1, n // slots - 1) as i:
        for k in range(slots):
            body(slots * i + k, i, k)
    for k in range(n - slots, n):
        body(k, n // slots - 1, k % slots)


def apart(eng):
    eng.nop(nofuse=True)


def scale_of_rows(dve, g, var_eps, rooted, scale_ready):
    dve.tensor_scalar(g.rstd[:, :], g.mv[:, :, 1], EPS, None, ALU.add).then_inc(var_eps, 1)
    dve.wait_ge(rooted, 1)
    dve.reciprocal(g.rstd[:, :], g.rstd[:, :]).then_inc(scale_ready, 1)
    dve.wait_ge(scale_ready, 1)


def root_of_variance(act, g, var_eps, rooted):
    act.wait_ge(var_eps, 1)
    act.activation(g.rstd[:, :], g.rstd[:, :], ACT.Sqrt).then_inc(rooted, 1)


def head_keys(a, b):
    return a["ctx_t"][ds(b, 1), 0:D, :].rearrange("o (g j d) k -> j d (o g) k", j=4, d=DH0)


def load_keys(sp, g, a, b, s):
    for j in range(4):
        sp.dma_start(g.kz[32 * j + 2:32 * j + 2 + DH0, s, j:H0:4, :], head_keys(a, b)[j]).then_inc(g.kv_loaded[s], 16)
    sp.dma_start(g.vraw[:, s, :, :],
                 a["ctx"][ds(b, 1), :, D:2 * D].rearrange("o (k p) d -> p (o k) d", p=P)).then_inc(g.kv_loaded[s], 16)


def load_biases(sp, g, b, s):
    for j in range(4):
        sp.dma_start(g.kz[32 * j:32 * j + 2, s, j:H0:4, :], g.bm_dram[ds(b, 1), :, :, :].rearrange("o r g k -> r (o g) k")
                     ).then_inc(g.kv_loaded[s], 16)


def load_narrow_keys(pool, g, a, b, s):
    for j in range(4):
        pool.dma_start(g.kzb[32 * j + 2:32 * j + 2 + DH0, s, j:H0:4, :], head_keys(a, b)[j]).then_inc(g.kb_loaded[s], 16)


def load_narrow_biases(pool, g, b, s):
    for j in range(4):
        pool.dma_start(g.kzb[32 * j:32 * j + 2, s, j:H0:4, :], g.bm_dram[ds(b, 1), :, :, :].rearrange("o r g k -> r (o g) k")
                       ).then_inc(g.kb_loaded[s], 16)


def load_expert(sp, g, a, e):
    for c in range(PARTS):
        n = slice(c * WCOLS // PARTS, (c + 1) * WCOLS // PARTS)
        sp.dma_start(g.wring[:, e, n], a["experts"][e, :, n]).then_inc(g.w_loaded[e], 16)


def setup(nc, g, a):
    with ExitStack() as ctx:
        def sb(name, shape, dt=F32):
            return ctx.enter_context(nc.sbuf_tensor(name, shape, dt))

        def sem(name):
            return ctx.enter_context(nc.semaphore(name))

        seq = sb("seq", [P, B], I32)
        seqf = sb("seqf", [P, B])
        bcol = sb("bcol", [P, QT])
        kpos = sb("kpos", [P, QT])
        valid = sb("valid", [P, QT, B])
        gates = sb("gates", [P, 4])
        bmrow = sb("bmrow", [B, 2, S])
        st = sb("st_setup", [P, T, 6])
        maskrow = sb("maskrow", [1, B * S])
        x_in, small_in, iotas, masks_made, mask_turned, row_made, row_out, chain, rows_in = [
            sem(n) for n in ("x_in", "small_in", "iotas", "masks_made", "mask_turned", "row_made",
                             "row_out", "su_chain", "rows_in")]
        zeroed, consts, padded, narrow_padded = sem("zeroed"), sem("consts"), sem("padded"), sem("narrow_padded")
        aggr, tanhs = sem("aggr"), sem("tanhs")
        block = ctx.enter_context(nc.Block())

        @block.sync
        def _(sp):
            sp.dma_start(g.x[:, :, :], a["x"].rearrange("(t p) d -> p t d", p=P)).then_inc(x_in, 16)
            sp.dma_start(seq[:, :], a["seq"]).then_inc(small_in, 16)
            sp.dma_start(bcol[:, :], a["b"]).then_inc(small_in, 16)
            sp.dma_start(gates[:, :], a["gates"]).then_inc(small_in, 16)
            sp.dma_start(g.maskcol[:, :, :], a["maskcol"]).then_inc(small_in, 16)
            for b in (0, 1):
                sp.wait_ge(padded, b + 1)
                load_keys(sp, g, a, b, b)
            sp.wait_ge(row_made, QT)
            for r in range(4):
                sp.dma_start(g.bm_dram[:, :, r, :], bmrow[:, :, :]).then_inc(row_out, 16)
            sp.wait_ge(row_out, 64)

        @block.gpsimd
        def _(pool):
            nc.gpsimd.memset(g.ident[:, :], 0.0).then_inc(zeroed, 1)
            nc.gpsimd.memset(g.tri[:, :], 1.0).then_inc(zeroed, 1)
            nc.gpsimd.memset(g.ones_bf[:, :], 1.0).then_inc(zeroed, 1)
            nc.gpsimd.memset(g.esel[:, :, :], 1.0).then_inc(zeroed, 1)
            nc.gpsimd.memset(g.ones_f[:, :], 1.0).then_inc(zeroed, 1)
            nc.gpsimd.memset(g.row0_bf[:, :], 0.0).then_inc(zeroed, 1)
            nc.gpsimd.iota(kpos[:, :], [[P, QT]], 0, 1, allow_small_or_imprecise_dtypes=True).then_inc(iotas, 1)
            nc.gpsimd.iota(g.iota8[:, :], [[1, E0]], 0, 0, allow_small_or_imprecise_dtypes=True).then_inc(iotas, 1)
            nc.gpsimd.iota(g.iota_b[:, :], [[1, RB]], 0, 0, allow_small_or_imprecise_dtypes=True).then_inc(iotas, 1)
            nc.gpsimd.iota(g.iota_p[:, :], [[1, 1]], 0, 1, allow_small_or_imprecise_dtypes=True).then_inc(iotas, 1)
            nc.gpsimd.iota(g.iota_t[:, :], [[1, T]], 1, 0, allow_small_or_imprecise_dtypes=True).then_inc(iotas, 1)
            nc.gpsimd.iota(g.iota_slot[:, :], [[1, CAP]], NT, 0, allow_small_or_imprecise_dtypes=True).then_inc(iotas, 1)
            pool.wait_ge(zeroed, 6)
            nc.gpsimd.affine_select(out=g.ident[:, :], in_=g.ident[:, :], compare_op=ALU.not_equal, fill=1.0,
                                    base=0, pattern=[[-1, P]], channel_multiplier=1).then_inc(consts, 1)
            nc.gpsimd.affine_select(out=g.tri[:, :], in_=g.tri[:, :], compare_op=ALU.is_ge, fill=0.0,
                                    base=-1, pattern=[[1, P]], channel_multiplier=-1).then_inc(consts, 1)
            nc.gpsimd.affine_select(out=g.esel[:, :, :], in_=g.esel[:, :, :], compare_op=ALU.is_equal, fill=0.0,
                                    base=0, pattern=[[-1, H1], [0, P]], channel_multiplier=1).then_inc(consts, 1)
            nc.gpsimd.memset(g.row0_bf[0:1, :], 1.0).then_inc(consts, 1)
            nc.gpsimd.memset(g.vaug[:, :, :, :, :], 0.0).then_inc(consts, 1)
            pool.wait_ge(consts, 5)
            nc.gpsimd.memset(g.vaug[:, :, :, :, DH0], 1.0)
            for b in (0, 1):
                pool.wait_ge(narrow_padded, b + 1)
                load_narrow_keys(pool, g, a, b, b)

        @block.vector
        def _(dve):
            ch = Chain(dve, chain, 4)
            dve.memset(g.kz[:, 0, :, :], 0.0).then_inc(padded, 1)
            dve.memset(bmrow[:, 0, :], 1.0)
            dve.wait_ge(small_in, 64)
            dve.wait_ge(iotas, 6)
            ch.link(dve.tensor_copy(seqf[:, :], seq[:, :]))
            for k in range(QT):
                ins = dve.tensor_scalar(valid[:, k, :], seqf[:, :], kpos[:, k:k + 1], None, ALU.is_gt)
            ch.link(ins)
            ch.link(dve.tensor_scalar(valid[:, :, :], valid[:, :, :], -1.0, -MASKED0, ALU.add, ALU.mult))
            for k in range(QT):
                ins = dve.tensor_scalar(g.bm0[:, k, :], valid[:, k, :], bcol[:, k:k + 1], None, ALU.add)
            ins.then_inc(masks_made, 1)
            ch.link(dve.tensor_scalar(g.bm1[:, :, :], g.maskcol[:, :, :], 0.0, MASKED1, ALU.is_equal, ALU.mult))
            for k in range(QT):
                dve.wait_ge(mask_turned, k + 1)
                dve.tensor_copy(bmrow[:, 1, k * P:(k + 1) * P], g.ps[0:B, k, 0:P]).then_inc(row_made, 1)
            dve.memset(g.kz[:, 1, :, :], 0.0).then_inc(padded, 1)
            dve.memset(g.kzb[:, 0, :, :], 0.0).then_inc(narrow_padded, 1)
            dve.memset(g.kzb[:, 1, :, :], 0.0).then_inc(narrow_padded, 1)
            dve.memset(g.qpad[:, :, :, :, :], 0.0)
            dve.wait_ge(x_in, 16)
            for t in range(T):
                ins = dve.bn_stats(st[:, t, :], g.x[:, t, :])
            ins.then_inc(aggr, 1)
            dve.wait_ge(aggr, 1)
            for t in range(T):
                ins = dve.bn_aggr(g.mv[:, t, :], st[:, t, :])
            ins.then_inc(aggr, 1)
            dve.wait_ge(aggr, 2)
            ch.end()

        @block.tensor
        def _(pe):
            pe.wait_ge(consts, 1)
            pe.wait_ge(masks_made, 1)
            for k in range(QT):
                pe.transpose(g.ps[0:B, k, 0:P], g.bm0[:, k, :], g.ident[:, :]).then_inc(mask_turned, 1)

        @block.scalar
        def _(act):
            act.wait_ge(small_in, 64)
            act.activation(g.tg[:, :], gates[:, :], ACT.Tanh).then_inc(tanhs, 1)
            act.wait_ge(tanhs, 1)


def attn0(nc, g, a):
    G = H0 // 4
    with ExitStack() as ctx:
        def sb(name, shape, dt=F32):
            return ctx.enter_context(nc.sbuf_tensor(name, shape, dt))

        def sem(name):
            return ctx.enter_context(nc.semaphore(name))

        qpad, kz, kzb, vraw, vaug = g.qpad, g.kz, g.kzb, g.vraw, g.vaug
        qtb = sb("qtb", [P, G, S], BF16)
        qt = sb("qt", [P, 2, G, S])
        pt = sb("pt", [P, 2, QT, 2, S])
        ot = sb("ot", [P, G, S])
        rec = sb("rec", [P, QT, H0])
        upd = sb("upd", [P, QT, H0, DH0])
        st = sb("st0", [P, QT, 6])
        mvb = sb("mvb0", [P, QT, 2])
        kv_loaded, kb_loaded = g.kv_loaded, g.kb_loaded
        weights_in = sem("weights_in")
        v_padded, q_ready, t1_done, qtb_ready = sem("v_padded"), sem("q_ready"), sem("t1_done"), sem("qtb_ready")
        max_ready, max_used, q2_ready, t2_done = sem("max_ready"), sem("max_used"), sem("q2_ready"), sem("t2_done")
        qt_ready, sc_ready, pt_ready, pv_done = sem("qt_ready"), sem("sc_ready"), sem("pt_ready"), sem("pv_done")
        ot_used, outt_done, fin_done, chain = sem("ot_used"), sem("outt_done"), sem("fin_done"), sem("a_chain")
        out_read = sem("out_read")
        ps = g.ps
        TB, MB, SB, QB, OB = 0, 2, 4, 6, 7
        var_eps, rooted, scale_ready = sem("a_var_eps"), sem("a_rooted"), sem("a_scale")
        block = ctx.enter_context(nc.Block())

        @block.sync
        def _(sp):
            def load(b, i, s):
                if isinstance(b, int) and b < 2:
                    load_biases(sp, g, b, s)
                else:
                    sp.wait_ge(sc_ready, 16 * (b - 1))
                    sp.wait_ge(v_padded, b - 1)
                    apart(sp)
                    load_keys(sp, g, a, b, s)
                    load_biases(sp, g, b, s)
                if isinstance(b, int) and b == 1:
                    load_weights()

            def load_weights():
                for dst, name in ((g.ew, "ew0"), (g.w_tgt, "w_tgt"), (g.w_src, "w_src"), (g.w_out, "w_out"), (g.sw, "shared"),
                                  (g.eb, "eb0"), (g.rw, "router_w"), (g.rb, "router_b"), (g.b_tgt, "b_tgt"),
                                  (g.b_key, "b_key"), (g.b_val, "b_val"), (g.b_out, "b_out"), (g.wg, "wg")):
                    sp.dma_start(dst, a[name]).then_inc(weights_in, 16)
                load_expert(sp, g, a, 3)

            steps(sp, B, load)
            sp.wait_ge(weights_in, 13 * 16)

        @block.gpsimd
        def _(pool):
            def prepare(b, i, s):
                if not (isinstance(b, int) and b < 2):
                    pool.wait_ge(max_ready, 16 * (b - 1))
                    apart(pool)
                    load_narrow_keys(pool, g, a, b, s)
                load_narrow_biases(pool, g, b, s)
                pool.wait_ge(kv_loaded[s], 16 * KV_LOADS * (i + 1))
                if not (isinstance(b, int) and b < 2):
                    pool.wait_ge(pv_done, 8 * (b - 1))
                apart(pool)
                nc.gpsimd.tensor_copy(vaug[:, s, :, :, 0:DH0],
                                      vraw[:, s, :, :].rearrange("p k (h d) -> p k h d", d=DH0)).then_inc(v_padded, 1)

            steps(pool, B, prepare)

        @block.vector
        def _(dve):
            ch = Chain(dve, chain, 5)
            scale_of_rows(dve, g, var_eps, rooted, scale_ready)
            dve.tensor_scalar(g.rstd[:, :], g.rstd[:, :], DH0 ** -0.5, None, ALU.mult).then_inc(scale_ready, 1)
            dve.wait_ge(scale_ready, 2)

            def queries(b, s):
                if not (isinstance(b, int) and b < 2):
                    dve.wait_ge(t2_done, b - 1)
                for k in range(QT):
                    dve.tensor_scalar(qpad[:, s, k, :, 2:2 + DH0],
                                      g.x[:, ds(2 * b + k, 1), :].rearrange("p o (h d) -> p (o h) d", d=DH0),
                                      g.mv[:, ds(2 * b + k, 1), 0], g.rstd[:, ds(2 * b + k, 1)],
                                      ALU.subtract, ALU.mult)
                dve.memset(qpad[:, s, :, :, 1], 1.0)
                dve.memset(qpad[:, s, :, :, 0], 0.0).then_inc(q_ready, 1)

            def maxima(b, s, u):
                j, k = u // 2, u % 2
                dve.wait_ge(max_ready, 16 * b + u + 1)
                dve.tensor_reduce(qpad[:, s, k, 2 * j:2 * j + 2, 0],
                                  ps[:, MB + u % 2, :].rearrange("p (h k) -> p h k", h=2), AX.X, ALU.max,
                                  negate=True).then_inc(max_used, 1)

            def mask_off(b, s):
                dve.memset(qpad[:, s, :, :, 1], 0.0).then_inc(q2_ready, 1)

            def keep_ot(b, q):
                dve.wait_ge(pv_done, 8 * b + 4 * q + 4)
                if q == 0 and not (isinstance(b, int) and b < 1):
                    dve.wait_ge(outt_done, b)
                dve.tensor_copy(ot[:, 2 * q:2 * q + 2, :], ps[:, OB, :].rearrange("p (g q) -> p g q", g=2)).then_inc(ot_used, 1)

            def finish(b):
                ch.step(b)
                dve.wait_ge(outt_done, b + 1)
                o = ps[:, TB:TB + 2, :].rearrange("p k (h d) -> p k h d", d=32)
                ch.link(dve.reciprocal(rec[:, :, :], o[:, :, :, DH0]))
                ch.link(dve.tensor_scalar(rec[:, :, :], rec[:, :, :], g.tg[:, 0:1], None, ALU.mult))
                dve.tensor_tensor(upd[:, :, :, :], o[:, :, :, 0:DH0],
                                  rec[:, :, :].unsqueeze(3).broadcast_to([P, QT, H0, DH0]), ALU.mult).then_inc(out_read, 1)
                dve.wait_ge(out_read, b + 1)
                xb = g.x[:, ds(2 * b, 2), :]
                dve.tensor_tensor(xb, xb, upd[:, :, :, :].rearrange("p k h d -> p k (h d)"), ALU.add).then_inc(fin_done, 1)
                dve.wait_ge(fin_done, b + 1)
                apart(dve)
                for k in range(QT):
                    ins = dve.bn_stats(st[:, k, :], g.x[:, ds(2 * b + k, 1), :].rearrange("p o d -> p (o d)"))
                ch.link(ins)
                apart(dve)
                for k in range(QT):
                    ins = dve.bn_aggr(mvb[:, k, :], st[:, k, :])
                ch.link(ins)
                apart(dve)
                ch.link(dve.tensor_copy(g.mv[:, ds(2 * b, 2), :], mvb[:, :, :]))
                ch.end()

            queries(0, 0)
            queries(1, 1)
            for u in range(16):
                maxima(0, 0, u)
            mask_off(0, 0)

            def body(b, i, s):
                last, last2 = isinstance(b, int) and b == B - 1, isinstance(b, int) and b >= B - 2
                if not (isinstance(b, int) and b == 0):
                    keep_ot(b - 1, 1)
                    finish(b - 1)
                if not last:
                    for u in range(8):
                        maxima(b + 1, 1 - s, u)
                keep_ot(b, 0)
                if not last:
                    for u in range(8, 16):
                        maxima(b + 1, 1 - s, u)
                    mask_off(b + 1, 1 - s)
                if not last2:
                    queries(b + 2, s)

            steps(dve, B, body)
            keep_ot(B - 1, 1)
            finish(B - 1)

        @block.scalar
        def _(act):
            root_of_variance(act, g, var_eps, rooted)

            def keep_qtb(b, k):
                act.wait_ge(t1_done, 2 * b + k + 1)
                act.activation(qtb[:, :, k * P:(k + 1) * P],
                               ps[:, QB, :].rearrange("p (g q) -> p g q", q=P), ACT.Copy).then_inc(qtb_ready, 1)

            def keep_qt(b, s):
                act.wait_ge(t2_done, b + 1)
                for k in range(QT):
                    act.activation(qt[:, s, :, k * P:(k + 1) * P],
                                   ps[:, TB + k, :].rearrange("p (g q) -> p g q", q=P), ACT.Copy).then_inc(qt_ready, 1)

            def exps(b, j, k):
                act.wait_ge(sc_ready, 16 * b + 2 * j + k + 1)
                if k == 0 and not (isinstance(b, int) and b == 0 and j < 2):
                    act.wait_ge(pv_done, 8 * b + j - 1)
                apart(act)
                act.activation(pt[:, j % 2, k, :, :], ps[:, SB + k, :].rearrange("p (h q) -> p h q", h=2),
                               ACT.Exp, bias=g.bm0[:, k, ds(b, 1)]).then_inc(pt_ready, 1)

            keep_qtb(0, 0)
            keep_qtb(0, 1)
            keep_qt(0, 0)

            def body(b, i, s):
                last = isinstance(b, int) and b == B - 1
                for j in range(8):
                    exps(b, j, 0)
                    if j == 7 and not last:
                        keep_qt(b + 1, 1 - s)
                    exps(b, j, 1)
                    if j < 2 and not last:
                        keep_qtb(b + 1, j)

            steps(act, B, body)

        @block.tensor
        def _(pe):
            def turn1(b, s, k):
                pe.wait_ge(q_ready, b + 1)
                if not (isinstance(b, int) and b == 0 and k == 0):
                    pe.wait_ge(qtb_ready, 2 * b + k)
                for q in range(G):
                    ins = pe.transpose(ps[:, QB, q * P:(q + 1) * P],
                                       qpad[:, s, k, 4 * q:4 * q + 4, :].rearrange("p h d -> p (h d)"), g.ident[:, :])
                ins.then_inc(t1_done, 1)

            def turn2(b, s):
                pe.wait_ge(q2_ready, b + 1)
                if not (isinstance(b, int) and b < 2):
                    pe.wait_ge(out_read, b - 1)
                for k in range(QT):
                    for q in range(G):
                        ins = pe.transpose(ps[:, TB + k, q * P:(q + 1) * P],
                                           qpad[:, s, k, 4 * q:4 * q + 4, :].rearrange("p h d -> p (h d)"), g.ident[:, :])
                ins.then_inc(t2_done, 1)

            def max_pass(b, i, s, u):
                j, k = u // 2, u % 2
                if u == 0:
                    pe.wait_ge(qtb_ready, 2 * b + 2)
                    pe.wait_ge(kb_loaded[s], 128 * (i + 1))
                    pe.wait_ge(kv_loaded[s], 16 * KV_LOADS * (i + 1))
                if not (isinstance(b, int) and b == 0 and u < 2):
                    pe.wait_ge(max_used, 16 * b + u - 1)
                pe.matmul(ps[:, MB + u % 2, :], qtb[:, j // 2, k * P:(k + 1) * P], kzb[:, s, 2 * j:2 * j + 2, :],
                          start=True, stop=True).then_inc(max_ready, 1)

            def scores(b, s, j, k):
                if j == 0 and k == 0:
                    pe.wait_ge(qt_ready, 2 * b + 2)
                if not (isinstance(b, int) and b == 0 and j == 0):
                    pe.wait_ge(pt_ready, 16 * b + 2 * j + k - 1)
                for h in (2 * j, 2 * j + 1):
                    ins = pe.matmul(ps[:, SB + k, (h % 2) * S:(h % 2 + 1) * S],
                                    kz[:, s, h, k * P:(k + 1) * P], qt[:, s, h // 4, :], start=True, stop=True)
                ins.then_inc(sc_ready, 1)

            def values(b, s, j):
                q = j // 2
                if j == 0:
                    pe.wait_ge(v_padded, b + 1)
                pe.wait_ge(pt_ready, 16 * b + 2 * j + 2)
                if j % 4 == 0 and not (isinstance(b, int) and b == 0 and j == 0):
                    pe.wait_ge(ot_used, 2 * b + j // 4)
                for k in range(QT):
                    for h in (2 * j, 2 * j + 1):
                        r = 32 * (h % 4)
                        ins = pe.matmul(ps[r:r + 32, OB, (q % 2) * S:(q % 2 + 1) * S], vaug[:, s, k, h, :],
                                        pt[:, j % 2, k, h % 2, :], start=(k == 0), stop=(k == QT - 1),
                                        tile_position=(0, r))
                ins.then_inc(pv_done, 1)

            def turn_out(b, last):
                pe.wait_ge(ot_used, 2 * b + 2)
                pe.wait_ge(qt_ready, 2 * b + (2 if last else 4))
                for k in range(QT):
                    for q in range(G):
                        ins = pe.transpose(ps[:, TB + k, q * P:(q + 1) * P], ot[:, q, k * P:(k + 1) * P], g.ident[:, :])
                ins.then_inc(outt_done, 1)

            turn1(0, 0, 0)
            turn1(0, 0, 1)
            for u in range(16):
                max_pass(0, 0, 0, u)
            turn2(0, 0)

            def body(b, i, s):
                first, last = isinstance(b, int) and b == 0, isinstance(b, int) and b == B - 1

                def maxima_ahead(j, *places):
                    if 3 <= j < 7 and not last:
                        for n in places:
                            max_pass(b + 1, i + s, 1 - s, 4 * (j - 3) + n)

                for j in range(8):
                    scores(b, s, j, 0)
                    maxima_ahead(j, 0)
                    if j == 7 and not last:
                        turn2(b + 1, 1 - s)
                    scores(b, s, j, 1)
                    maxima_ahead(j, 1)
                    if j == 0:
                        if not first:
                            values(b - 1, 1 - s, 7)
                    else:
                        values(b, s, j - 1)
                    maxima_ahead(j, 2, 3)
                    if j < 2 and not last:
                        turn1(b + 1, 1 - s, j)
                    if j == 1 and not first:
                        turn_out(b - 1, False)

            steps(pe, B, body)
            values(B - 1, (B - 1) % 2, 7)
            turn_out(B - 1, True)


def ffn0(nc, g, a):
    with ExitStack() as ctx:
        def sb(name, shape, dt=F32):
            return ctx.enter_context(nc.sbuf_tensor(name, shape, dt))

        def sem(name):
            return ctx.enter_context(nc.semaphore(name))

        ew = g.ew.rearrange("p (k e d) -> p k e d", k=2, e=E0)
        rw = g.rw.rearrange("p (k e) -> p k e", k=2)
        eb, rb = g.eb, g.rb
        y = sb("y0", [P, D])
        yt = sb("yt0", [P, 2, 2, P])
        lg = sb("lg0", [P, E0])
        top = sb("top0", [P, 8])
        neg = sb("neg0", [P, 1])
        at = sb("at0", [P, 8], U32)
        atf = sb("atf0", [P, 1])
        hot = sb("hot0", [P, E0])
        ex = sb("ex0", [P, E0])
        total = sb("total0", [P, 1])
        inv = sb("inv0", [P, 1])
        gm = sb("gm0", [P, 2, E0])
        gmt = sb("gmt0", [E0, P])
        st = sb("stf", [P, 6])
        mvb = sb("mvf", [P, 2])
        y_ready, yt_turned, yt_ready, lg_ready = sem("f_y"), sem("f_yt_turned"), sem("f_yt"), sem("f_lg")
        neg_ready, ex_ready, gm_ready, gmt_turned = sem("f_neg"), sem("f_ex"), sem("f_gm"), sem("f_gmt_turned")
        gmt_ready, bias_ready, mm_ready, acc_done = sem("f_gmt"), sem("f_bias"), sem("f_mm"), sem("f_acc")
        route_chain, stat_chain = sem("f_route_chain"), sem("f_stat_chain")
        ps = g.ps
        TURN, LOGIT, EXP, GATE, BIAS = 0, 1, 2, 6, 7
        var_eps, rooted, scale_ready = sem("f_var_eps"), sem("f_rooted"), sem("f_scale")
        block = ctx.enter_context(nc.Block())

        @block.vector
        def _(dve):
            route, stat = Chain(dve, route_chain, 6), Chain(dve, stat_chain, 3)
            scale_of_rows(dve, g, var_eps, rooted, scale_ready)

            def normalise(t):
                if not (isinstance(t, int) and t == 0):
                    dve.wait_ge(yt_turned, t)
                dve.tensor_scalar(y[:, :], g.x[:, ds(t, 1), :].rearrange("p o d -> p (o d)"),
                                  g.mv[:, ds(t, 1), 0], g.rstd[:, ds(t, 1)], ALU.subtract, ALU.mult).then_inc(y_ready, 1)

            def pick(t):
                route.step(t)
                dve.wait_ge(lg_ready, t + 1)
                route.link(dve.tensor_copy(lg[:, :], ps[:, LOGIT, 0:E0]))
                apart(dve)
                route.link(dve.max(top[:, :], lg[:, :]))
                if not (isinstance(t, int) and t == 0):
                    dve.wait_ge(ex_ready, t)
                dve.tensor_scalar(neg[:, :], top[:, 0:1], -1.0, None, ALU.mult).then_inc(neg_ready, 1)
                route.link(dve.max_index(at[:, :], top[:, :], lg[:, :]))
                route.link(dve.tensor_copy(atf[:, :], at[:, 0:1]))
                route.link(dve.tensor_scalar(hot[:, :], g.iota8[:, :], atf[:, 0:1], None, ALU.is_equal))

            def weigh(t, s):
                dve.wait_ge(ex_ready, t + 1)
                route.link(dve.reciprocal(inv[:, :], total[:, :]))
                route.end()
                if not (isinstance(t, int) and t < 2):
                    dve.wait_ge(gmt_turned, t - 1)
                dve.tensor_scalar(gm[:, s, :], hot[:, :], inv[:, 0:1], g.tg[:, 1:2], ALU.mult, ALU.mult).then_inc(gm_ready, 1)
                dve.wait_ge(gm_ready, t + 1)

            def add_bias(t):
                dve.wait_ge(bias_ready, t + 1)
                xt = g.x[:, ds(t, 1), :].rearrange("p o d -> p (o d)")
                dve.tensor_tensor(xt, xt, ps[:, BIAS, 0:D], ALU.add).then_inc(acc_done, 1)
                dve.wait_ge(acc_done, 9 * t + 1)

            def add_experts(t, s, q):
                dve.wait_ge(mm_ready, 4 * t + q + 1)
                xt = g.x[:, ds(t, 1), :].rearrange("p o d -> p (o d)")
                for e in range(2):
                    dve.scalar_tensor_tensor(xt, ps[:, EXP + q, e * D:(e + 1) * D], gm[:, s, 2 * q + e:2 * q + e + 1], xt,
                                             ALU.mult, ALU.add).then_inc(acc_done, 1)
                    dve.wait_ge(acc_done, 9 * t + 2 + 2 * q + e)

            def statistics(t):
                stat.step(t)
                apart(dve)
                stat.link(dve.bn_stats(st[:, :], g.x[:, ds(t, 1), :].rearrange("p o d -> p (o d)")))
                apart(dve)
                stat.link(dve.bn_aggr(mvb[:, :], st[:, :]))
                apart(dve)
                stat.link(dve.tensor_copy(g.mv[:, ds(t, 1), :].rearrange("p o d -> p (o d)"), mvb[:, :]))
                stat.end()

            normalise(0)
            pick(0)
            weigh(0, 0)

            def body(t, i, s):
                last = isinstance(t, int) and t == T - 1
                if not last:
                    normalise(t + 1)
                add_bias(t)
                add_experts(t, s, 0)
                add_experts(t, s, 1)
                if not last:
                    pick(t + 1)
                add_experts(t, s, 2)
                if not last:
                    weigh(t + 1, 1 - s)
                add_experts(t, s, 3)
                statistics(t)

            steps(dve, T, body)

        @block.scalar
        def _(act):
            root_of_variance(act, g, var_eps, rooted)

            def keep_yt(t, s):
                act.wait_ge(yt_turned, t + 1)
                if not (isinstance(t, int) and t < 2):
                    act.wait_ge(mm_ready, 4 * (t - 1))
                act.activation(yt[:, s, :, :], ps[:, TURN, 0:2 * P].rearrange("p (k q) -> p k q", k=2), ACT.Copy).then_inc(yt_ready, 1)

            def route(t, s):
                act.wait_ge(neg_ready, t + 1)
                if not (isinstance(t, int) and t < 1):
                    act.wait_ge(gm_ready, t)
                act.activation(ex[:, :], lg[:, :], ACT.Exp, bias=neg[:, 0:1], accum_out=total[:, :]).then_inc(ex_ready, 1)
                act.wait_ge(gmt_turned, t + 1)
                if not (isinstance(t, int) and t < 1):
                    act.wait_ge(bias_ready, t)
                act.activation(gmt[:, :], ps[0:E0, GATE, 0:P], ACT.Copy).then_inc(gmt_ready, 1)

            keep_yt(0, 0)
            route(0, 0)

            def body(t, i, s):
                if not (isinstance(t, int) and t == T - 1):
                    keep_yt(t + 1, 1 - s)
                    route(t + 1, 1 - s)

            steps(act, T, body)

        @block.tensor
        def _(pe):
            def turn(t):
                pe.wait_ge(y_ready, t + 1)
                if not (isinstance(t, int) and t == 0):
                    pe.wait_ge(yt_ready, t)
                for k in range(2):
                    ins = pe.transpose(ps[:, TURN, k * P:(k + 1) * P], y[:, k * P:(k + 1) * P], g.ident[:, :])
                ins.then_inc(yt_turned, 1)

            def logits(t, s):
                pe.wait_ge(yt_ready, t + 1)
                if not (isinstance(t, int) and t == 0):
                    pe.wait_ge(neg_ready, t)
                for k in range(2):
                    pe.matmul(ps[:, LOGIT, 0:E0], yt[:, s, k, :], rw[:, k, :], start=(k == 0), stop=False)
                pe.matmul(ps[:, LOGIT, 0:E0], g.ones_f[:, :], rb[:, :], start=False, stop=True).then_inc(lg_ready, 1)

            def turn_gates(t, s):
                pe.wait_ge(gm_ready, t + 1)
                if not (isinstance(t, int) and t == 0):
                    pe.wait_ge(gmt_ready, t)
                pe.transpose(ps[0:E0, GATE, 0:P], gm[:, s, :], g.ident[:, :]).then_inc(gmt_turned, 1)

            def bias(t):
                pe.wait_ge(gmt_ready, t + 1)
                if not (isinstance(t, int) and t == 0):
                    pe.wait_ge(acc_done, 9 * t - 8)
                pe.matmul(ps[:, BIAS, 0:D], gmt[:, :], eb[:, :], start=True, stop=True).then_inc(bias_ready, 1)

            def experts(t, s, q):
                if not (isinstance(t, int) and t == 0):
                    pe.wait_ge(acc_done, 9 * t - 9 + 3 + 2 * q)
                for k in range(2):
                    ins = pe.matmul(ps[:, EXP + q, :], yt[:, s, k, :], ew[:, k, 2 * q:2 * q + 2, :],
                                    start=(k == 0), stop=(k == 1))
                ins.then_inc(mm_ready, 1)

            turn(0)
            logits(0, 0)
            turn_gates(0, 0)
            bias(0)

            def body(t, i, s):
                last = isinstance(t, int) and t == T - 1
                experts(t, s, 0)
                if not last:
                    turn(t + 1)
                experts(t, s, 1)
                if not last:
                    logits(t + 1, 1 - s)
                experts(t, s, 2)
                experts(t, s, 3)
                if not last:
                    turn_gates(t + 1, 1 - s)
                    bias(t + 1)

            steps(pe, T, body)


def attn1(nc, g, a):
    with ExitStack() as ctx:
        def sb(name, shape, dt=F32):
            return ctx.enter_context(nc.sbuf_tensor(name, shape, dt))

        def sem(name):
            return ctx.enter_context(nc.semaphore(name))

        w_tgt, w_src, w_out = [w.rearrange("p (k n) -> p k n", k=k) for w, k in ((g.w_tgt, 2), (g.w_src, 4), (g.w_out, 4))]
        b_tgt, b_key, b_val, b_out = g.b_tgt, g.b_key, g.b_val, g.b_out
        ctx_t = sb("ctx_t", [P, 2, 4, S])
        maskrow = sb("maskrow1", [P, 2, S])
        pen = sb("pen", [P, 2, 2, S], BF16)
        ones32 = sb("ones32", [P, 32])
        y = sb("y1", [P, QT, D])
        yt = sb("yt1", [P, 2, 2, S])
        qt = sb("qt1", [P, 2, 2, S])
        qtb = sb("qtb1", [P, 2, S], BF16)
        kz = sb("kz1", [P, 2, H1, S])
        kzb = sb("kzb1", [P, H1, S], BF16)
        vb = sb("vb1", [P, QT, D])
        v = sb("v1", [P, 2, QT, D])
        nm = sb("nm1", [P, QT, H1])
        nmt = sb("nmt1", [P, 2, S], BF16)
        pt = sb("pt1", [P, 2, QT, 2, S])
        rec = sb("rec1", [P, S])
        ut = sb("ut1", [P, 2, S])
        st = sb("st1", [P, QT, 6])
        mvb = sb("mvb1", [P, QT, 2])
        padded = sem("b_padded")
        ctx_loaded = [sem(f"b_ctx_loaded{s}") for s in (0, 1)]
        bo_ready = sem("b_bo")
        y_ready, yt_turned, yt_ready = sem("b_y"), sem("b_yt_turned"), sem("b_yt")
        q_done, q_kept, qb_ready, k_done, k_kept, kb_ready = [sem("b_" + n) for n in (
            "q_done", "q_kept", "qb_ready", "k_done", "k_kept", "kb_ready")]
        v_done, v_kept, v_ready, pen_ready, max_ready, max_used = [sem("b_" + n) for n in (
            "v_done", "v_kept", "v_ready", "pen_ready", "max_ready", "max_used")]
        nm_turned, nmt_ready, sc_ready, pt_ready, pv_done, ut_ready = [sem("b_" + n) for n in (
            "nm_turned", "nmt_ready", "sc_ready", "pt_ready", "pv_done", "ut_ready")]
        o_done, x_done, rec_ready, chain = sem("b_o_done"), sem("b_x_done"), sem("b_rec"), sem("b_chain")
        ps = g.ps
        TURN, QO, KV, PV, MB, SB = 0, 1, 2, 3, 4, 6
        SCALE = DH1 ** -0.5
        var_eps, rooted, scale_ready = sem("b_var_eps"), sem("b_rooted"), sem("b_scale")
        block = ctx.enter_context(nc.Block())

        @block.sync
        def _(sp):
            def load(b, i, s):
                if not (isinstance(b, int) and b < 2):
                    sp.wait_ge(v_done, b - 1)
                    apart(sp)
                    sp.wait_ge(k_kept, 8 * (b - 1))
                    apart(sp)
                    sp.wait_ge(pen_ready, b - 1)
                    apart(sp)
                sp.dma_start(ctx_t[:, s, :, :], a["ctx_t"][ds(b, 1), :, :].rearrange("o (k p) q -> p (o k) q", p=P)
                             ).then_inc(ctx_loaded[s], 16)
                sp.dma_start(maskrow[:, s, :], a["maskrow"][:, ds(b * S, S)].partition_broadcast(P)
                             ).then_inc(ctx_loaded[s], 16)

            steps(sp, B, load)
            load_expert(sp, g, a, 0)

        @block.gpsimd
        def _(pool):
            nc.gpsimd.memset(kz[:, :, :, :], 0.0).then_inc(padded, 1)
            nc.gpsimd.memset(nmt[:, :, :], 0.0).then_inc(padded, 1)
            nc.gpsimd.memset(pen[:, :, :, :], 0.0).then_inc(padded, 1)
            nc.gpsimd.memset(ones32[:, :], 1.0).then_inc(padded, 1)

            def narrow(b, i, s):
                pool.wait_ge(q_kept, 2 * b + 2)
                if not (isinstance(b, int) and b < 1):
                    pool.wait_ge(max_ready, 8 * b)
                apart(pool)
                nc.gpsimd.tensor_copy(qtb[:, :, :], qt[:, s, :, :]).then_inc(qb_ready, 1)

            steps(pool, B, narrow)

        @block.vector
        def _(dve):
            ch = Chain(dve, chain, 4)
            scale_of_rows(dve, g, var_eps, rooted, scale_ready)
            dve.tensor_scalar(b_out[:, :], b_out[:, :], g.tg[:, 2:3], None, ALU.mult).then_inc(bo_ready, 1)
            dve.wait_ge(bo_ready, 1)
            dve.wait_ge(padded, 4)

            def normalise(b):
                if not (isinstance(b, int) and b == 0):
                    dve.wait_ge(yt_turned, b)
                for k in range(QT):
                    ins = dve.tensor_scalar(y[:, k, :], g.x[:, ds(2 * b + k, 1), :].rearrange("p o d -> p (o d)"),
                                            g.mv[:, ds(2 * b + k, 1), 0], g.rstd[:, ds(2 * b + k, 1)],
                                            ALU.subtract, ALU.mult)
                ins.then_inc(y_ready, 1)

            def mask_bias(b, i, s):
                dve.wait_ge(ctx_loaded[s], 32 * (i + 1))
                if not (isinstance(b, int) and b < 2):
                    dve.wait_ge(max_ready, 8 * (b - 1))
                dve.tensor_scalar(pen[0:1, s, :, :], maskrow[0:1, s, :].unsqueeze(1).broadcast_to([1, 2, S]), 0.0, MASKED1,
                                  ALU.is_equal, ALU.mult).then_inc(pen_ready, 1)

            def keep_qk(b, s):
                dve.wait_ge(q_done, b + 1)
                if not (isinstance(b, int) and b < 2):
                    dve.wait_ge(sc_ready, 8 * (b - 1))
                for m in range(2):
                    dve.scalar_tensor_tensor(qt[:, s, m, :], ps[:, QO, m * S:(m + 1) * S], b_tgt[:, m:m + 1],
                                             maskrow[:, s, :], ALU.add, ALU.mult).then_inc(q_kept, 1)
                dve.wait_ge(k_done, b + 1)
                for h in range(H1):
                    m, r = h // 4, 32 * (h % 4)
                    dve.scalar_tensor_tensor(kz[r:r + 32, s, h, :], ps[r:r + 32, KV, m * S:(m + 1) * S],
                                             b_key[r:r + 32, m:m + 1], maskrow[r:r + 32, s, :],
                                             ALU.add, ALU.mult).then_inc(k_kept, 1)

            def keep_v(b):
                dve.wait_ge(v_done, b + 1)
                if not (isinstance(b, int) and b < 1):
                    dve.wait_ge(v_ready, 2 * b)
                dve.tensor_tensor(vb[:, :, :], ps[:, KV, :].rearrange("p (k d) -> p k d", k=2),
                                  b_val[:, :].unsqueeze(1).broadcast_to([P, QT, D]), ALU.add).then_inc(v_kept, 1)

            def maxima(b, u):
                j, k = u // 2, u % 2
                dve.wait_ge(max_ready, 8 * b + u + 1)
                if u == 0 and not (isinstance(b, int) and b == 0):
                    dve.wait_ge(nm_turned, b)
                dve.tensor_reduce(nm[:, k, 2 * j:2 * j + 2], ps[:, MB + u % 2, :].rearrange("p (h k) -> p h k", h=2),
                                  AX.X, ALU.max, negate=True).then_inc(max_used, 1)

            def keep_ut(b, q):
                dve.wait_ge(pv_done, 4 * b + 2 * q + 2)
                if q == 0 and not (isinstance(b, int) and b == 0):
                    dve.wait_ge(o_done, b)
                dve.reciprocal(rec[:, :], ps[:, PV, S:2 * S]).then_inc(rec_ready, 1)
                dve.wait_ge(rec_ready, 2 * b + q + 1)
                dve.tensor_tensor(ut[:, q, :], ps[:, PV, 0:S], rec[:, :], ALU.mult).then_inc(ut_ready, 1)

            def finish(b):
                ch.step(b)
                dve.wait_ge(o_done, b + 1)
                xb = g.x[:, ds(2 * b, 2), :]
                dve.scalar_tensor_tensor(xb, ps[:, QO, :].rearrange("p (k d) -> p k d", k=2), g.tg[:, 2:3], xb,
                                         ALU.mult, ALU.add).then_inc(x_done, 1)
                dve.wait_ge(x_done, b + 1)
                ch.link(dve.tensor_tensor(xb, xb, b_out[:, :].unsqueeze(1).broadcast_to([P, QT, D]), ALU.add))
                apart(dve)
                for k in range(QT):
                    ins = dve.bn_stats(st[:, k, :], g.x[:, ds(2 * b + k, 1), :].rearrange("p o d -> p (o d)"))
                ch.link(ins)
                apart(dve)
                for k in range(QT):
                    ins = dve.bn_aggr(mvb[:, k, :], st[:, k, :])
                ch.link(ins)
                apart(dve)
                ch.link(dve.tensor_copy(g.mv[:, ds(2 * b, 2), :], mvb[:, :, :]))
                ch.end()

            normalise(0)
            mask_bias(0, 0, 0)
            keep_qk(0, 0)
            keep_v(0)
            for u in range(8):
                maxima(0, u)

            def body(b, i, s):
                last = isinstance(b, int) and b == B - 1
                if not last:
                    normalise(b + 1)
                    mask_bias(b + 1, i + s, 1 - s)
                    keep_qk(b + 1, 1 - s)
                    keep_ut(b, 0)
                    keep_v(b + 1)
                    for u in range(4):
                        maxima(b + 1, u)
                    keep_ut(b, 1)
                    for u in range(4, 8):
                        maxima(b + 1, u)
                else:
                    keep_ut(b, 0)
                    keep_ut(b, 1)
                finish(b)

            steps(dve, B, body)

        @block.scalar
        def _(act):
            root_of_variance(act, g, var_eps, rooted)

            def keep_yt(b, s):
                act.wait_ge(yt_turned, b + 1)
                if not (isinstance(b, int) and b < 2):
                    act.wait_ge(o_done, b - 1)
                act.activation(yt[:, s, :, :], ps[:, TURN, :].rearrange("p (k q) -> p k q", k=2), ACT.Copy).then_inc(yt_ready, 1)

            def narrow(b, s):
                if not (isinstance(b, int) and b < 1):
                    act.wait_ge(max_ready, 8 * b)
                for m in range(2):
                    act.wait_ge(k_kept, 8 * b + 4 * m + 4)
                    act.activation(kzb[:, 4 * m:4 * m + 4, :], kz[:, s, 4 * m:4 * m + 4, :], ACT.Copy).then_inc(kb_ready, 1)

            def keep_v(b, s):
                act.wait_ge(v_kept, b + 1)
                if not (isinstance(b, int) and b < 2):
                    act.wait_ge(pv_done, 4 * (b - 1))
                apart(act)
                for k in range(QT):
                    act.activation(v[:, s, k, :], vb[:, k, :], ACT.Copy, scale=g.maskcol[:, k, ds(b, 1)]).then_inc(v_ready, 1)

            def keep_nmt(b, s):
                act.wait_ge(nm_turned, b + 1)
                if not (isinstance(b, int) and b < 2):
                    act.wait_ge(sc_ready, 8 * (b - 1))
                act.activation(nmt[0:H1, s, :], ps[0:H1, TURN, 0:S], ACT.Copy).then_inc(nmt_ready, 1)

            def exps(b, j):
                for k in range(QT):
                    u = 2 * j + k
                    act.wait_ge(sc_ready, 8 * b + u + 1)
                    if k == 0 and not (isinstance(b, int) and b == 0 and j < 2):
                        act.wait_ge(pv_done, 4 * b + j - 1)
                    apart(act)
                    act.activation(pt[:, j % 2, k, :, :], ps[:, SB + u % 2, :].rearrange("p (h q) -> p h q", h=2),
                                   ACT.Exp, bias=g.bm1[:, k, ds(b, 1)], scale=SCALE).then_inc(pt_ready, 1)

            act.wait_ge(padded, 4)
            keep_yt(0, 0)
            narrow(0, 0)
            keep_v(0, 0)
            keep_nmt(0, 0)

            def body(b, i, s):
                last = isinstance(b, int) and b == B - 1
                exps(b, 0)
                if not last:
                    keep_yt(b + 1, 1 - s)
                exps(b, 1)
                exps(b, 2)
                if not last:
                    narrow(b + 1, 1 - s)
                exps(b, 3)
                if not last:
                    keep_v(b + 1, 1 - s)
                    keep_nmt(b + 1, 1 - s)

            steps(act, B, body)

        @block.tensor
        def _(pe):
            pe.wait_ge(padded, 4)

            def turn(b):
                pe.wait_ge(y_ready, b + 1)
                if not (isinstance(b, int) and b == 0):
                    pe.wait_ge(nmt_ready, b)
                for d in range(2):
                    for k in range(QT):
                        ins = pe.transpose(ps[:, TURN, d * S + k * P:d * S + (k + 1) * P], y[:, k, d * P:(d + 1) * P],
                                           g.ident[:, :])
                ins.then_inc(yt_turned, 1)

            def project_q(b, s):
                pe.wait_ge(yt_ready, b + 1)
                if not (isinstance(b, int) and b < 2):
                    pe.wait_ge(x_done, b - 1)
                for m in range(2):
                    for d in range(2):
                        ins = pe.matmul(ps[:, QO, m * S:(m + 1) * S], w_tgt[:, d, m * P:(m + 1) * P], yt[:, s, d, :],
                                        start=(d == 0), stop=(d == 1))
                ins.then_inc(q_done, 1)

            def project_k(b, i, s):
                pe.wait_ge(ctx_loaded[s], 32 * (i + 1))
                if not (isinstance(b, int) and b == 0):
                    pe.wait_ge(v_kept, b)
                for m in range(2):
                    for d in range(4):
                        ins = pe.matmul(ps[:, KV, m * S:(m + 1) * S], w_src[:, d, m * P:(m + 1) * P], ctx_t[:, s, d, :],
                                        start=(d == 0), stop=(d == 3))
                ins.then_inc(k_done, 1)

            def project_v(b, s):
                pe.wait_ge(k_kept, 8 * b + 8)
                for k in range(QT):
                    for d in range(4):
                        ins = pe.matmul(ps[:, KV, k * D:(k + 1) * D], ctx_t[:, s, d, k * P:(k + 1) * P], w_src[:, d, D:2 * D],
                                        start=(d == 0), stop=(d == 3))
                ins.then_inc(v_done, 1)

            def max_pass(b, s, u):
                j, k = u // 2, u % 2
                if u == 0:
                    pe.wait_ge(qb_ready, b + 1)
                    pe.wait_ge(pen_ready, b + 1)
                if u % 4 == 0:
                    pe.wait_ge(kb_ready, 2 * b + u // 4 + 1)
                if not (isinstance(b, int) and b == 0 and u < 2):
                    pe.wait_ge(max_used, 8 * b + u - 1)
                pe.matmul(ps[:, MB + u % 2, :], qtb[:, j // 2, k * P:(k + 1) * P], kzb[:, 2 * j:2 * j + 2, :],
                          start=True, stop=False)
                pe.matmul(ps[:, MB + u % 2, :], g.row0_bf[:, :], pen[:, s, :, :], start=False, stop=True).then_inc(max_ready, 1)

            def turn_maxima(b):
                pe.wait_ge(max_used, 8 * b + 8)
                pe.wait_ge(yt_ready, b + 1)
                for k in range(QT):
                    ins = pe.transpose(ps[0:H1, TURN, k * P:(k + 1) * P], nm[:, k, :], g.ident[:, :])
                ins.then_inc(nm_turned, 1)

            def scores(b, s, j):
                if j == 0:
                    pe.wait_ge(nmt_ready, b + 1)
                    pe.wait_ge(k_kept, 8 * b + 8)
                for k in range(QT):
                    u = 2 * j + k
                    if not (isinstance(b, int) and b == 0 and u < 2):
                        pe.wait_ge(pt_ready, 8 * b + u - 1)
                    for h in (2 * j, 2 * j + 1):
                        o = ps[:, SB + u % 2, (h % 2) * S:(h % 2 + 1) * S]
                        pe.matmul(o, kz[:, s, h, k * P:(k + 1) * P], qt[:, s, h // 4, :], start=True, stop=False)
                        ins = pe.matmul(o, g.esel[:, h, :], nmt[:, s, :], start=False, stop=True)
                    ins.then_inc(sc_ready, 1)

            def values(b, s, j):
                if j == 0:
                    pe.wait_ge(v_ready, 2 * b + 2)
                pe.wait_ge(pt_ready, 8 * b + 2 * j + 2)
                if j % 2 == 0 and not (isinstance(b, int) and b == 0 and j == 0):
                    pe.wait_ge(ut_ready, 2 * b + j // 2)
                for lhs, c in ((v, 0), (ones32, S)):
                    for k in range(QT):
                        for h in (2 * j, 2 * j + 1):
                            r = 32 * (h % 4)
                            w = v[:, s, k, h * DH1:(h + 1) * DH1] if lhs is v else ones32[:, :]
                            ins = pe.matmul(ps[r:r + 32, PV, c:c + S], w, pt[:, j % 2, k, h % 2, :],
                                            start=(k == 0), stop=(k == QT - 1), tile_position=(0, r))
                ins.then_inc(pv_done, 1)

            def project_out(b, s, last):
                pe.wait_ge(ut_ready, 2 * b + 2)
                pe.wait_ge(q_kept, 2 * b + (2 if last else 4))
                for k in range(QT):
                    for d in range(4):
                        lhs = (yt[:, s, d, k * P:(k + 1) * P] if d < 2 else ut[:, d - 2, k * P:(k + 1) * P])
                        ins = pe.matmul(ps[:, QO, k * D:(k + 1) * D], lhs, w_out[:, d, :], start=(d == 0), stop=(d == 3))
                ins.then_inc(o_done, 1)

            turn(0)
            project_q(0, 0)
            project_k(0, 0, 0)
            project_v(0, 0)
            for u in range(8):
                max_pass(0, 0, u)
            turn_maxima(0)

            def body(b, i, s):
                last = isinstance(b, int) and b == B - 1
                scores(b, s, 0)
                if not last:
                    turn(b + 1)
                scores(b, s, 1)
                values(b, s, 0)
                if not last:
                    project_q(b + 1, 1 - s)
                    project_k(b + 1, i + s, 1 - s)
                scores(b, s, 2)
                values(b, s, 1)
                if not last:
                    project_v(b + 1, 1 - s)
                scores(b, s, 3)
                values(b, s, 2)
                if not last:
                    for u in range(4):
                        max_pass(b + 1, 1 - s, u)
                values(b, s, 3)
                if not last:
                    for u in range(4, 8):
                        max_pass(b + 1, 1 - s, u)
                project_out(b, s, last)
                if not last:
                    turn_maxima(b + 1)

            steps(pe, B, body)


def route(nc, g, a):
    with ExitStack() as ctx:
        def sb(name, shape, dt=F32):
            return ctx.enter_context(nc.sbuf_tensor(name, shape, dt))

        def sem(name):
            return ctx.enter_context(nc.semaphore(name))

        W1 = 2 * 2 * FF
        wg = g.wg.rearrange("p (k e) -> p k e", k=2)
        sw1 = g.sw[:, 0:W1].rearrange("p (k f) -> p k f", k=2)
        sw2 = g.sw[:, W1:WCOLS].rearrange("p (k d) -> p k d", k=KF)
        y = sb("y2", [P, 2, QT, D])
        yt = sb("yt2", [P, 2, 2, S])
        lg = sb("lg2", [P, QT, E1])
        top = sb("top2", [P, QT, 8])
        neg = sb("neg2", [P, QT])
        rest = sb("rest2", [P, QT, E1])
        mask = sb("mask2", [P, QT, E1])
        maskb = sb("maskb2", [P, QT, E1], BF16)
        seen = sb("seen2", [P, 2, E1], BF16)
        ex = sb("ex2", [P, QT, E1])
        total = sb("total2", [P, QT])
        picked = sb("picked2", [P, QT])
        coef = sb("coef2", [P, 3, QT])
        wrow = sb("wrow2", [P, 2, QT, E1])
        rank = sb("rank2", [P, QT, E1])
        ranki = sb("ranki2", [P, QT, E1], I32)
        hi = sb("hi2", [P, QT, E1], I32)
        lo = sb("lo2", [P, QT, E1], I32)
        hif = sb("hif2", [P, QT, E1], BF16)
        lof = sb("lof2", [P, QT, E1], BF16)
        hot_a = sb("hot_a", [P, QT, E1, RA], BF16)
        aa = sb("aa", [P, QT, E1, 32], BF16)
        bb = sb("bb", [P, QT, E1, RB], BF16)
        zero = sb("zero2", [P, 512], BF16)
        zrow = sb("zrow2", [32, CAP // 32 * ROW])
        sil = sb("sil2", [P, 2, S])
        gt = sb("gt2", [P, KF, S])
        base = sb("base2", [P, 2, QT, D])
        tt = sb("tt2", [P, E1 // 4, RB])
        pair = sb("pair2", [E1, 2, CAP])
        tok = sb("tok2", [E1, 3, CAP])
        names = ("r_zeroed", "r_y", "r_yt_turned", "r_yt", "r_lg",
                 "r_neg", "r_ex", "r_chain", "r_maskb", "r_rank", "r_wrow", "r_hot", "r_hot_used", "r_up", "r_sil",
                 "r_gt", "r_out", "r_base", "r_tt", "r_tt_out", "r_pair", "r_tok", "r_tok_turned", "r_fill")
        (zeroed, y_ready, yt_turned, yt_ready, lg_ready, neg_ready, ex_ready,
         chain, maskb_ready, rank_ready, wrow_ready, hot_ready, hot_used, up_ready, sil_ready, gt_ready, out_ready,
         base_ready, tt_ready, tt_out, pair_in, tok_ready, tok_turned, filled) = [sem(n) for n in names]
        table_out = [sem(f"table_out{s}") for s in (0, 1)]
        base_out = [sem(f"base_out{s}") for s in (0, 1)]
        tchain = sem("r_tchain")
        ps = g.ps
        TURN, LOGIT, RANK, UP, OUT, LIST = 0, 1, 2, 3, 5, 6
        var_eps, rooted, scale_ready = sem("r_var_eps"), sem("r_rooted"), sem("r_scale")
        block = ctx.enter_context(nc.Block())

        @block.sync
        def _(sp):
            sp.wait_ge(zeroed, 4)
            sp.dma_start(g.table[NT:NT + CAP, :].rearrange("(p r) d -> p (r d)", p=32), zrow[:, :]).then_inc(filled, 16)
            sp.dma_start(a["out"][NT:NT + CAP, :].rearrange("(p r) d -> p (r d)", p=32), zrow[:, 0:CAP // 32 * D]
                         ).then_inc(filled, 16)

            def store_table(b, s):
                sp.wait_ge(wrow_ready, b + 1)
                apart(sp)
                rows = g.table[ds(b * S, S), :].rearrange("(k p) d -> p k d", p=P)
                sp.dma_start(rows[:, :, 0:D], y[:, s, :, :]).then_inc(table_out[s], 16)
                sp.dma_start(rows[:, :, D:ROW], wrow[:, s, :, :]).then_inc(table_out[s], 16)

            def store(b, i, s):
                if not (isinstance(b, int) and b == B - 1):
                    store_table(b + 1, 1 - s)
                sp.wait_ge(base_ready, b + 1)
                apart(sp)
                sp.dma_start(a["out"][ds(b * S, S), :].rearrange("(k p) d -> p k d", p=P), base[:, s, :, :]
                             ).then_inc(base_out[s], 16)

            store_table(0, 0)
            load_expert(sp, g, a, 1)
            steps(sp, B, store)
            sp.wait_ge(tt_ready, 4)
            for i in range(4):
                for m in range(2):
                    r = 32 * i + m * RA
                    sp.dma_start(g.lists[i:E1:4, m, :].rearrange("g (a b) -> a g b", b=RB), tt[r:r + RA, :, :]
                                 ).then_inc(tt_out, 16)
            sp.wait_ge(tt_out, 128)
            sp.dma_start(pair[:, :, :], g.lists[:, :, :]).then_inc(pair_in, 16)
            for s in (0, 1):
                sp.wait_ge(base_out[s], 16 * (B // 2))
                sp.wait_ge(table_out[s], 32 * (B // 2))
            sp.wait_ge(filled, 32)
            sp.wait_ge(pair_in, 16)

        @block.gpsimd
        def _(pool):
            nc.gpsimd.memset(aa[:, :, :, :], 0.0).then_inc(zeroed, 1)
            nc.gpsimd.memset(zero[:, :], 0.0).then_inc(zeroed, 1)
            nc.gpsimd.memset(zrow[:, :], 0.0).then_inc(zeroed, 1)
            nc.gpsimd.memset(seen[:, :, :], 0.0).then_inc(zeroed, 1)

        @block.vector
        def _(dve):
            ch = Chain(dve, chain, 18)
            scale_of_rows(dve, g, var_eps, rooted, scale_ready)
            dve.wait_ge(zeroed, 4)

            def normalise(b, i, s):
                if not (isinstance(b, int) and b < 2):
                    dve.wait_ge(yt_turned, b - 1)
                    dve.wait_ge(table_out[s], 32 * i)
                    apart(dve)
                for k in range(QT):
                    ins = dve.tensor_scalar(y[:, s, k, :], g.x[:, ds(2 * b + k, 1), :].rearrange("p o d -> p (o d)"),
                                            g.mv[:, ds(2 * b + k, 1), 0], g.rstd[:, ds(2 * b + k, 1)],
                                            ALU.subtract, ALU.mult)
                ins.then_inc(y_ready, 1)

            def pick(b):
                ch.step(b)
                dve.wait_ge(lg_ready, b + 1)
                ch.link(dve.tensor_copy(lg[:, :, :], ps[:, LOGIT, 0:QT * E1].rearrange("p (k e) -> p k e", k=QT)))
                apart(dve)
                for k in range(QT):
                    ins = dve.max(top[:, k, :], lg[:, k, :])
                ch.link(ins)
                dve.tensor_scalar(neg[:, :], top[:, :, 0], -1.0, None, ALU.mult).then_inc(neg_ready, 1)
                apart(dve)
                for k in range(QT):
                    ins = dve.match_replace(rest[:, k, :], top[:, k, :], lg[:, k, :], NEG)
                ch.link(ins)
                if not (isinstance(b, int) and b == 0):
                    dve.wait_ge(rank_ready, b)
                ch.link(dve.tensor_tensor(mask[:, :, :], rest[:, :, :], lg[:, :, :], ALU.not_equal))
                dve.tensor_copy(maskb[:, :, :], mask[:, :, :]).then_inc(maskb_ready, 1)

            def weigh(b, i, s):
                dve.wait_ge(ex_ready, 2 * b + 2)
                ch.link(dve.tensor_tensor(ex[:, :, :], ex[:, :, :], mask[:, :, :], ALU.mult))
                dve.tensor_reduce(picked[:, :], ex[:, :, :], AX.X, ALU.add)
                ch.link(dve.reciprocal(coef[:, 0, :], total[:, :]))
                ch.link(dve.tensor_tensor(coef[:, 1, :], picked[:, :], coef[:, 0, :], ALU.mult))
                ch.link(dve.tensor_scalar(coef[:, 1, :], coef[:, 1, :], 1.1920929e-07, None, ALU.max))
                ch.link(dve.reciprocal(coef[:, 2, :], coef[:, 1, :]))
                ch.link(dve.tensor_tensor(coef[:, 2, :], coef[:, 2, :], coef[:, 0, :], ALU.mult))
                ch.link(dve.tensor_scalar(coef[:, 2, :], coef[:, 2, :], g.tg[:, 3:4], None, ALU.mult))
                if not (isinstance(b, int) and b < 2):
                    dve.wait_ge(table_out[s], 32 * i)
                dve.tensor_tensor(wrow[:, s, :, :], ex[:, :, :], coef[:, 2, :].unsqueeze(2).broadcast_to([P, QT, E1]),
                                  ALU.mult).then_inc(wrow_ready, 1)

            def slots(b, s):
                dve.wait_ge(rank_ready, b + 1)
                ch.link(dve.scalar_tensor_tensor(rank[:, :, :], mask[:, :, :], -4096.0,
                                                 ps[:, RANK, 0:QT * E1].rearrange("p (k e) -> p k e", k=QT),
                                                 ALU.mult, ALU.add))
                ch.link(dve.tensor_scalar(ranki[:, :, :], rank[:, :, :], 4096.0, None, ALU.add))
                dve.tensor_scalar(hi[:, :, :], ranki[:, :, :], 4, None, ALU.logical_shift_right)
                ch.link(dve.tensor_scalar(lo[:, :, :], ranki[:, :, :], 15, None, ALU.bitwise_and))
                dve.tensor_copy(hif[:, :, :], hi[:, :, :])
                ch.link(dve.tensor_copy(lof[:, :, :], lo[:, :, :]))
                ch.link(dve.tensor_tensor(seen[:, 1 - s, :], seen[:, s, :], maskb[:, 0, :], ALU.add))
                ch.link(dve.tensor_tensor(seen[:, 1 - s, :], seen[:, 1 - s, :], maskb[:, 1, :], ALU.add))
                if not (isinstance(b, int) and b == 0):
                    dve.wait_ge(hot_used, b)
                iota = g.iota_b[:, :].unsqueeze(1).broadcast_to([P, E1, RB])
                for k in range(QT):
                    dve.tensor_tensor(hot_a[:, k, :, :], hif[:, k, :].unsqueeze(2).broadcast_to([P, E1, RA]),
                                      iota[:, :, 0:RA], ALU.is_equal)
                    ins = dve.tensor_tensor(bb[:, k, :, :], lof[:, k, :].unsqueeze(2).broadcast_to([P, E1, RB]), iota,
                                            ALU.is_equal)
                ch.link(ins)
                for k in range(QT):
                    dve.tensor_scalar(aa[:, k, :, 0:RA], hot_a[:, k, :, :], g.iota_p[:, 0:1], None, ALU.mult)
                    ins = dve.tensor_scalar(aa[:, k, :, RA:2 * RA], hot_a[:, k, :, :], g.iota_t[:, ds(2 * b + k, 1)], None,
                                            ALU.mult)
                ins.then_inc(hot_ready, 1)

            def hidden(b, f):
                dve.wait_ge(sil_ready, KF * b + f + 1)
                if f == 0 and not (isinstance(b, int) and b == 0):
                    dve.wait_ge(out_ready, b)
                dve.tensor_tensor(gt[:, f, :], ps[:, UP + f % 2, S:2 * S], sil[:, f % 2, :], ALU.mult).then_inc(gt_ready, 1)

            def residual(b, i, s):
                dve.wait_ge(out_ready, b + 1)
                if not (isinstance(b, int) and b < 2):
                    dve.wait_ge(base_out[s], 16 * i)
                dve.scalar_tensor_tensor(base[:, s, :, :], ps[:, OUT, :].rearrange("p (k d) -> p k d", k=QT),
                                         g.tg[:, 3:4], g.x[:, ds(2 * b, 2), :], ALU.mult, ALU.add).then_inc(base_ready, 1)

            def front(b, i, s):
                pick(b)
                weigh(b, i, s)
                slots(b, s)
                ch.end()

            normalise(0, 0, 0)
            front(0, 0, 0)

            def body(b, i, s):
                last = isinstance(b, int) and b == B - 1
                if not last:
                    normalise(b + 1, i + s, 1 - s)
                hidden(b, 0)
                hidden(b, 1)
                if not last:
                    pick(b + 1)
                hidden(b, 2)
                hidden(b, 3)
                if not last:
                    weigh(b + 1, i + s, 1 - s)
                hidden(b, 4)
                hidden(b, 5)
                if not last:
                    slots(b + 1, 1 - s)
                    ch.end()
                residual(b, i, s)

            steps(dve, B, body)
            dve.wait_ge(hot_used, B)
            for i in range(4):
                dve.tensor_copy(tt[32 * i:32 * i + 32, :, :],
                                ps[32 * i:32 * i + 32, LIST:LIST + 2, :].rearrange("p n (g c) -> p (n g) c", c=4 * RB)[
                                    :, :, i * RB:(i + 1) * RB]).then_inc(tt_ready, 1)
            ct = Chain(dve, tchain, 4)
            dve.wait_ge(pair_in, 16)
            ct.link(dve.tensor_scalar(tok[:, 0, :], pair[:, 1, :], 0.0, float(P), ALU.is_equal, ALU.mult))
            dve.tensor_scalar(tok[:, 1, :], pair[:, 1, :], 0.0, None, ALU.is_equal)
            ct.link(dve.scalar_tensor_tensor(tok[:, 2, :], pair[:, 1, :], float(P), pair[:, 0, :], ALU.mult, ALU.add))
            dve.scalar_tensor_tensor(tok[:, 2, :], tok[:, 2, :], -float(P), tok[:, 0, :], ALU.add, ALU.add)
            ct.link(dve.tensor_tensor(tok[:, 1, :], tok[:, 1, :], g.iota_slot[0:E1, :], ALU.mult))
            ct.link(dve.tensor_tensor(tok[:, 2, :], tok[:, 2, :], tok[:, 1, :], ALU.add))
            ct.end()
            dve.tensor_copy(tok[:, 1, :], tok[:, 2, :]).then_inc(tok_ready, 1)
            dve.wait_ge(tok_turned, 1)
            dve.tensor_copy(g.list_a[:, :], ps[:, TURN, 0:E1])
            dve.tensor_copy(g.list_b[:, :], ps[0:CAPX, TURN, E1:2 * E1])

        @block.scalar
        def _(act):
            root_of_variance(act, g, var_eps, rooted)

            def keep_yt(b, s):
                act.wait_ge(yt_turned, b + 1)
                if not (isinstance(b, int) and b < 2):
                    act.wait_ge(up_ready, KF * (b - 1))
                act.activation(yt[:, s, :, :], ps[:, TURN, :].rearrange("p (k q) -> p k q", k=2), ACT.Copy).then_inc(yt_ready, 1)

            def exps(b):
                act.wait_ge(neg_ready, b + 1)
                if not (isinstance(b, int) and b < 1):
                    act.wait_ge(wrow_ready, b)
                for k in range(QT):
                    act.activation(ex[:, k, :], lg[:, k, :], ACT.Exp, bias=neg[:, k:k + 1], accum_out=total[:, k:k + 1]
                                   ).then_inc(ex_ready, 1)

            def silu(b, f):
                act.wait_ge(up_ready, KF * b + f + 1)
                if not (isinstance(b, int) and b == 0 and f < 2):
                    act.wait_ge(gt_ready, KF * b + f - 1)
                act.activation(sil[:, f % 2, :], ps[:, UP + f % 2, 0:S], ACT.Silu).then_inc(sil_ready, 1)

            keep_yt(0, 0)
            exps(0)

            def body(b, i, s):
                last = isinstance(b, int) and b == B - 1
                silu(b, 0)
                if not last:
                    keep_yt(b + 1, 1 - s)
                silu(b, 1)
                silu(b, 2)
                if not last:
                    exps(b + 1)
                for f in (3, 4, 5):
                    silu(b, f)

            steps(act, B, body)

        @block.tensor
        def _(pe):
            pe.wait_ge(zeroed, 4)
            for n in range(2):
                pe.matmul(ps[:, LIST + n, :], g.ones_bf[:, :], zero[:, :], start=True, stop=False, skip_group_check=True)

            def turn(b, s):
                pe.wait_ge(y_ready, b + 1)
                if not (isinstance(b, int) and b == 0):
                    pe.wait_ge(yt_ready, b)
                for d in range(2):
                    for k in range(QT):
                        ins = pe.transpose(ps[:, TURN, d * S + k * P:d * S + (k + 1) * P], y[:, s, k, d * P:(d + 1) * P],
                                           g.ident[:, :])
                ins.then_inc(yt_turned, 1)

            def logits(b, s):
                pe.wait_ge(yt_ready, b + 1)
                if not (isinstance(b, int) and b == 0):
                    pe.wait_ge(neg_ready, b)
                for k in range(QT):
                    for d in range(2):
                        ins = pe.matmul(ps[:, LOGIT, k * E1:(k + 1) * E1], yt[:, s, d, k * P:(k + 1) * P], wg[:, d, :],
                                        start=(d == 0), stop=(d == 1))
                ins.then_inc(lg_ready, 1)

            def ranks(b, s):
                pe.wait_ge(maskb_ready, b + 1)
                if not (isinstance(b, int) and b == 0):
                    pe.wait_ge(hot_ready, b)
                for k in range(QT):
                    o = ps[:, RANK, k * E1:(k + 1) * E1]
                    pe.matmul(o, g.ones_bf[:, :], seen[:, s, :], start=True, stop=False)
                    if k == 1:
                        pe.matmul(o, g.ones_bf[:, :], maskb[:, 0, :], start=False, stop=False)
                    ins = pe.matmul(o, g.tri[:, :], maskb[:, k, :], start=False, stop=True)
                ins.then_inc(rank_ready, 1)

            def lists(b):
                pe.wait_ge(hot_ready, b + 1)
                for k in range(QT):
                    for q in range(E1 // 4):
                        ins = pe.matmul(ps[:, LIST + q // 8, (q % 8) * 4 * RB:(q % 8 + 1) * 4 * RB],
                                        aa[:, k, 4 * q:4 * q + 4, :], bb[:, k, 4 * q:4 * q + 4, :],
                                        start=False, stop=True, skip_group_check=True)
                ins.then_inc(hot_used, 1)

            def up(b, s, f):
                if not (isinstance(b, int) and b == 0 and f < 2):
                    pe.wait_ge(gt_ready, KF * b + f - 1)
                for c, m in ((0, KF + f), (S, f)):
                    for d in range(2):
                        ins = pe.matmul(ps[:, UP + f % 2, c:c + S], sw1[:, d, m * P:(m + 1) * P], yt[:, s, d, :],
                                        start=(d == 0), stop=(d == 1))
                ins.then_inc(up_ready, 1)

            def down(b):
                pe.wait_ge(gt_ready, KF * b + KF)
                if not (isinstance(b, int) and b == 0):
                    pe.wait_ge(base_ready, b)
                for k in range(QT):
                    for f in range(KF):
                        ins = pe.matmul(ps[:, OUT, k * D:(k + 1) * D], gt[:, f, k * P:(k + 1) * P], sw2[:, f, :],
                                        start=(f == 0), stop=(f == KF - 1))
                ins.then_inc(out_ready, 1)

            turn(0, 0)
            logits(0, 0)
            ranks(0, 0)

            def body(b, i, s):
                last = isinstance(b, int) and b == B - 1
                up(b, s, 0)
                if not last:
                    turn(b + 1, 1 - s)
                up(b, s, 1)
                if not last:
                    logits(b + 1, 1 - s)
                up(b, s, 2)
                lists(b)
                up(b, s, 3)
                if not last:
                    ranks(b + 1, 1 - s)
                up(b, s, 4)
                up(b, s, 5)
                down(b)

            steps(pe, B, body)
            pe.wait_ge(tok_ready, 1)
            pe.wait_ge(yt_ready, B)
            pe.transpose(ps[:, TURN, 0:E1], tok[:, 1, 0:P], g.ident[0:E1, 0:E1])
            pe.transpose(ps[0:CAPX, TURN, E1:2 * E1], tok[:, 1, P:CAP], g.ident[0:E1, 0:E1]).then_inc(tok_turned, 1)


def experts(nc, g, a):
    with ExitStack() as ctx:
        def sb(name, shape, dt=F32):
            return ctx.enter_context(nc.sbuf_tensor(name, shape, dt))

        def sem(name):
            return ctx.enter_context(nc.semaphore(name))

        W1 = 2 * 2 * FF
        HF = KF // 2
        w1 = [g.wring[:, s, 0:W1].rearrange("p (k f) -> p k f", k=2) for s in range(RING)]
        w2 = [g.wring[:, s, W1:WCOLS].rearrange("p (k d) -> p k d", k=KF) for s in range(RING)]
        rows_a = sb("rows_a", [P, RING], U32)
        rows_b = sb("rows_b", [CAPX, RING], U32)
        to_a = sb("to_a", [P, 2], U32)
        to_b = sb("to_b", [CAPX, 2], U32)
        xa = sb("xa", [P, RING, ROW])
        xb = sb("xb", [CAPX, RING, ROW])
        wa = sb("wa", [P, RING])
        wb = sb("wb", [CAPX, RING])
        xt = sb("xt", [P, 2, 2, CAP])
        sil = sb("sil3", [P, 2, HF, CAP])
        gt = sb("gt3", [P, 2, KF, CAP])
        zt = sb("zt", [P, 2, 2, CAP])
        za = sb("za", [P, 2, D])
        zb = sb("zb", [CAPX, 2, D])
        names = ("x_rows", "x_turned", "x_ready", "x_weights", "x_up", "x_sil", "x_gt", "x_down", "x_zt", "x_zturned",
                 "x_z", "x_added")
        (rows_ready, turned, xt_ready, weights_kept, up_ready, sil_ready, gt_ready, down_ready, zt_ready, z_turned,
         z_ready, added) = [sem(n) for n in names]
        gathered = [sem(f"gathered{s}") for s in range(RING)]
        to_ready = sem("x_to")
        AHEAD = 3
        ps = g.ps
        UP, DOWN, BACK, TURN = 0, 4, 5, 6
        block = ctx.enter_context(nc.Block())

        @block.sync
        def _(sp):
            def load(e, i, s):
                if isinstance(e, int) and e < RING:
                    if e == 2:
                        load_expert(sp, g, a, e)
                    return
                sp.wait_ge(down_ready, e - RING + 1)
                apart(sp)
                for c in range(PARTS):
                    if 1 <= c <= 2:
                        sp.wait_ge(up_ready, 2 * (e - RING + 2) + c)
                        apart(sp)
                    n = slice(c * WCOLS // PARTS, (c + 1) * WCOLS // PARTS)
                    sp.dma_start(g.wring[:, s, n], a["experts"][ds(e, 1), :, n].rearrange("o p n -> p (o n)")
                                 ).then_inc(g.w_loaded[s], 16)

            steps(sp, E1, load, RING)

        @block.gpsimd
        def _(pool):
            def gather(e, i, s):
                if not (isinstance(e, int) and e < RING):
                    pool.wait_ge(turned, e - RING + 1)
                    apart(pool)
                    pool.wait_ge(weights_kept, e - RING + 1)
                    apart(pool)
                nc.gpsimd.tensor_copy(rows_a[:, s:s + 1], g.list_a[:, ds(e, 1)]).then_inc(rows_ready, 1)
                nc.gpsimd.tensor_copy(rows_b[:, s:s + 1], g.list_b[:, ds(e, 1)]).then_inc(rows_ready, 1)
                pool.wait_ge(rows_ready, 2 * e + 2)
                apart(pool)
                pool.indirect_dma_start(xa[:, s, :], None, g.table,
                                        bass.IndirectOffsetOnAxis(ap=rows_a[:, s:s + 1], axis=0)).then_inc(gathered[s], 16)
                pool.indirect_dma_start(xb[:, s, :], None, g.table,
                                        bass.IndirectOffsetOnAxis(ap=rows_b[:, s:s + 1], axis=0)).then_inc(gathered[s], 16)

            def add(e, s):
                if not (isinstance(e, int) and e < 2):
                    pool.wait_ge(added, 32 * (e - 1))
                    apart(pool)
                nc.gpsimd.tensor_copy(to_a[:, s % 2:s % 2 + 1], g.list_a[:, ds(e, 1)]).then_inc(to_ready, 1)
                nc.gpsimd.tensor_copy(to_b[:, s % 2:s % 2 + 1], g.list_b[:, ds(e, 1)]).then_inc(to_ready, 1)
                pool.wait_ge(to_ready, 2 * e + 2)
                apart(pool)
                pool.wait_ge(z_ready, e + 1)
                apart(pool)
                if not (isinstance(e, int) and e == 0):
                    pool.wait_ge(added, 32 * e)
                    apart(pool)
                pool.indirect_dma_start(a["out"], bass.IndirectOffsetOnAxis(ap=to_a[:, s % 2:s % 2 + 1], axis=0),
                                        za[:, s % 2, :], None, compute_op=ALU.add).then_inc(added, 16)
                pool.indirect_dma_start(a["out"], bass.IndirectOffsetOnAxis(ap=to_b[:, s % 2:s % 2 + 1], axis=0),
                                        zb[:, s % 2, :], None, compute_op=ALU.add).then_inc(added, 16)

            for e in range(AHEAD):
                gather(e, 0, e)

            def body(e, i, s):
                if not (isinstance(e, int) and e >= E1 - AHEAD):
                    gather(e + AHEAD, i + (s + AHEAD) // RING, (s + AHEAD) % RING)
                if not (isinstance(e, int) and e < 2):
                    add(e - 2, (s - 2) % RING)

            steps(pool, E1, body, RING)
            add(E1 - 2, (E1 - 2) % RING)
            add(E1 - 1, (E1 - 1) % RING)
            pool.wait_ge(added, 32 * E1)

        @block.vector
        def _(dve):
            def keep_weights(e, i, s):
                dve.wait_ge(gathered[s], 32 * (i + 1))
                if not (isinstance(e, int) and e < RING):
                    dve.wait_ge(z_ready, e - RING + 1)
                apart(dve)
                dve.tensor_copy(wa[:, s:s + 1], xa[:, s, ds(e + D, 1)])
                dve.tensor_copy(wb[:, s:s + 1], xb[:, s, ds(e + D, 1)]).then_inc(weights_kept, 1)

            def hidden(e, s, h):
                dve.wait_ge(sil_ready, 2 * e + h + 1)
                if h == 0 and not (isinstance(e, int) and e < 2):
                    dve.wait_ge(down_ready, e - 1)
                dve.tensor_tensor(gt[:, s % 2, h * HF:(h + 1) * HF, :],
                                  ps[:, UP + 2 * h + 1, 0:HF * CAP].rearrange("p (f c) -> p f c", c=CAP),
                                  sil[:, h, :, :], ALU.mult).then_inc(gt_ready, 1)

            def scale(e, s):
                dve.wait_ge(z_turned, e + 1)
                dve.wait_ge(weights_kept, e + 1)
                if not (isinstance(e, int) and e < 2):
                    dve.wait_ge(added, 32 * (e - 1))
                dve.tensor_scalar(za[:, s % 2, :], ps[:, BACK, 0:D], wa[:, s:s + 1], None, ALU.mult)
                dve.tensor_scalar(zb[:, s % 2, :], ps[0:CAPX, BACK, D:2 * D], wb[:, s:s + 1], None, ALU.mult).then_inc(z_ready, 1)

            def body(e, i, s):
                keep_weights(e, i, s)
                hidden(e, s, 0)
                if not (isinstance(e, int) and e < 2):
                    scale(e - 2, (s - 2) % RING)
                hidden(e, s, 1)

            steps(dve, E1, body, RING)
            scale(E1 - 2, (E1 - 2) % RING)
            scale(E1 - 1, (E1 - 1) % RING)

        @block.scalar
        def _(act):
            def keep_xt(e, s):
                act.wait_ge(turned, e + 1)
                if not (isinstance(e, int) and e < 2):
                    act.wait_ge(up_ready, 2 * (e - 1))
                act.activation(xt[:, s % 2, :, :], ps[:, TURN, 0:2 * CAP].rearrange("p (k c) -> p k c", k=2), ACT.Copy
                               ).then_inc(xt_ready, 1)

            def silu(e, h):
                act.wait_ge(up_ready, 2 * e + h + 1)
                if not (isinstance(e, int) and e == 0):
                    act.wait_ge(gt_ready, 2 * e + h - 1)
                act.activation(sil[:, h, :, :], ps[:, UP + 2 * h, 0:HF * CAP].rearrange("p (f c) -> p f c", c=CAP), ACT.Silu
                               ).then_inc(sil_ready, 1)

            def keep_zt(e, s):
                act.wait_ge(down_ready, e + 1)
                if not (isinstance(e, int) and e < 2):
                    act.wait_ge(z_turned, e - 1)
                act.activation(zt[:, s % 2, :, :], ps[:, DOWN, 0:2 * CAP].rearrange("p (k c) -> p k c", k=2), ACT.Copy
                               ).then_inc(zt_ready, 1)

            keep_xt(0, 0)

            def body(e, i, s):
                silu(e, 0)
                if not (isinstance(e, int) and e == E1 - 1):
                    keep_xt(e + 1, (s + 1) % RING)
                silu(e, 1)
                if not (isinstance(e, int) and e == 0):
                    keep_zt(e - 1, (s - 1) % RING)

            steps(act, E1, body, RING)
            keep_zt(E1 - 1, (E1 - 1) % RING)

        @block.tensor
        def _(pe):
            def turn(e, i, s):
                pe.wait_ge(gathered[s], 32 * (i + 1))
                if not (isinstance(e, int) and e == 0):
                    pe.wait_ge(xt_ready, e)
                for k in range(2):
                    pe.transpose(ps[:, TURN, k * CAP:k * CAP + P], xa[:, s, k * P:(k + 1) * P], g.ident[:, :])
                    ins = pe.transpose(ps[:, TURN, k * CAP + P:(k + 1) * CAP], xb[:, s, k * P:(k + 1) * P],
                                       g.ident[0:CAPX, 0:CAPX])
                ins.then_inc(turned, 1)

            def up(e, i, s, h):
                if h == 0:
                    pe.wait_ge(xt_ready, e + 1)
                    pe.wait_ge(g.w_loaded[s], 16 * PARTS * (i + 1))
                if not (isinstance(e, int) and e == 0):
                    pe.wait_ge(gt_ready, 2 * e + h - 1)
                for n, m in ((0, KF), (1, 0)):
                    for f in range(HF):
                        c = (m + h * HF + f) * P
                        for d in range(2):
                            ins = pe.matmul(ps[:, UP + 2 * h + n, f * CAP:(f + 1) * CAP], w1[s][:, d, c:c + P],
                                            xt[:, s % 2, d, :], start=(d == 0), stop=(d == 1))
                ins.then_inc(up_ready, 1)

            def down(e, s):
                pe.wait_ge(gt_ready, 2 * e + 2)
                if not (isinstance(e, int) and e == 0):
                    pe.wait_ge(zt_ready, e)
                for d in range(2):
                    for f in range(KF):
                        ins = pe.matmul(ps[:, DOWN, d * CAP:(d + 1) * CAP], w2[s][:, f, d * P:(d + 1) * P],
                                        gt[:, s % 2, f, :], start=(f == 0), stop=(f == KF - 1))
                ins.then_inc(down_ready, 1)

            def turn_back(e, s):
                pe.wait_ge(zt_ready, e + 1)
                if not (isinstance(e, int) and e == 0):
                    pe.wait_ge(z_ready, e)
                for d in range(2):
                    pe.transpose(ps[:, BACK, d * P:(d + 1) * P], zt[:, s % 2, d, 0:P], g.ident[:, :])
                    ins = pe.transpose(ps[0:CAPX, BACK, D + d * P:D + (d + 1) * P], zt[:, s % 2, d, P:CAP], g.ident[:, :])
                ins.then_inc(z_turned, 1)

            turn(0, 0, 0)

            def body(e, i, s):
                up(e, i, s, 0)
                if not (isinstance(e, int) and e < 2):
                    turn_back(e - 2, (s - 2) % RING)
                if not (isinstance(e, int) and e == E1 - 1):
                    turn(e + 1, i + (s + 1) // RING, (s + 1) % RING)
                up(e, i, s, 1)
                if not (isinstance(e, int) and e == 0):
                    down(e - 1, (s - 1) % RING)

            steps(pe, E1, body, RING)
            turn_back(E1 - 2, (E1 - 2) % RING)
            down(E1 - 1, (E1 - 1) % RING)
            turn_back(E1 - 1, (E1 - 1) % RING)


def program(nc, a):
    with ExitStack() as ctx:
        def sb(name, shape, dt=F32):
            return ctx.enter_context(nc.sbuf_tensor(name, shape, dt))

        g = Shared()
        g.ps = ctx.enter_context(nc.psum_tensor("ps", [P, 8, 512], F32))
        g.x = sb("x_state", [P, T, D])
        g.mv = sb("mv", [P, T, 2])
        g.rstd = sb("rstd", [P, T])
        g.ident = sb("ident", [P, P])
        g.tri = sb("tri", [P, P], BF16)
        g.ones_bf = sb("ones_bf", [P, P], BF16)
        g.row0_bf = sb("row0_bf", [P, P], BF16)
        g.ones_f = sb("ones_f", [1, P])
        g.esel = sb("esel", [P, H1, P], BF16)
        g.iota8 = sb("iota8", [P, E0])
        g.iota_b = sb("iota_b", [P, RB])
        g.iota_p = sb("iota_p", [P, 1])
        g.iota_t = sb("iota_t", [P, T])
        g.iota_slot = sb("iota_slot", [P, CAP])
        g.maskcol = sb("maskcol", [P, QT, B])
        g.bm0 = sb("bm0", [P, QT, B])
        g.bm1 = sb("bm1", [P, QT, B])
        g.tg = sb("tg", [P, 4])
        g.wring = sb("wring", [P, RING, WCOLS])
        g.w_loaded = [ctx.enter_context(nc.semaphore(f"w_loaded{k}")) for k in range(RING)]
        g.bm_dram = nc.dram_tensor("bm_dram", [B, 2, 4, S], F32).ap()
        g.ew = g.wring[:, 0, 0:2 * E0 * D]
        g.w_tgt = g.wring[:, 1, 0:2 * D]
        g.w_src = g.wring[:, 1, 2 * D:10 * D]
        g.w_out = g.wring[:, 1, 10 * D:14 * D]
        g.sw = g.wring[:, 2, :]
        g.eb, g.rw, g.rb = sb("eb", [E0, D])[:, :], sb("rw", [P, 2 * E0])[:, :], sb("rb", [1, E0])[:, :]
        g.b_tgt, g.b_key = sb("b_tgt", [P, 2])[:, :], sb("b_key", [P, 2])[:, :]
        g.b_val, g.b_out, g.wg = sb("b_val", [P, D])[:, :], sb("b_out", [P, D])[:, :], sb("wg", [P, 2 * E1])[:, :]
        with ExitStack() as padded:
            g.qpad, g.kz, g.kzb, g.vraw, g.vaug = [padded.enter_context(nc.sbuf_tensor(*t)) for t in (
                ("qpad", [P, 2, QT, H0, 32], F32), ("kz", [P, 2, H0, S], F32), ("kzb", [P, 2, H0, S], BF16),
                ("vraw", [P, 2, QT, D], F32), ("vaug", [P, 2, QT, H0, 32], F32))]
            g.kv_loaded = [padded.enter_context(nc.semaphore(f"kv_loaded{s}")) for s in (0, 1)]
            g.kb_loaded = [padded.enter_context(nc.semaphore(f"kb_loaded{s}")) for s in (0, 1)]
            setup(nc, g, a)
            attn0(nc, g, a)
        ffn0(nc, g, a)
        attn1(nc, g, a)
        g.list_a = sb("list_a", [P, E1], U32)
        g.list_b = sb("list_b", [CAPX, E1], U32)
        g.table = nc.dram_tensor("table", [NT + CAP, ROW], F32).ap()
        g.lists = nc.dram_tensor("lists", [E1, 2, CAP], F32).ap()
        route(nc, g, a)
        experts(nc, g, a)

def lay_out(inputs):
    import numpy as np
    n = {k: np.asarray(v) for k, v in inputs.items()}
    E, F2, H = n["L1_ffn_expert_w1"].shape
    F = F2 // 2

    def rows(w):
        k = w.shape[-2] // 128
        return np.swapaxes(w.reshape(*w.shape[:-2], k, 128, w.shape[-1]), -3, -2).reshape(
            *w.shape[:-2], 128, k * w.shape[-1])

    def everywhere(v, shape):
        return np.broadcast_to(v, shape)

    out = {
        "x": n["x"].reshape(2048, 256),
        "ctx": n["ctx_2048"],
        "ctx_t": n["ctx_2048"].transpose(0, 2, 1),
        "seq": everywhere(n["itok_Bx1_68_817"].reshape(1, 8), (128, 8)),
        "b": n["L0_xattn_b"].reshape(2, 128).T,
        "gates": everywhere(np.stack([n["g_xattn"][0], n["g_ffn"][0], n["g_xattn"][1], n["g_ffn"][1]]).reshape(1, 4), (128, 4)),
        "maskcol": n["mask_BxS2_fk1"].reshape(8, 2, 128).transpose(2, 1, 0),
        "maskrow": n["mask_BxS2_fk1"].reshape(1, 2048),
        "router_w": rows(n["L0_ffn_router_w"]),
        "router_b": n["L0_ffn_router_b"].reshape(1, 8),
        "ew0": n["L0_ffn_expert_w"].reshape(8, 2, 128, 256).transpose(2, 1, 0, 3).reshape(128, 4096),
        "eb0": n["L0_ffn_expert_b"],
        "w_tgt": rows(n["L1_xattn_W_tgt"].T),
        "w_src": rows(n["L1_xattn_W_src"].T),
        "w_out": rows(n["L1_xattn_W_out"].T),
        "b_tgt": n["L1_xattn_b_tgt"].reshape(2, 128).T,
        "b_key": n["L1_xattn_b_src"][:256].reshape(2, 128).T,
        "b_val": everywhere(n["L1_xattn_b_src"][256:].reshape(1, 256), (128, 256)),
        "b_out": everywhere(n["L1_xattn_b_out"].reshape(1, 256), (128, 256)),
        "wg": rows(n["L1_ffn_wg"].T),
        "shared": np.concatenate([rows(n["L1_ffn_shared_w1"].T), rows(n["L1_ffn_shared_w2"].T)], axis=1),
        "experts": np.concatenate([rows(n["L1_ffn_expert_w1"].transpose(0, 2, 1)),
                                   rows(n["L1_ffn_expert_w2"].transpose(0, 2, 1))], axis=2),
    }
    return {k: np.ascontiguousarray(v) for k, v in out.items()}


def kernel(**inputs):
    import concourse.bacc as _bacc
    from concourse import mybir as _mybir
    from concourse.bass_utils import run_bass_kernel_spmd as _run

    nc = _bacc.Bacc("TRN2", target_bir_lowering=False, num_devices=1)
    arrays = lay_out(inputs)
    aps = {k: nc.dram_tensor("in_" + k, v.shape, _mybir.dt.from_np(v.dtype), kind="ExternalInput").ap()
           for k, v in arrays.items()}
    aps["out"] = nc.dram_tensor("out", (NT + CAP, D), F32, kind="ExternalOutput").ap()
    program(nc, aps)
    r = _run(nc, [{"in_" + k: v for k, v in arrays.items()}], core_ids=[0])
    return r.results[0]["out"][0:NT].reshape(B, S, D)
```

```python
from contextlib import ExitStack

import concourse.bass as bass
from concourse import mybir

F32 = mybir.dt.float32
F32R = mybir.dt.float32r
BF16 = mybir.dt.bfloat16
I32 = mybir.dt.int32
U32 = mybir.dt.uint32
ALU = mybir.AluOpType
ACT = mybir.ActivationFunctionType
AX = mybir.AxisListType
ds = bass.ds

P = 128
B, S, D = 8, 256, 256
T = B * S // P
NT = B * S
QT = S // P
EPS = 1e-5
H0, DH0 = 16, 16
E0 = 8
H1, DH1 = 8, 32
E1, TOPK, FF, CAP = 64, 8, 768, 160
KF = FF // P
RA, RB = CAP // 16, 16
CAPX = CAP - P
ROW = D + E1
MASKED0 = -1e12
MASKED1 = -1e30
NEG = -3.0e38
WCOLS = 2 * 2 * FF + KF * D
RING = 4
PARTS = 4
KV_LOADS = 9


class Shared:
    pass


class Chain:

    def __init__(self, eng, sem, per_step):
        self.eng, self.sem, self.per_step = eng, sem, per_step
        self.base = self.k = 0

    def step(self, n):
        self.base, self.k = n * self.per_step, 0

    def resume(self, n, k):
        self.base, self.k = n * self.per_step, k

    def end(self):
        assert self.k == self.per_step, self.k

    def link(self, ins):
        ins.then_inc(self.sem, 1)
        self.k += 1
        self.eng.wait_ge(self.sem, self.base + self.k)


def steps(eng, n, body, slots=2):
    for k in range(slots):
        body(k, 0, k)
    with eng.Fori(1, n // slots - 1) as i:
        for k in range(slots):
            body(slots * i + k, i, k)
    for k in range(n - slots, n):
        body(k, n // slots - 1, k % slots)


def apart(eng):
    eng.nop(nofuse=True)


def tile_statistics(dve, g, t):
    dve.bn_stats(g.st[:, ds(t, 1), :].rearrange("p o n -> p (o n)"), g.x[:, ds(t, 1), :].rearrange("p o d -> p (o d)"))


def scale_of_rows(dve, g, stage):
    done = 2 * stage + (stage > 0)
    for t in range(T):
        ins = dve.bn_aggr(g.mv[:, t, :], g.st[:, t, :])
    ins.then_inc(g.scale_ready, 1)
    dve.wait_ge(g.scale_ready, done + 1)
    dve.tensor_scalar(g.rstd[:, :], g.mv[:, :, 1], EPS, None, ALU.add).then_inc(g.var_eps, 1)
    dve.wait_ge(g.rooted, stage + 1)
    dve.reciprocal(g.rstd[:, :], g.rstd[:, :]).then_inc(g.scale_ready, 1)
    dve.wait_ge(g.scale_ready, done + 2)


def root_of_variance(act, g, stage):
    act.wait_ge(g.var_eps, stage + 1)
    act.activation(g.rstd[:, :], g.rstd[:, :], ACT.Sqrt).then_inc(g.rooted, 1)


def split_matmul(pe, out, lhs, rhs, start, stop):
    for n, (a, b) in enumerate(((0, 0), (0, 1), (1, 0))):
        ins = pe.matmul(out, lhs[a], rhs[b], start=start and n == 0, stop=stop and n == 2)
    return ins


def head_keys(a, b):
    return a["ctx_t"][ds(b, 1), 0:D, :].rearrange("o (g j d) k -> j d (o g) k", j=4, d=DH0)


def load_keys(sp, g, a, b, s):
    for j in range(4):
        sp.dma_start(g.kz[32 * j + 2:32 * j + 2 + DH0, s, j:H0:4, :], head_keys(a, b)[j]).then_inc(g.kv_loaded[s], 16)
    sp.dma_start(g.vraw[:, s, :, :],
                 a["ctx"][ds(b, 1), :, D:2 * D].rearrange("o (k p) d -> p (o k) d", p=P)).then_inc(g.kv_loaded[s], 16)


def load_biases(sp, g, b, s):
    for j in range(4):
        sp.dma_start(g.kz[32 * j:32 * j + 2, s, j:H0:4, :], g.bm_dram[ds(b, 1), :, :, :].rearrange("o r g k -> r (o g) k")
                     ).then_inc(g.kv_loaded[s], 16)


def load_narrow_keys(pool, g, a, b, s):
    for j in range(4):
        pool.dma_start(g.kzb[32 * j + 2:32 * j + 2 + DH0, s, j:H0:4, :], head_keys(a, b)[j]).then_inc(g.kb_loaded[s], 16)


def load_narrow_biases(pool, g, b, s):
    for j in range(4):
        pool.dma_start(g.kzb[32 * j:32 * j + 2, s, j:H0:4, :], g.bm_dram[ds(b, 1), :, :, :].rearrange("o r g k -> r (o g) k")
                       ).then_inc(g.kb_loaded[s], 16)


def load_expert(sp, g, a, e):
    for c in range(PARTS):
        n = slice(c * WCOLS // PARTS, (c + 1) * WCOLS // PARTS)
        sp.dma_start(g.wring[:, e, n], a["experts"][e, :, n]).then_inc(g.w_loaded[e], 16)


def setup(nc, g, a):
    with ExitStack() as ctx:
        def sb(name, shape, dt=F32):
            return ctx.enter_context(nc.sbuf_tensor(name, shape, dt))

        def sem(name):
            return ctx.enter_context(nc.semaphore(name))

        seq = sb("seq", [P, B], I32)
        seqf = sb("seqf", [P, B])
        bcol = sb("bcol", [P, QT])
        kpos = sb("kpos", [P, QT])
        valid = sb("valid", [P, QT, B])
        gates = sb("gates", [P, 4])
        bmrow = sb("bmrow", [B, 2, S])
        mask_rows = sb("mask_rows", [B, S])
        pen_rows = sb("pen_rows", [B, S], BF16)
        const_rows = sb("const_rows", [1, 2, S], BF16)
        x_in, small_in, iotas, masks_made, mask_turned, row_made, row_out, chain = [
            sem(n) for n in ("x_in", "small_in", "iotas", "masks_made", "mask_turned", "row_made",
                             "row_out", "su_chain")]
        zeroed, consts, padded, narrow_padded = sem("zeroed"), sem("consts"), sem("padded"), sem("narrow_padded")
        block = ctx.enter_context(nc.Block())

        @block.sync
        def _(sp):
            sp.dma_start(g.x[:, :, :], a["x"].rearrange("(t p) d -> p t d", p=P)).then_inc(x_in, 16)
            sp.dma_start(seq[:, :], a["seq"]).then_inc(small_in, 16)
            sp.dma_start(bcol[:, :], a["b"]).then_inc(small_in, 16)
            sp.dma_start(gates[:, :], a["gates"]).then_inc(small_in, 16)
            sp.dma_start(g.maskcol[:, :, :], a["maskcol"]).then_inc(small_in, 16)
            sp.dma_start(mask_rows[:, :], a["maskrow"].rearrange("o (b s) -> (o b) s", b=B)).then_inc(small_in, 16)
            sp.wait_ge(padded, 2)
            for b in (0, 1):
                load_keys(sp, g, a, b, b)
            sp.wait_ge(row_made, QT + 2)
            for r in range(4):
                sp.dma_start(g.bm_dram[:, :, r, :], bmrow[:, :, :]).then_inc(row_out, 16)
            sp.dma_start(g.pen_dram[0:B, :], pen_rows[:, :]).then_inc(row_out, 16)
            sp.dma_start(g.pen_dram[B:B + 2, :].unsqueeze(0), const_rows[:, :, :]).then_inc(row_out, 16)
            sp.wait_ge(row_out, 96)

        @block.gpsimd
        def _(pool):
            nc.gpsimd.memset(g.ident[:, :], 0.0).then_inc(zeroed, 1)
            nc.gpsimd.memset(g.tri[:, :], 1.0).then_inc(zeroed, 1)
            nc.gpsimd.memset(g.ones_bf[:, :], 1.0).then_inc(zeroed, 1)
            nc.gpsimd.memset(g.ones_f[:, :], 1.0).then_inc(zeroed, 1)
            nc.gpsimd.iota(kpos[:, :], [[P, QT]], 0, 1, allow_small_or_imprecise_dtypes=True).then_inc(iotas, 1)
            nc.gpsimd.iota(g.iota8[:, :], [[1, E0]], 0, 0, allow_small_or_imprecise_dtypes=True).then_inc(iotas, 1)
            nc.gpsimd.iota(g.iota_b[:, :], [[1, RB]], 0, 0, allow_small_or_imprecise_dtypes=True).then_inc(iotas, 1)
            nc.gpsimd.iota(g.iota_p[:, :], [[1, 1]], 0, 1, allow_small_or_imprecise_dtypes=True).then_inc(iotas, 1)
            nc.gpsimd.iota(g.iota_t[:, :], [[1, T]], 1, 0, allow_small_or_imprecise_dtypes=True).then_inc(iotas, 1)
            nc.gpsimd.iota(g.iota_slot[:, :], [[1, CAP]], NT, 0, allow_small_or_imprecise_dtypes=True).then_inc(iotas, 1)
            pool.wait_ge(zeroed, 4)
            nc.gpsimd.affine_select(out=g.ident[:, :], in_=g.ident[:, :], compare_op=ALU.not_equal, fill=1.0,
                                    base=0, pattern=[[-1, P]], channel_multiplier=1).then_inc(consts, 1)
            nc.gpsimd.affine_select(out=g.tri[:, :], in_=g.tri[:, :], compare_op=ALU.is_ge, fill=0.0,
                                    base=-1, pattern=[[1, P]], channel_multiplier=-1).then_inc(consts, 1)
            nc.gpsimd.memset(g.vaug[:, :, :, :, :], 0.0).then_inc(consts, 1)
            pool.wait_ge(consts, 3)
            nc.gpsimd.memset(g.vaug[:, :, :, :, DH0], 1.0)
            nc.gpsimd.memset(g.kz[:, 1, :, :], 0.0).then_inc(padded, 1)
            nc.gpsimd.memset(g.kzb[:, 1, :, :].bitcast(F32), 0.0).then_inc(narrow_padded, 1)
            nc.gpsimd.memset(g.qpad[:, :, :, :, :], 0.0)
            pool.wait_ge(narrow_padded, 2)
            for b in (0, 1):
                load_narrow_keys(pool, g, a, b, b)

        @block.vector
        def _(dve):
            ch = Chain(dve, chain, 3)
            dve.memset(g.kz[:, 0, :, :], 0.0).then_inc(padded, 1)
            dve.memset(bmrow[:, 0, :], 1.0)
            dve.wait_ge(small_in, 80)
            dve.wait_ge(iotas, 6)
            ch.link(dve.tensor_copy(seqf[:, :], seq[:, :]))
            for k in range(QT):
                ins = dve.tensor_scalar(valid[:, k, :], seqf[:, :], kpos[:, k:k + 1], None, ALU.is_gt)
            ch.link(ins)
            ch.link(dve.tensor_scalar(valid[:, :, :], valid[:, :, :], -1.0, -MASKED0, ALU.add, ALU.mult))
            for k in range(QT):
                ins = dve.tensor_scalar(g.bm0[:, k, :], valid[:, k, :], bcol[:, k:k + 1], None, ALU.add)
            ins.then_inc(masks_made, 1)
            dve.memset(const_rows[:, 0, :], 0.0)
            dve.memset(const_rows[:, 1, :], 1.0).then_inc(row_made, 1)
            dve.tensor_scalar(pen_rows[:, :], mask_rows[:, :], 0.0, MASKED1, ALU.is_equal, ALU.mult).then_inc(row_made, 1)
            for k in range(QT):
                dve.wait_ge(mask_turned, k + 1)
                dve.tensor_copy(bmrow[:, 1, k * P:(k + 1) * P], g.ps[0:B, k, 0:P]).then_inc(row_made, 1)
            dve.memset(g.kzb[:, 0, :, :].bitcast(F32), 0.0).then_inc(narrow_padded, 1)
            dve.wait_ge(x_in, 16)
            for t in range(T):
                dve.bn_stats(g.st[:, t, :], g.x[:, t, :])
            ch.end()

        @block.tensor
        def _(pe):
            pe.wait_ge(consts, 1)
            pe.wait_ge(masks_made, 1)
            for k in range(QT):
                pe.transpose(g.ps[0:B, k, 0:P], g.bm0[:, k, :], g.ident[:, :]).then_inc(mask_turned, 1)

        @block.scalar
        def _(act):
            act.wait_ge(small_in, 80)
            act.activation(g.tg[:, :], gates[:, :], ACT.Tanh)


def attn0(nc, g, a):
    G = H0 // 4
    with ExitStack() as ctx:
        def sb(name, shape, dt=F32):
            return ctx.enter_context(nc.sbuf_tensor(name, shape, dt))

        def sem(name):
            return ctx.enter_context(nc.semaphore(name))

        qpad, kz, kzb, vraw, vaug = g.qpad, g.kz, g.kzb, g.vraw, g.vaug
        qtb = sb("qtb", [P, G, S], BF16)
        qt = sb("qt", [P, 2, G, S])
        pt = sb("pt", [P, 2, QT, 2, S])
        ot = sb("ot", [P, G, S])
        rec = sb("rec", [P, QT, H0])
        upd = sb("upd", [P, QT, H0, DH0])
        kv_loaded, kb_loaded = g.kv_loaded, g.kb_loaded
        weights_in = sem("weights_in")
        v_padded, q_ready, t1_done, qtb_ready = sem("v_padded"), sem("q_ready"), sem("t1_done"), sem("qtb_ready")
        max_ready, max_used, q2_ready, t2_done = sem("max_ready"), sem("max_used"), sem("q2_ready"), sem("t2_done")
        qt_ready, sc_ready, pt_ready, pv_done = sem("qt_ready"), sem("sc_ready"), sem("pt_ready"), sem("pv_done")
        ot_used, outt_done, fin_done, chain = sem("ot_used"), sem("outt_done"), sem("fin_done"), sem("a_chain")
        out_read = sem("out_read")
        ps = g.ps
        TB, MB, SB, QB, OB = 0, 2, 4, 6, 7
        block = ctx.enter_context(nc.Block())

        @block.sync
        def _(sp):
            def load(b, i, s):
                if isinstance(b, int) and b < 2:
                    load_biases(sp, g, b, s)
                else:
                    sp.wait_ge(sc_ready, 16 * (b - 1))
                    sp.wait_ge(v_padded, b - 1)
                    apart(sp)
                    load_keys(sp, g, a, b, s)
                    load_biases(sp, g, b, s)
                if isinstance(b, int) and b == 1:
                    load_weights()

            def load_weights():
                for dst, name in ((g.ew, "ew0"), (g.w_tgt, "w_tgt"), (g.w_src, "w_src"), (g.w_out, "w_out"), (g.sw, "shared"),
                                  (g.eb, "eb0"), (g.rw, "router_w"), (g.rb, "router_b"), (g.b_tgt, "b_tgt"),
                                  (g.b_key, "b_key"), (g.b_val, "b_val"), (g.b_out, "b_out"), (g.wg, "wg")):
                    sp.dma_start(dst, a[name]).then_inc(weights_in, 16)
                load_expert(sp, g, a, 3)

            steps(sp, B, load)
            sp.wait_ge(weights_in, 13 * 16)

        @block.gpsimd
        def _(pool):
            def prepare(b, i, s):
                if not (isinstance(b, int) and b < 2):
                    pool.wait_ge(max_ready, 16 * (b - 1))
                    apart(pool)
                    load_narrow_keys(pool, g, a, b, s)
                load_narrow_biases(pool, g, b, s)
                pool.wait_ge(kv_loaded[s], 16 * KV_LOADS * (i + 1))
                if not (isinstance(b, int) and b < 2):
                    pool.wait_ge(pv_done, 8 * (b - 1))
                apart(pool)
                nc.gpsimd.tensor_copy(vaug[:, s, :, :, 0:DH0],
                                      vraw[:, s, :, :].rearrange("p k (h d) -> p k h d", d=DH0)).then_inc(v_padded, 1)

            steps(pool, B, prepare)

        @block.vector
        def _(dve):
            ch = Chain(dve, chain, 2)
            scale_of_rows(dve, g, 0)
            dve.tensor_scalar(g.rstd[:, :], g.rstd[:, :], DH0 ** -0.5, None, ALU.mult).then_inc(g.scale_ready, 1)
            dve.wait_ge(g.scale_ready, 3)

            def queries(b, s):
                if not (isinstance(b, int) and b < 2):
                    dve.wait_ge(t2_done, b - 1)
                for k in range(QT):
                    dve.tensor_scalar(qpad[:, s, k, :, 2:2 + DH0],
                                      g.x[:, ds(2 * b + k, 1), :].rearrange("p o (h d) -> p (o h) d", d=DH0),
                                      g.mv[:, ds(2 * b + k, 1), 0], g.rstd[:, ds(2 * b + k, 1)],
                                      ALU.subtract, ALU.mult)
                dve.memset(qpad[:, s, :, :, 1], 1.0)
                dve.memset(qpad[:, s, :, :, 0], 0.0).then_inc(q_ready, 1)

            def maxima(b, s, u):
                j, k = u // 2, u % 2
                dve.wait_ge(max_ready, 16 * b + u + 1)
                dve.tensor_reduce(qpad[:, s, k, 2 * j:2 * j + 2, 0],
                                  ps[:, MB + u % 2, :].rearrange("p (h k) -> p h k", h=2), AX.X, ALU.max,
                                  negate=True).then_inc(max_used, 1)

            def mask_off(b, s):
                dve.memset(qpad[:, s, :, :, 1], 0.0).then_inc(q2_ready, 1)

            def keep_ot(b, q):
                dve.wait_ge(pv_done, 8 * b + 4 * q + 4)
                if q == 0 and not (isinstance(b, int) and b < 1):
                    dve.wait_ge(outt_done, b)
                dve.tensor_copy(ot[:, 2 * q:2 * q + 2, :], ps[:, OB, :].rearrange("p (g q) -> p g q", g=2)).then_inc(ot_used, 1)

            def finish(b):
                ch.step(b)
                dve.wait_ge(outt_done, b + 1)
                o = ps[:, TB:TB + 2, :].rearrange("p k (h d) -> p k h d", d=32)
                ch.link(dve.reciprocal(rec[:, :, :], o[:, :, :, DH0]))
                ch.link(dve.tensor_scalar(rec[:, :, :], rec[:, :, :], g.tg[:, 0:1], None, ALU.mult))
                dve.tensor_tensor(upd[:, :, :, :], o[:, :, :, 0:DH0],
                                  rec[:, :, :].unsqueeze(3).broadcast_to([P, QT, H0, DH0]), ALU.mult).then_inc(out_read, 1)
                dve.wait_ge(out_read, b + 1)
                xb = g.x[:, ds(2 * b, 2), :]
                dve.tensor_tensor(xb, xb, upd[:, :, :, :].rearrange("p k h d -> p k (h d)"), ALU.add).then_inc(fin_done, 1)
                dve.wait_ge(fin_done, b + 1)
                apart(dve)
                for k in range(QT):
                    tile_statistics(dve, g, 2 * b + k)
                ch.end()

            queries(0, 0)
            queries(1, 1)
            for u in range(16):
                maxima(0, 0, u)
            mask_off(0, 0)

            def body(b, i, s):
                last, last2 = isinstance(b, int) and b == B - 1, isinstance(b, int) and b >= B - 2
                if not (isinstance(b, int) and b == 0):
                    keep_ot(b - 1, 1)
                    finish(b - 1)
                if not last:
                    for u in range(8):
                        maxima(b + 1, 1 - s, u)
                keep_ot(b, 0)
                if not last:
                    for u in range(8, 16):
                        maxima(b + 1, 1 - s, u)
                    mask_off(b + 1, 1 - s)
                if not last2:
                    queries(b + 2, s)

            steps(dve, B, body)
            keep_ot(B - 1, 1)
            finish(B - 1)

        @block.scalar
        def _(act):
            root_of_variance(act, g, 0)

            def keep_qtb(b, k):
                act.wait_ge(t1_done, 2 * b + k + 1)
                act.activation(qtb[:, :, k * P:(k + 1) * P],
                               ps[:, QB, :].rearrange("p (g q) -> p g q", q=P), ACT.Copy).then_inc(qtb_ready, 1)

            def keep_qt(b, s):
                act.wait_ge(t2_done, b + 1)
                for k in range(QT):
                    act.activation(qt[:, s, :, k * P:(k + 1) * P],
                                   ps[:, TB + k, :].rearrange("p (g q) -> p g q", q=P), ACT.Copy).then_inc(qt_ready, 1)

            def exps(b, j, k):
                act.wait_ge(sc_ready, 16 * b + 2 * j + k + 1)
                if k == 0 and not (isinstance(b, int) and b == 0 and j < 2):
                    act.wait_ge(pv_done, 8 * b + j - 1)
                apart(act)
                act.activation(pt[:, j % 2, k, :, :], ps[:, SB + k, :].rearrange("p (h q) -> p h q", h=2),
                               ACT.Exp, bias=g.bm0[:, k, ds(b, 1)]).then_inc(pt_ready, 1)

            keep_qtb(0, 0)
            keep_qtb(0, 1)
            keep_qt(0, 0)

            def body(b, i, s):
                last = isinstance(b, int) and b == B - 1
                for j in range(8):
                    exps(b, j, 0)
                    if j == 7 and not last:
                        keep_qt(b + 1, 1 - s)
                    exps(b, j, 1)
                    if j < 2 and not last:
                        keep_qtb(b + 1, j)

            steps(act, B, body)

        @block.tensor
        def _(pe):
            def turn1(b, s, k):
                pe.wait_ge(q_ready, b + 1)
                if not (isinstance(b, int) and b == 0 and k == 0):
                    pe.wait_ge(qtb_ready, 2 * b + k)
                for q in range(G):
                    ins = pe.transpose(ps[:, QB, q * P:(q + 1) * P],
                                       qpad[:, s, k, 4 * q:4 * q + 4, :].rearrange("p h d -> p (h d)"), g.ident[:, :])
                ins.then_inc(t1_done, 1)

            def turn2(b, s):
                pe.wait_ge(q2_ready, b + 1)
                if not (isinstance(b, int) and b < 2):
                    pe.wait_ge(out_read, b - 1)
                for k in range(QT):
                    for q in range(G):
                        ins = pe.transpose(ps[:, TB + k, q * P:(q + 1) * P],
                                           qpad[:, s, k, 4 * q:4 * q + 4, :].rearrange("p h d -> p (h d)"), g.ident[:, :])
                ins.then_inc(t2_done, 1)

            def max_pass(b, i, s, u):
                j, k = u // 2, u % 2
                if u == 0:
                    pe.wait_ge(qtb_ready, 2 * b + 2)
                    pe.wait_ge(kb_loaded[s], 128 * (i + 1))
                    pe.wait_ge(kv_loaded[s], 16 * KV_LOADS * (i + 1))
                if not (isinstance(b, int) and b == 0 and u < 2):
                    pe.wait_ge(max_used, 16 * b + u - 1)
                pe.matmul(ps[:, MB + u % 2, :], qtb[:, j // 2, k * P:(k + 1) * P], kzb[:, s, 2 * j:2 * j + 2, :],
                          start=True, stop=True).then_inc(max_ready, 1)

            def scores(b, s, j, k):
                if j == 0 and k == 0:
                    pe.wait_ge(qt_ready, 2 * b + 2)
                if not (isinstance(b, int) and b == 0 and j == 0):
                    pe.wait_ge(pt_ready, 16 * b + 2 * j + k - 1)
                for h in (2 * j, 2 * j + 1):
                    ins = pe.matmul(ps[:, SB + k, (h % 2) * S:(h % 2 + 1) * S],
                                    kz[:, s, h, k * P:(k + 1) * P], qt[:, s, h // 4, :], start=True, stop=True)
                ins.then_inc(sc_ready, 1)

            def values(b, s, j):
                q = j // 2
                if j == 0:
                    pe.wait_ge(v_padded, b + 1)
                pe.wait_ge(pt_ready, 16 * b + 2 * j + 2)
                if j % 4 == 0 and not (isinstance(b, int) and b == 0 and j == 0):
                    pe.wait_ge(ot_used, 2 * b + j // 4)
                for k in range(QT):
                    for h in (2 * j, 2 * j + 1):
                        r = 32 * (h % 4)
                        ins = pe.matmul(ps[r:r + 32, OB, (q % 2) * S:(q % 2 + 1) * S], vaug[:, s, k, h, :],
                                        pt[:, j % 2, k, h % 2, :], start=(k == 0), stop=(k == QT - 1),
                                        tile_position=(0, r))
                ins.then_inc(pv_done, 1)

            def turn_out(b, last):
                pe.wait_ge(ot_used, 2 * b + 2)
                pe.wait_ge(qt_ready, 2 * b + (2 if last else 4))
                for k in range(QT):
                    for q in range(G):
                        ins = pe.transpose(ps[:, TB + k, q * P:(q + 1) * P], ot[:, q, k * P:(k + 1) * P], g.ident[:, :])
                ins.then_inc(outt_done, 1)

            turn1(0, 0, 0)
            turn1(0, 0, 1)
            for u in range(16):
                max_pass(0, 0, 0, u)
            turn2(0, 0)

            def body(b, i, s):
                first, last = isinstance(b, int) and b == 0, isinstance(b, int) and b == B - 1

                def maxima_ahead(j, *places):
                    if 3 <= j < 7 and not last:
                        for n in places:
                            max_pass(b + 1, i + s, 1 - s, 4 * (j - 3) + n)

                for j in range(8):
                    scores(b, s, j, 0)
                    maxima_ahead(j, 0)
                    if j == 7 and not last:
                        turn2(b + 1, 1 - s)
                    scores(b, s, j, 1)
                    maxima_ahead(j, 1)
                    if j == 0:
                        if not first:
                            values(b - 1, 1 - s, 7)
                    else:
                        values(b, s, j - 1)
                    maxima_ahead(j, 2, 3)
                    if j < 2 and not last:
                        turn1(b + 1, 1 - s, j)
                    if j == 1 and not first:
                        turn_out(b - 1, False)

            steps(pe, B, body)
            values(B - 1, (B - 1) % 2, 7)
            turn_out(B - 1, True)


def ffn0(nc, g, a):
    with ExitStack() as ctx:
        def sb(name, shape, dt=F32):
            return ctx.enter_context(nc.sbuf_tensor(name, shape, dt))

        def sem(name):
            return ctx.enter_context(nc.semaphore(name))

        ew = g.ew.rearrange("p (k e d) -> p k e d", k=2, e=E0)
        rw = g.rw.rearrange("p (k e) -> p k e", k=2)
        eb, rb = g.eb, g.rb
        y = sb("y0", [P, D])
        yt = sb("yt0", [P, 2, 2, P])
        yt_hi = sb("yt_hi0", [P, 2, 2, P], F32R)
        yt_lo = sb("yt_lo0", [P, 2, 2, P], F32R)
        ew_hi = sb("ew_hi", [P, 2, E0, D], F32R)
        ew_lo = sb("ew_lo", [P, 2, E0, D], F32R)
        lg = sb("lg0", [P, E0])
        top = sb("top0", [P, 8])
        neg = sb("neg0", [P, 1])
        at = sb("at0", [P, 8], U32)
        atf = sb("atf0", [P, 1])
        hot = sb("hot0", [P, E0])
        ex = sb("ex0", [P, E0])
        total = sb("total0", [P, 1])
        inv = sb("inv0", [P, 1])
        gm = sb("gm0", [P, 2, E0])
        gmt = sb("gmt0", [E0, P])
        y_ready, yt_turned, yt_ready, lg_ready = sem("f_y"), sem("f_yt_turned"), sem("f_yt"), sem("f_lg")
        neg_ready, ex_ready, gm_ready, gmt_turned = sem("f_neg"), sem("f_ex"), sem("f_gm"), sem("f_gmt_turned")
        gmt_ready, bias_ready, mm_ready, acc_done = sem("f_gmt"), sem("f_bias"), sem("f_mm"), sem("f_acc")
        lg_kept, top_ready, at_ready, atf_ready, hot_ready, inv_ready = [sem("f_" + n) for n in (
            "lg_kept", "top", "at", "atf", "hot", "inv")]
        ps = g.ps
        hi_ready, lo_ready, w_hi, w_lo = sem("f_hi"), sem("f_lo"), sem("f_w_hi"), sem("f_w_lo")
        TURN, LOGIT, EXP, GATE, BIAS = 0, 1, 2, 6, 7
        block = ctx.enter_context(nc.Block())

        @block.gpsimd
        def _(pool):
            def rest(t, s):
                pool.wait_ge(hi_ready, t + 1)
                if not (isinstance(t, int) and t < 2):
                    pool.wait_ge(mm_ready, 4 * (t - 1))
                apart(pool)
                nc.gpsimd.tensor_tensor(yt_lo[:, s, :, :], yt[:, s, :, :], yt_hi[:, s, :, :].bitcast(F32), ALU.subtract
                                        ).then_inc(lo_ready, 1)

            def weigh(t, s):
                pool.wait_ge(top_ready, t + 1)
                if not (isinstance(t, int) and t == 0):
                    pool.wait_ge(ex_ready, t)
                apart(pool)
                nc.gpsimd.tensor_scalar(neg[:, :], top[:, 0:1], -1.0, None, ALU.mult).then_inc(neg_ready, 1)
                pool.wait_ge(at_ready, t + 1)
                apart(pool)
                nc.gpsimd.tensor_copy(atf[:, :], at[:, 0:1]).then_inc(atf_ready, 1)
                pool.wait_ge(atf_ready, t + 1)
                apart(pool)
                nc.gpsimd.tensor_scalar(hot[:, :], g.iota8[:, :], atf[:, 0:1], None, ALU.is_equal).then_inc(hot_ready, 1)
                pool.wait_ge(hot_ready, t + 1)
                pool.wait_ge(inv_ready, t + 1)
                if not (isinstance(t, int) and t < 2):
                    pool.wait_ge(gmt_turned, t - 1)
                    apart(pool)
                    pool.wait_ge(acc_done, 9 * (t - 1))
                apart(pool)
                nc.gpsimd.tensor_scalar(gm[:, s, :], hot[:, :], inv[:, 0:1], g.tg[:, 1:2], ALU.mult, ALU.mult).then_inc(gm_ready, 1)

            def body(t, i, s):
                rest(t, s)
                weigh(t, s)

            steps(pool, T, body)

        @block.vector
        def _(dve):
            scale_of_rows(dve, g, 1)

            def normalise(t):
                if not (isinstance(t, int) and t == 0):
                    dve.wait_ge(yt_turned, t)
                dve.tensor_scalar(y[:, :], g.x[:, ds(t, 1), :].rearrange("p o d -> p (o d)"),
                                  g.mv[:, ds(t, 1), 0], g.rstd[:, ds(t, 1)], ALU.subtract, ALU.mult).then_inc(y_ready, 1)

            def pick(t):
                dve.wait_ge(lg_kept, t + 1)
                if not (isinstance(t, int) and t == 0):
                    dve.wait_ge(hot_ready, t)
                apart(dve)
                dve.max(top[:, :], lg[:, :]).then_inc(top_ready, 1)
                dve.wait_ge(top_ready, t + 1)
                apart(dve)
                dve.max_index(at[:, :], top[:, :], lg[:, :]).then_inc(at_ready, 1)

            def gate(t):
                dve.wait_ge(ex_ready, t + 1)
                if not (isinstance(t, int) and t == 0):
                    dve.wait_ge(gm_ready, t)
                dve.reciprocal(inv[:, :], total[:, :]).then_inc(inv_ready, 1)

            def add_bias(t):
                dve.wait_ge(bias_ready, t + 1)
                xt = g.x[:, ds(t, 1), :].rearrange("p o d -> p (o d)")
                dve.tensor_tensor(xt, xt, ps[:, BIAS, 0:D], ALU.add).then_inc(acc_done, 1)
                dve.wait_ge(acc_done, 9 * t + 7)

            def add_experts(t, s, q):
                dve.wait_ge(mm_ready, 4 * t + q + 1)
                if q == 0:
                    dve.wait_ge(gm_ready, t + 1)
                xt = g.x[:, ds(t, 1), :].rearrange("p o d -> p (o d)")
                for e in range(2):
                    dve.scalar_tensor_tensor(xt, ps[:, EXP + q, e * D:(e + 1) * D], gm[:, s, 2 * q + e:2 * q + e + 1], xt,
                                             ALU.mult, ALU.add).then_inc(acc_done, 1)
                    dve.wait_ge(acc_done, 9 * t + (1 if q < 3 else 2) + 2 * q + e)

            def rest_of_weights(q):
                dve.wait_ge(w_hi, q + 1)
                e = slice(2 * q, 2 * q + 2)
                dve.tensor_tensor(ew_lo[:, :, e, :], ew[:, :, e, :], ew_hi[:, :, e, :].bitcast(F32), ALU.subtract
                                  ).then_inc(w_lo, 1)

            normalise(0)
            for q in range(2):
                rest_of_weights(q)
            pick(0)
            gate(0)
            normalise(1)
            for q in range(2, 4):
                rest_of_weights(q)

            def body(t, i, s):
                last = isinstance(t, int) and t == T - 1
                add_experts(t, s, 0)
                add_experts(t, s, 1)
                if not last:
                    pick(t + 1)
                add_experts(t, s, 2)
                if not (isinstance(t, int) and t >= T - 2):
                    normalise(t + 2)
                if not last:
                    gate(t + 1)
                add_bias(t)
                add_experts(t, s, 3)
                apart(dve)
                tile_statistics(dve, g, t)

            steps(dve, T, body)

        @block.scalar
        def _(act):
            root_of_variance(act, g, 1)

            def keep_yt(t, s):
                act.wait_ge(yt_turned, t + 1)
                if not (isinstance(t, int) and t < 2):
                    act.wait_ge(mm_ready, 4 * (t - 1))
                turned = ps[:, TURN, 0:2 * P].rearrange("p (k q) -> p k q", k=2)
                act.activation(yt[:, s, :, :], turned, ACT.Copy).then_inc(yt_ready, 1)
                act.activation(yt_hi[:, s, :, :], turned, ACT.Copy).then_inc(hi_ready, 1)

            def route(t, s):
                act.wait_ge(lg_ready, t + 1)
                if not (isinstance(t, int) and t < 1):
                    act.wait_ge(at_ready, t)
                act.activation(lg[:, :], ps[:, LOGIT, 0:E0], ACT.Copy).then_inc(lg_kept, 1)
                act.wait_ge(neg_ready, t + 1)
                act.wait_ge(lg_kept, t + 1)
                if not (isinstance(t, int) and t < 1):
                    act.wait_ge(inv_ready, t)
                act.activation(ex[:, :], lg[:, :], ACT.Exp, bias=neg[:, 0:1], accum_out=total[:, :]).then_inc(ex_ready, 1)
                act.wait_ge(gmt_turned, t + 1)
                if not (isinstance(t, int) and t < 1):
                    act.wait_ge(bias_ready, t)
                act.activation(gmt[:, :], ps[0:E0, GATE, 0:P], ACT.Copy).then_inc(gmt_ready, 1)

            for q in range(4):
                e = slice(2 * q, 2 * q + 2)
                act.activation(ew_hi[:, :, e, :], ew[:, :, e, :], ACT.Copy).then_inc(w_hi, 1)
                if q == 0:
                    keep_yt(0, 0)
            route(0, 0)

            def body(t, i, s):
                if not (isinstance(t, int) and t == T - 1):
                    keep_yt(t + 1, 1 - s)
                    route(t + 1, 1 - s)

            steps(act, T, body)

        @block.tensor
        def _(pe):
            def turn(t):
                pe.wait_ge(y_ready, t + 1)
                if not (isinstance(t, int) and t == 0):
                    pe.wait_ge(hi_ready, t)
                for k in range(2):
                    ins = pe.transpose(ps[:, TURN, k * P:(k + 1) * P], y[:, k * P:(k + 1) * P], g.ident[:, :])
                ins.then_inc(yt_turned, 1)

            def logits(t, s):
                pe.wait_ge(yt_ready, t + 1)
                if not (isinstance(t, int) and t == 0):
                    pe.wait_ge(lg_kept, t)
                for k in range(2):
                    pe.matmul(ps[:, LOGIT, 0:E0], yt[:, s, k, :], rw[:, k, :], start=(k == 0), stop=False)
                pe.matmul(ps[:, LOGIT, 0:E0], g.ones_f[:, :], rb[:, :], start=False, stop=True).then_inc(lg_ready, 1)

            def turn_gates(t, s):
                pe.wait_ge(gm_ready, t + 1)
                if not (isinstance(t, int) and t == 0):
                    pe.wait_ge(gmt_ready, t)
                pe.transpose(ps[0:E0, GATE, 0:P], gm[:, s, :], g.ident[:, :]).then_inc(gmt_turned, 1)

            def bias(t):
                pe.wait_ge(gmt_ready, t + 1)
                if not (isinstance(t, int) and t == 0):
                    pe.wait_ge(acc_done, 9 * t - 2)
                pe.matmul(ps[:, BIAS, 0:D], gmt[:, :], eb[:, :], start=True, stop=True).then_inc(bias_ready, 1)

            def experts(t, s, q):
                if q == 0:
                    pe.wait_ge(lo_ready, t + 1)
                if isinstance(t, int) and t == 0:
                    pe.wait_ge(w_lo, q + 1)
                else:
                    pe.wait_ge(acc_done, 9 * t - 9 + (2 if q < 3 else 3) + 2 * q)
                e = slice(2 * q, 2 * q + 2)
                for k in range(2):
                    ins = split_matmul(pe, ps[:, EXP + q, :], (yt_hi[:, s, k, :], yt_lo[:, s, k, :]),
                                       (ew_hi[:, k, e, :], ew_lo[:, k, e, :]), k == 0, k == 1)
                ins.then_inc(mm_ready, 1)

            turn(0)
            logits(0, 0)

            def body(t, i, s):
                last = isinstance(t, int) and t == T - 1
                experts(t, s, 0)
                if not last:
                    turn(t + 1)
                turn_gates(t, s)
                experts(t, s, 1)
                if not last:
                    logits(t + 1, 1 - s)
                bias(t)
                experts(t, s, 2)
                experts(t, s, 3)

            steps(pe, T, body)


def attn1(nc, g, a):
    with ExitStack() as ctx:
        def sb(name, shape, dt=F32):
            return ctx.enter_context(nc.sbuf_tensor(name, shape, dt))

        def sem(name):
            return ctx.enter_context(nc.semaphore(name))

        w_tgt, w_src, w_out = [w.rearrange("p (k n) -> p k n", k=k) for w, k in ((g.w_tgt, 2), (g.w_src, 4), (g.w_out, 4))]
        b_tgt, b_key, b_val, b_out = g.b_tgt, g.b_key, g.b_val, g.b_out
        ctx_t = sb("ctx_t", [P, 2, 4, S])
        maskrow = sb("maskrow1", [P, 2, S])
        ones32 = sb("ones32", [P, 32])
        y = sb("y1", [P, QT, D])
        yt = sb("yt1", [P, 2, 2, S])
        kf = sb("kf", [P, 2, S])
        qf = sb("qf", [P, 2, S])
        left = sb("left", [P, 2, S])
        parts = sb("parts", [P, 3, 2, S], BF16)
        ks = sb("ks1", [P, 2, 2, H1, S], BF16)
        qs = sb("qs1", [P, 2, 2, H1, S], BF16)
        vb = sb("vb1", [P, QT, D])
        v = sb("v1", [P, 2, QT, D])
        nm = sb("nm1", [P, QT, H1])
        nmt = sb("nmt1", [H1, S], BF16)
        pt = sb("pt1", [P, 2, QT, 2, S])
        pv = sb("pv1", [P, 2 * S])
        ut = sb("ut1", [P, 2, S])
        ones_in, padded, sw_split, pv_kept = sem("b_ones_in"), sem("b_padded"), sem("sw_split"), sem("b_pv_kept")
        ctx_loaded = [sem(f"b_ctx_loaded{s}") for s in (0, 1)]
        bo_ready = sem("b_bo")
        y_ready, yt_turned, yt_ready = sem("b_y"), sem("b_yt_turned"), sem("b_yt")
        q_done, q_kept, q_hi, q_left, q_mid, q_lo, q_out = [sem("b_" + n) for n in (
            "q_done", "q_kept", "q_hi", "q_left", "q_mid", "q_lo", "q_out")]
        k_done, k_kept, k_hi, k_left, k_mid, k_lo, k_out = [sem("b_" + n) for n in (
            "k_done", "k_kept", "k_hi", "k_left", "k_mid", "k_lo", "k_out")]
        k_in = [sem(f"b_k_in{s}") for s in (0, 1)]
        q_in = [sem(f"b_q_in{s}") for s in (0, 1)]
        v_done, v_kept, v_ready, max_ready, max_used = [sem("b_" + n) for n in (
            "v_done", "v_kept", "v_ready", "max_ready", "max_used")]
        nm_turned, nmt_ready, row_in, sc_ready, pt_ready, pv_done, ut_ready = [sem("b_" + n) for n in (
            "nm_turned", "nmt_ready", "row_in", "sc_ready", "pt_ready", "pv_done", "ut_ready")]
        o_done, x_done, rec_ready, chain = sem("b_o_done"), sem("b_x_done"), sem("b_rec"), sem("b_chain")
        ps = g.ps
        TURN, QO, KV, PV, MB, SB = 0, 1, 2, 3, 4, 6
        SCALE = DH1 ** -0.5
        block = ctx.enter_context(nc.Block())

        @block.sync
        def _(sp):
            def stack(c, s, lo_ready, out, dram, rows, places, loaded, extra, row):
                sp.wait_ge(lo_ready, c + 1)
                apart(sp)
                if not (isinstance(c, int) and c < 2):
                    sp.wait_ge(sc_ready, 8 * (c - 1))
                    apart(sp)
                sp.dma_start(dram[s].rearrange("t (m p) k -> p t m k", p=P), parts[:, :, :, :]).then_inc(out, 16)
                sp.wait_ge(out, 16 * (c + 1))
                apart(sp)
                for n, part in enumerate(places):
                    h, r = n // 4, 32 * (n % 4)
                    sp.dma_start(rows[r:r + 32, s, h, :, :], dram[s, part].rearrange("(h d) k -> d h k", d=DH1)
                                 ).then_inc(loaded[s], 16)
                sp.dma_start(rows[row:row + 1, s, 1, :, :], g.pen_dram[ds(extra, 1), :].unsqueeze(1).broadcast_to([1, H1, S])
                             ).then_inc(loaded[s], 16)

            def keys(c, s):
                stack(c, s, k_lo, k_out, g.k_dram, ks, (0, 0, 1, 1, 0, 2), k_in, c, 64)

            def queries(c, s):
                stack(c, s, q_lo, q_out, g.q_dram, qs, (0, 1, 0, 1, 2, 0), q_in, B, 96)

            sp.wait_ge(padded, 3)
            for rows, row in ((ks, 96), (qs, 64)):
                for s in (0, 1):
                    sp.dma_start(rows[row:row + 1, s, 1, :, :],
                                 g.pen_dram[B + 1:B + 2, :].unsqueeze(1).broadcast_to([1, H1, S])).then_inc(ones_in, 16)
            for c in (0, 1):
                keys(c, c)
                queries(c, c)

            def body(b, i, s):
                ahead = not (isinstance(b, int) and b >= B - 2)
                if ahead:
                    keys(b + 2, s)
                    queries(b + 2, s)

            steps(sp, B, body)
            load_expert(sp, g, a, 0)

        @block.gpsimd
        def _(pool):
            nc.gpsimd.memset(ones32[:, :], 1.0).then_inc(padded, 1)

            def split_weights(c):
                n = slice(c * WCOLS // PARTS, (c + 1) * WCOLS // PARTS)
                nc.gpsimd.tensor_copy(g.sw_hi[:, n], g.sw[:, n]).then_inc(sw_split, 1)
                pool.wait_ge(sw_split, 2 * c + 1)
                nc.gpsimd.tensor_tensor(g.sw_lo[:, n], g.sw[:, n], g.sw_hi[:, n].bitcast(F32), ALU.subtract).then_inc(sw_split, 1)

            def rests(c, f, hi, left_ready, mid, lo):
                pool.wait_ge(hi, c + 1)
                apart(pool)
                nc.gpsimd.tensor_tensor(left[:, :, :], f[:, :, :], parts[:, 0, :, :], ALU.subtract).then_inc(left_ready, 1)
                pool.wait_ge(mid, c + 1)
                apart(pool)
                nc.gpsimd.tensor_tensor(parts[:, 2, :, :], left[:, :, :], parts[:, 1, :, :], ALU.subtract).then_inc(lo, 1)

            def prepare(c):
                rests(c, kf, k_hi, k_left, k_mid, k_lo)
                rests(c, qf, q_hi, q_left, q_mid, q_lo)

            prepare(0)
            prepare(1)

            def body(b, i, s):
                if not (isinstance(b, int) and b >= B - 2):
                    prepare(b + 2)
                else:
                    for c in (2 * (b - B + 2), 2 * (b - B + 2) + 1):
                        split_weights(c)

            steps(pool, B, body)

        @block.vector
        def _(dve):
            ch = Chain(dve, chain, 1)
            scale_of_rows(dve, g, 2)
            dve.tensor_scalar(b_out[:, :], b_out[:, :], g.tg[:, 2:3], None, ALU.mult).then_inc(bo_ready, 1)
            dve.wait_ge(bo_ready, 1)

            def normalise(b):
                if not (isinstance(b, int) and b == 0):
                    dve.wait_ge(yt_turned, b)
                for k in range(QT):
                    ins = dve.tensor_scalar(y[:, k, :], g.x[:, ds(2 * b + k, 1), :].rearrange("p o d -> p (o d)"),
                                            g.mv[:, ds(2 * b + k, 1), 0], g.rstd[:, ds(2 * b + k, 1)],
                                            ALU.subtract, ALU.mult)
                ins.then_inc(y_ready, 1)

            def keep_k(b, i, s):
                dve.wait_ge(k_done, b + 1)
                dve.wait_ge(ctx_loaded[s], 32 * (i + 1))
                if not (isinstance(b, int) and b == 0):
                    dve.wait_ge(k_left, b)
                for m in range(2):
                    ins = dve.scalar_tensor_tensor(kf[:, m, :], ps[:, KV, m * S:(m + 1) * S], b_key[:, m:m + 1],
                                                   maskrow[:, s, :], ALU.add, ALU.mult)
                ins.then_inc(k_kept, 1)

            def keep_q(b, s):
                dve.wait_ge(q_done, b + 1)
                if not (isinstance(b, int) and b == 0):
                    dve.wait_ge(q_left, b)
                for m in range(2):
                    ins = dve.scalar_tensor_tensor(qf[:, m, :], ps[:, QO, m * S:(m + 1) * S], b_tgt[:, m:m + 1],
                                                   maskrow[:, s, :], ALU.add, ALU.mult)
                ins.then_inc(q_kept, 1)

            def keep_v(b):
                dve.wait_ge(v_done, b + 1)
                if not (isinstance(b, int) and b < 1):
                    dve.wait_ge(v_ready, 2 * b)
                dve.tensor_tensor(vb[:, :, :], ps[:, KV, :].rearrange("p (k d) -> p k d", k=2),
                                  b_val[:, :].unsqueeze(1).broadcast_to([P, QT, D]), ALU.add).then_inc(v_kept, 1)

            def maxima(b, u):
                j, k = u // 2, u % 2
                dve.wait_ge(max_ready, 8 * b + u + 1)
                if u == 0 and not (isinstance(b, int) and b == 0):
                    dve.wait_ge(nm_turned, b)
                dve.tensor_reduce(nm[:, k, 2 * j:2 * j + 2], ps[:, MB + u % 2, :].rearrange("p (h k) -> p h k", h=2),
                                  AX.X, ALU.max, negate=True).then_inc(max_used, 1)

            def keep_ut(b, q):
                dve.wait_ge(pv_kept, 2 * b + q + 1)
                if q == 0 and not (isinstance(b, int) and b == 0):
                    dve.wait_ge(o_done, b)
                dve.reciprocal(pv[:, S:2 * S], pv[:, S:2 * S]).then_inc(rec_ready, 1)
                dve.wait_ge(rec_ready, 2 * b + q + 1)
                dve.tensor_tensor(ut[:, q, :], pv[:, 0:S], pv[:, S:2 * S], ALU.mult).then_inc(ut_ready, 1)

            def finish(b):
                ch.step(b)
                dve.wait_ge(o_done, b + 1)
                xb = g.x[:, ds(2 * b, 2), :]
                dve.scalar_tensor_tensor(xb, ps[:, QO, :].rearrange("p (k d) -> p k d", k=2), g.tg[:, 2:3], xb,
                                         ALU.mult, ALU.add).then_inc(x_done, 1)
                dve.wait_ge(x_done, b + 1)
                ch.link(dve.tensor_tensor(xb, xb, b_out[:, :].unsqueeze(1).broadcast_to([P, QT, D]), ALU.add))
                apart(dve)
                for k in range(QT):
                    tile_statistics(dve, g, 2 * b + k)
                ch.end()

            normalise(0)
            dve.memset(ks[64:P, :, 1, :, :].bitcast(F32), 0.0).then_inc(padded, 1)
            dve.memset(qs[64:P, :, 1, :, :].bitcast(F32), 0.0).then_inc(padded, 1)
            for c in (0, 1):
                if c == 1:
                    normalise(1)
                keep_k(c, 0, c)
                keep_v(c)
                keep_q(c, c)
            for u in range(8):
                maxima(0, u)

            def body(b, i, s):
                last, ahead = isinstance(b, int) and b == B - 1, not (isinstance(b, int) and b >= B - 2)
                if ahead:
                    normalise(b + 2)
                keep_ut(b, 0)
                keep_ut(b, 1)
                if ahead:
                    keep_k(b + 2, i + 1, s)
                if not last:
                    for u in range(4):
                        maxima(b + 1, u)
                finish(b)
                if not last:
                    for u in range(4, 8):
                        maxima(b + 1, u)
                if ahead:
                    keep_v(b + 2)
                    keep_q(b + 2, s)

            steps(dve, B, body)

        @block.scalar
        def _(act):
            def keep_yt(b, s):
                act.wait_ge(yt_turned, b + 1)
                if not (isinstance(b, int) and b < 2):
                    act.wait_ge(o_done, b - 1)
                act.activation(yt[:, s, :, :], ps[:, TURN, :].rearrange("p (k q) -> p k q", k=2), ACT.Copy).then_inc(yt_ready, 1)

            def load(b, s):
                if not (isinstance(b, int) and b < 2):
                    act.wait_ge(v_done, b - 1)
                    apart(act)
                act.dma_start(ctx_t[:, s, :, :], a["ctx_t"][ds(b, 1), :, :].rearrange("o (k p) q -> p (o k) q", p=P)
                             ).then_inc(ctx_loaded[s], 16)
                act.dma_start(maskrow[:, s, :], a["maskrow"][:, ds(b * S, S)].partition_broadcast(P)
                             ).then_inc(ctx_loaded[s], 16)

            def first_part(c, f, kept, hi):
                act.wait_ge(kept, c + 1)
                if f is qf:
                    act.wait_ge(k_out, 16 * (c + 1))
                elif not (isinstance(c, int) and c == 0):
                    act.wait_ge(q_out, 16 * c)
                act.activation(parts[:, 0, :, :], f[:, :, :], ACT.Copy).then_inc(hi, 1)

            def second_part(c, left_ready, mid):
                act.wait_ge(left_ready, c + 1)
                act.activation(parts[:, 1, :, :], left[:, :, :], ACT.Copy).then_inc(mid, 1)

            def keep_v(b, s):
                act.wait_ge(v_kept, b + 1)
                if not (isinstance(b, int) and b < 2):
                    act.wait_ge(pv_done, 4 * (b - 1))
                apart(act)
                for k in range(QT):
                    act.activation(v[:, s, k, :], vb[:, k, :], ACT.Copy, scale=g.maskcol[:, k, ds(b, 1)]).then_inc(v_ready, 1)

            def keep_nmt(b, s):
                act.wait_ge(nm_turned, b + 1)
                if not (isinstance(b, int) and b == 0):
                    act.wait_ge(row_in, 16 * b)
                act.activation(nmt[:, :], ps[0:H1, TURN, 0:S], ACT.Copy).then_inc(nmt_ready, 1)
                act.wait_ge(nmt_ready, b + 1)
                apart(act)
                act.dma_start(qs[96:97, s, 1, :, :], nmt[:, :]).then_inc(row_in, 16)

            def exps(b, j):
                for k in range(QT):
                    u = 2 * j + k
                    act.wait_ge(sc_ready, 8 * b + u + 1)
                    if k == 0 and not (isinstance(b, int) and b == 0 and j < 2):
                        act.wait_ge(pv_done, 4 * b + j - 1)
                    act.activation(pt[:, j % 2, k, :, :], ps[:, SB + u % 2, :].rearrange("p (h q) -> p h q", h=2),
                                   ACT.Exp, scale=SCALE).then_inc(pt_ready, 1)

            def keep_pv(b, q):
                act.wait_ge(pv_done, 4 * b + 2 * q + 2)
                if not (isinstance(b, int) and b == 0 and q == 0):
                    act.wait_ge(ut_ready, 2 * b + q)
                act.activation(pv[:, :], ps[:, PV, :], ACT.Copy).then_inc(pv_kept, 1)

            def keys(c):
                first_part(c, kf, k_kept, k_hi)
                second_part(c, k_left, k_mid)

            load(0, 0)
            load(1, 1)
            root_of_variance(act, g, 2)
            for c in (0, 1):
                keys(c)
                keep_yt(c, c)
                keep_v(c, c)
                first_part(c, qf, q_kept, q_hi)
                second_part(c, q_left, q_mid)
            keep_nmt(0, 0)

            def body(b, i, s):
                ahead = not (isinstance(b, int) and b >= B - 2)
                if ahead:
                    load(b + 2, s)
                exps(b, 0)
                if not (isinstance(b, int) and b in (0, B - 1)):
                    first_part(b + 1, qf, q_kept, q_hi)
                exps(b, 1)
                if not (isinstance(b, int) and b in (0, B - 1)):
                    second_part(b + 1, q_left, q_mid)
                exps(b, 2)
                keep_pv(b, 0)
                exps(b, 3)
                keep_pv(b, 1)
                if ahead:
                    keys(b + 2)
                    keep_yt(b + 2, s)
                if not (isinstance(b, int) and b == B - 1):
                    keep_nmt(b + 1, 1 - s)
                if ahead:
                    keep_v(b + 2, s)

            steps(act, B, body)

        @block.tensor
        def _(pe):

            def turn(b):
                pe.wait_ge(y_ready, b + 1)
                if isinstance(b, int) and b == 1:
                    pe.wait_ge(yt_ready, 1)
                elif not isinstance(b, int) or b > 1:
                    pe.wait_ge(nmt_ready, b - 1)
                for d in range(2):
                    for k in range(QT):
                        ins = pe.transpose(ps[:, TURN, d * S + k * P:d * S + (k + 1) * P], y[:, k, d * P:(d + 1) * P],
                                           g.ident[:, :])
                ins.then_inc(yt_turned, 1)

            def project_q(b, s):
                pe.wait_ge(yt_ready, b + 1)
                if isinstance(b, int) and b == 1:
                    pe.wait_ge(q_kept, 1)
                elif not isinstance(b, int) or b > 1:
                    pe.wait_ge(x_done, b - 1)
                for m in range(2):
                    for d in range(2):
                        ins = pe.matmul(ps[:, QO, m * S:(m + 1) * S], w_tgt[:, d, m * P:(m + 1) * P], yt[:, s, d, :],
                                        start=(d == 0), stop=(d == 1))
                ins.then_inc(q_done, 1)

            def project_k(b, i, s, m):
                if m == 0:
                    pe.wait_ge(ctx_loaded[s], 32 * (i + 1))
                    if not (isinstance(b, int) and b == 0):
                        pe.wait_ge(v_kept, b)
                for d in range(4):
                    ins = pe.matmul(ps[:, KV, m * S:(m + 1) * S], w_src[:, d, m * P:(m + 1) * P], ctx_t[:, s, d, :],
                                    start=(d == 0), stop=(d == 3))
                if m == 1:
                    ins.then_inc(k_done, 1)

            def project_v(b, s, k):
                if k == 0:
                    pe.wait_ge(k_kept, b + 1)
                for d in range(4):
                    ins = pe.matmul(ps[:, KV, k * D:(k + 1) * D], ctx_t[:, s, d, k * P:(k + 1) * P], w_src[:, d, D:2 * D],
                                    start=(d == 0), stop=(d == 3))
                if k == 1:
                    ins.then_inc(v_done, 1)

            def max_pass(b, i, s, u):
                j, k = u // 2, u % 2
                if u == 0:
                    pe.wait_ge(k_in[s], 16 * 7 * (i + 1))
                    pe.wait_ge(q_in[s], 16 * 7 * (i + 1))
                if not (isinstance(b, int) and b == 0 and u < 2):
                    pe.wait_ge(max_used, 8 * b + u - 1)
                for h in (2 * j, 2 * j + 1):
                    for n in range(2):
                        ins = pe.matmul(ps[:, MB + u % 2, (h % 2) * S:(h % 2 + 1) * S], qs[:, s, n, h, k * P:(k + 1) * P],
                                        ks[:, s, n, h, :], start=(n == 0), stop=(n == 1))
                ins.then_inc(max_ready, 1)

            def turn_maxima(b, last):
                pe.wait_ge(max_used, 8 * b + 8)
                pe.wait_ge(yt_ready, b + (1 if last else 2))
                for k in range(QT):
                    ins = pe.transpose(ps[0:H1, TURN, k * P:(k + 1) * P], nm[:, k, :], g.ident[:, :])
                ins.then_inc(nm_turned, 1)

            def scores(b, s, j):
                if j == 0:
                    pe.wait_ge(row_in, 16 * (b + 1))
                for k in range(QT):
                    u = 2 * j + k
                    if not (isinstance(b, int) and b == 0 and u < 2):
                        pe.wait_ge(pt_ready, 8 * b + u - 1)
                    for h in (2 * j, 2 * j + 1):
                        for n in range(2):
                            ins = pe.matmul(ps[:, SB + u % 2, (h % 2) * S:(h % 2 + 1) * S], ks[:, s, n, h, k * P:(k + 1) * P],
                                            qs[:, s, n, h, :], start=(n == 0), stop=(n == 1))
                    ins.then_inc(sc_ready, 1)

            def values(b, s, j):
                if j == 0:
                    pe.wait_ge(v_ready, 2 * b + 2)
                pe.wait_ge(pt_ready, 8 * b + 2 * j + 2)
                if j % 2 == 0 and not (isinstance(b, int) and b == 0 and j == 0):
                    pe.wait_ge(pv_kept, 2 * b + j // 2)
                for lhs, c in ((v, 0), (ones32, S)):
                    for k in range(QT):
                        for h in (2 * j, 2 * j + 1):
                            r = 32 * (h % 4)
                            w = v[:, s, k, h * DH1:(h + 1) * DH1] if lhs is v else ones32[:, :]
                            ins = pe.matmul(ps[r:r + 32, PV, c:c + S], w, pt[:, j % 2, k, h % 2, :],
                                            start=(k == 0), stop=(k == QT - 1), tile_position=(0, r))
                ins.then_inc(pv_done, 1)

            def project_out(b, s, k, last):
                if k == 0:
                    pe.wait_ge(ut_ready, 2 * b + 2)
                    pe.wait_ge(q_kept, b + (1 if last else 2))
                for d in range(4):
                    lhs = (yt[:, s, d, k * P:(k + 1) * P] if d < 2 else ut[:, d - 2, k * P:(k + 1) * P])
                    ins = pe.matmul(ps[:, QO, k * D:(k + 1) * D], lhs, w_out[:, d, :], start=(d == 0), stop=(d == 3))
                if k == 1:
                    ins.then_inc(o_done, 1)

            for c in (0, 1):
                project_k(c, 0, c, 0)
                project_k(c, 0, c, 1)
                turn(c)
                project_v(c, c, 0)
                project_v(c, c, 1)
                project_q(c, c)
            pe.wait_ge(padded, 3)
            pe.wait_ge(ones_in, 64)
            for u in range(8):
                max_pass(0, 0, 0, u)
            turn_maxima(0, False)

            def body(b, i, s):
                last, ahead = isinstance(b, int) and b == B - 1, not (isinstance(b, int) and b >= B - 2)
                scores(b, s, 0)
                scores(b, s, 1)
                values(b, s, 0)
                scores(b, s, 2)
                values(b, s, 1)
                scores(b, s, 3)
                values(b, s, 2)
                values(b, s, 3)
                def maxima_ahead(u):
                    if not last:
                        max_pass(b + 1, i + s, 1 - s, u)
                        max_pass(b + 1, i + s, 1 - s, u + 1)

                if ahead:
                    project_k(b + 2, i + 1, s, 0)
                    project_k(b + 2, i + 1, s, 1)
                project_out(b, s, 0, last)
                maxima_ahead(0)
                project_out(b, s, 1, last)
                maxima_ahead(2)
                if ahead:
                    turn(b + 2)
                maxima_ahead(4)
                if ahead:
                    project_v(b + 2, s, 0)
                maxima_ahead(6)
                if ahead:
                    project_v(b + 2, s, 1)
                if not last:
                    turn_maxima(b + 1, not ahead)
                if ahead:
                    project_q(b + 2, s)

            steps(pe, B, body)


def route(nc, g, a):
    with ExitStack() as ctx:
        def sb(name, shape, dt=F32):
            return ctx.enter_context(nc.sbuf_tensor(name, shape, dt))

        def sem(name):
            return ctx.enter_context(nc.semaphore(name))

        W1 = 2 * 2 * FF
        wg = g.wg.rearrange("p (k e) -> p k e", k=2)
        sw1 = [w[:, 0:W1].rearrange("p (k f) -> p k f", k=2) for w in (g.sw_hi, g.sw_lo)]
        sw2 = [w[:, W1:WCOLS].rearrange("p (k d) -> p k d", k=KF) for w in (g.sw_hi, g.sw_lo)]
        y = sb("y2", [P, 2, QT, D])
        yt = sb("yt2", [P, 2, 2, S])
        yt_hi = sb("yt_hi2", [P, 2, 2, S], F32R)
        yt_lo = sb("yt_lo2", [P, 2, 2, S], F32R)
        lg = sb("lg2", [P, QT, E1])
        top = sb("top2", [P, QT, 8])
        neg = sb("neg2", [P, QT])
        rest = sb("rest2", [P, QT, E1])
        mask = sb("mask2", [P, QT, E1])
        maskb = sb("maskb2", [P, QT, E1], BF16)
        seen = sb("seen2", [P, 2, E1], BF16)
        ex = sb("ex2", [P, QT, E1])
        total = sb("total2", [P, QT])
        picked = sb("picked2", [P, QT])
        coef = sb("coef2", [P, 3, QT])
        wrow = sb("wrow2", [P, 2, QT, E1])
        rank = sb("rank2", [P, QT, E1])
        ranki = sb("ranki2", [P, QT, E1], I32)
        hi = sb("hi2", [P, QT, E1], I32)
        lo = sb("lo2", [P, QT, E1], I32)
        hif = sb("hif2", [P, QT, E1], BF16)
        lof = sb("lof2", [P, QT, E1], BF16)
        hot_a = sb("hot_a", [P, QT, E1, RA], BF16)
        aa = sb("aa", [P, QT, E1, 32], BF16)
        bb = sb("bb", [P, QT, E1, RB], BF16)
        zero = sb("zero2", [P, 512], BF16)
        zrow = sb("zrow2", [P, CAP * ROW // P])
        sil = sb("sil2", [P, 2, S])
        gt = sb("gt2", [P, 2, S])
        gt_hi = sb("gt_hi2", [P, 2, KF, S], F32R)
        gt_lo = sb("gt_lo2", [P, 2, KF, S], F32R)
        base = sb("base2", [P, QT, D])
        tt = sb("tt2", [P, E1 // 4, RB])
        pair = sb("pair2", [E1, 2, CAP])
        tok = sb("tok2", [E1, 3, CAP])
        names = ("r_zeroed", "r_y", "r_yt_turned", "r_yt", "r_lg",
                 "r_neg", "r_ex", "r_chain", "r_maskb", "r_rank", "r_wrow", "r_hot", "r_hot_used", "r_up", "r_sil",
                 "r_gt", "r_out", "r_base", "r_tt", "r_tt_out", "r_pair", "r_tok", "r_tok_turned", "r_fill")
        (zeroed, y_ready, yt_turned, yt_ready, lg_ready, neg_ready, ex_ready,
         chain, maskb_ready, rank_ready, wrow_ready, hot_ready, hot_used, up_ready, sil_ready, gt_ready, out_ready,
         base_ready, tt_ready, tt_out, pair_in, tok_ready, tok_turned, filled) = [sem(n) for n in names]
        table_out = [sem(f"table_out{s}") for s in (0, 1)]
        base_out = sem("base_out")
        hi_ready, lo_ready, gt_hi_ready, gt_lo_ready, compared = [sem("r_" + n) for n in (
            "yt_hi", "yt_lo", "gt_hi", "gt_lo", "compared")]
        tchain = sem("r_tchain")
        ps = g.ps
        TURN, LOGIT, RANK, UP, OUT, LIST = 0, 1, 2, 3, 5, 6
        block = ctx.enter_context(nc.Block())

        @block.sync
        def _(sp):
            sp.wait_ge(zeroed, 4)
            sp.dma_start(g.table[NT:NT + CAP, :].rearrange("r d -> (r d)").rearrange("(p n) -> p n", p=P), zrow[:, :]).then_inc(filled, 16)
            sp.dma_start(a["out"][NT:NT + CAP, :].rearrange("r d -> (r d)").rearrange("(p n) -> p n", p=P), zrow[:, 0:CAP * D // P]
                         ).then_inc(filled, 16)

            def store_table(b, s):
                sp.wait_ge(wrow_ready, b + 1)
                apart(sp)
                rows = g.table[ds(b * S, S), :].rearrange("(k p) d -> p k d", p=P)
                sp.dma_start(rows[:, :, 0:D], y[:, s, :, :]).then_inc(table_out[s], 16)
                sp.dma_start(rows[:, :, D:ROW], wrow[:, s, :, :]).then_inc(table_out[s], 16)

            def store_base(b):
                sp.wait_ge(base_ready, b + 1)
                apart(sp)
                sp.dma_start(a["out"][ds(b * S, S), :].rearrange("(k p) d -> p k d", p=P), base[:, :, :]).then_inc(base_out, 16)

            def store(b, i, s):
                store_table(b, s)
                if not (isinstance(b, int) and b == 0):
                    store_base(b - 1)

            load_expert(sp, g, a, 1)
            steps(sp, B, store)
            sp.wait_ge(tt_ready, 4)
            for i in range(4):
                for m in range(2):
                    r = 32 * i + m * RA
                    sp.dma_start(g.lists[i:E1:4, m, :].rearrange("g (a b) -> a g b", b=RB), tt[r:r + RA, :, :]
                                 ).then_inc(tt_out, 16)
            sp.wait_ge(tt_out, 128)
            sp.dma_start(pair[:, :, :], g.lists[:, :, :]).then_inc(pair_in, 16)
            store_base(B - 1)
            sp.wait_ge(base_out, 16 * B)
            for s in (0, 1):
                sp.wait_ge(table_out[s], 32 * (B // 2))
            sp.wait_ge(filled, 32)
            sp.wait_ge(pair_in, 16)

        @block.gpsimd
        def _(pool):
            nc.gpsimd.memset(aa[:, :, :, :], 0.0).then_inc(zeroed, 1)
            nc.gpsimd.memset(zero[:, :], 0.0).then_inc(zeroed, 1)
            nc.gpsimd.memset(zrow[:, :], 0.0).then_inc(zeroed, 1)
            nc.gpsimd.memset(seen[:, :, :], 0.0).then_inc(zeroed, 1)

            def rest_of_rows(b, s):
                pool.wait_ge(hi_ready, b + 1)
                if not (isinstance(b, int) and b < 2):
                    pool.wait_ge(up_ready, KF * (b - 1))
                apart(pool)
                nc.gpsimd.tensor_tensor(yt_lo[:, s, :, :], yt[:, s, :, :], yt_hi[:, s, :, :].bitcast(F32), ALU.subtract
                                        ).then_inc(lo_ready, 1)

            def rest_of_hidden(b, s, f):
                pool.wait_ge(gt_hi_ready, KF * b + f + 1)
                if f == 0 and not (isinstance(b, int) and b < 2):
                    pool.wait_ge(out_ready, b - 1)
                apart(pool)
                nc.gpsimd.tensor_tensor(gt_lo[:, s, f, :], gt[:, f % 2, :], gt_hi[:, s, f, :].bitcast(F32), ALU.subtract
                                        ).then_inc(gt_lo_ready, 1)

            def body(b, i, s):
                if isinstance(b, int) and b == 0:
                    rest_of_rows(0, 0)
                for f in range(3):
                    rest_of_hidden(b, s, f)
                if not (isinstance(b, int) and b == B - 1):
                    rest_of_rows(b + 1, 1 - s)
                for f in range(3, KF):
                    rest_of_hidden(b, s, f)

            steps(pool, B, body)

        @block.vector
        def _(dve):
            ch = Chain(dve, chain, 17)
            scale_of_rows(dve, g, 3)
            dve.wait_ge(zeroed, 4)

            def normalise(b, i, s):
                if not (isinstance(b, int) and b < 2):
                    dve.wait_ge(yt_turned, b - 1)
                    dve.wait_ge(table_out[s], 32 * i)
                    apart(dve)
                for k in range(QT):
                    ins = dve.tensor_scalar(y[:, s, k, :], g.x[:, ds(2 * b + k, 1), :].rearrange("p o d -> p (o d)"),
                                            g.mv[:, ds(2 * b + k, 1), 0], g.rstd[:, ds(2 * b + k, 1)],
                                            ALU.subtract, ALU.mult)
                ins.then_inc(y_ready, 1)

            def pick(b):
                ch.step(b)
                dve.wait_ge(lg_ready, b + 1)
                ch.link(dve.tensor_copy(lg[:, :, :], ps[:, LOGIT, 0:QT * E1].rearrange("p (k e) -> p k e", k=QT)))
                apart(dve)
                for k in range(QT):
                    ins = dve.max(top[:, k, :], lg[:, k, :])
                ch.link(ins)
                dve.tensor_scalar(neg[:, :], top[:, :, 0], -1.0, None, ALU.mult).then_inc(neg_ready, 1)
                apart(dve)
                for k in range(QT):
                    ins = dve.match_replace(rest[:, k, :], top[:, k, :], lg[:, k, :], NEG)
                ch.link(ins)
                if not (isinstance(b, int) and b == 0):
                    dve.wait_ge(rank_ready, b)
                ch.link(dve.tensor_tensor(mask[:, :, :], rest[:, :, :], lg[:, :, :], ALU.not_equal))
                dve.tensor_copy(maskb[:, :, :], mask[:, :, :]).then_inc(maskb_ready, 1)

            def weigh(b, i, s):
                dve.wait_ge(ex_ready, 2 * b + 2)
                ch.link(dve.tensor_tensor(ex[:, :, :], ex[:, :, :], mask[:, :, :], ALU.mult))
                dve.tensor_reduce(picked[:, :], ex[:, :, :], AX.X, ALU.add)
                ch.link(dve.reciprocal(coef[:, 0, :], total[:, :]))
                ch.link(dve.tensor_tensor(coef[:, 1, :], picked[:, :], coef[:, 0, :], ALU.mult))
                ch.link(dve.tensor_scalar(coef[:, 1, :], coef[:, 1, :], 1.1920929e-07, None, ALU.max))
                ch.link(dve.reciprocal(coef[:, 2, :], coef[:, 1, :]))
                ch.link(dve.tensor_tensor(coef[:, 2, :], coef[:, 2, :], coef[:, 0, :], ALU.mult))
                ch.link(dve.tensor_scalar(coef[:, 2, :], coef[:, 2, :], g.tg[:, 3:4], None, ALU.mult))
                if not (isinstance(b, int) and b < 2):
                    dve.wait_ge(table_out[s], 32 * i)
                dve.tensor_tensor(wrow[:, s, :, :], ex[:, :, :], coef[:, 2, :].unsqueeze(2).broadcast_to([P, QT, E1]),
                                  ALU.mult).then_inc(wrow_ready, 1)

            def ranks_to_digits(b, s):
                dve.wait_ge(rank_ready, b + 1)
                ch.link(dve.scalar_tensor_tensor(rank[:, :, :], mask[:, :, :], -4096.0,
                                                 ps[:, RANK, 0:QT * E1].rearrange("p (k e) -> p k e", k=QT),
                                                 ALU.mult, ALU.add))
                ch.link(dve.tensor_scalar(ranki[:, :, :], rank[:, :, :], 4096.0, None, ALU.add))
                dve.tensor_scalar(hi[:, :, :], ranki[:, :, :], 4, None, ALU.logical_shift_right)
                ch.link(dve.tensor_scalar(lo[:, :, :], ranki[:, :, :], 15, None, ALU.bitwise_and))
                dve.tensor_copy(hif[:, :, :], hi[:, :, :])
                ch.link(dve.tensor_copy(lof[:, :, :], lo[:, :, :]))
                ch.link(dve.tensor_tensor(seen[:, 1 - s, :], seen[:, s, :], maskb[:, 0, :], ALU.add))
                ch.link(dve.tensor_tensor(seen[:, 1 - s, :], seen[:, 1 - s, :], maskb[:, 1, :], ALU.add))

            def slots(b):
                if not (isinstance(b, int) and b == 0):
                    dve.wait_ge(hot_used, b)
                iota = g.iota_b[:, :].unsqueeze(1).broadcast_to([P, E1, RB])
                for k in range(QT):
                    dve.tensor_tensor(hot_a[:, k, :, :], hif[:, k, :].unsqueeze(2).broadcast_to([P, E1, RA]),
                                      iota[:, :, 0:RA], ALU.is_equal)
                    ins = dve.tensor_tensor(bb[:, k, :, :], lof[:, k, :].unsqueeze(2).broadcast_to([P, E1, RB]), iota,
                                            ALU.is_equal)
                ins.then_inc(compared, 1)

            def hidden(b, f):
                dve.wait_ge(sil_ready, KF * b + f + 1)
                if not (isinstance(b, int) and b == 0 and f < 2):
                    dve.wait_ge(gt_lo_ready, KF * b + f - 1)
                dve.tensor_tensor(gt[:, f % 2, :], ps[:, UP + f % 2, S:2 * S], sil[:, f % 2, :], ALU.mult).then_inc(gt_ready, 1)

            def residual(b):
                dve.wait_ge(out_ready, b + 1)
                if not (isinstance(b, int) and b == 0):
                    dve.wait_ge(base_out, 16 * b)
                dve.scalar_tensor_tensor(base[:, :, :], ps[:, OUT, :].rearrange("p (k d) -> p k d", k=QT),
                                         g.tg[:, 3:4], g.x[:, ds(2 * b, 2), :], ALU.mult, ALU.add).then_inc(base_ready, 1)

            normalise(0, 0, 0)
            pick(0)
            normalise(1, 0, 1)
            ranks_to_digits(0, 0)
            slots(0)

            def body(b, i, s):
                last = isinstance(b, int) and b == B - 1
                hidden(b, 0)
                hidden(b, 1)
                ch.resume(b, 10)
                weigh(b, i, s)
                ch.end()
                if not (isinstance(b, int) and b == 0):
                    residual(b - 1)
                if not last:
                    pick(b + 1)
                hidden(b, 2)
                hidden(b, 3)
                hidden(b, 4)
                hidden(b, 5)
                if not (isinstance(b, int) and b >= B - 2):
                    normalise(b + 2, i + 1, s)
                if not last:
                    ranks_to_digits(b + 1, 1 - s)
                    slots(b + 1)
                else:
                    own_columns()

            def own_columns():
                dve.wait_ge(hot_used, B)
                for i in range(4):
                    dve.tensor_copy(tt[32 * i:32 * i + 32, :, :],
                                    ps[32 * i:32 * i + 32, LIST:LIST + 2, :].rearrange("p n (g c) -> p (n g) c", c=4 * RB)[
                                        :, :, i * RB:(i + 1) * RB]).then_inc(tt_ready, 1)

            steps(dve, B, body)
            residual(B - 1)
            ct = Chain(dve, tchain, 4)
            dve.wait_ge(pair_in, 16)
            ct.link(dve.tensor_scalar(tok[:, 0, :], pair[:, 1, :], 0.0, float(P), ALU.is_equal, ALU.mult))
            dve.tensor_scalar(tok[:, 1, :], pair[:, 1, :], 0.0, None, ALU.is_equal)
            ct.link(dve.scalar_tensor_tensor(tok[:, 2, :], pair[:, 1, :], float(P), pair[:, 0, :], ALU.mult, ALU.add))
            dve.scalar_tensor_tensor(tok[:, 2, :], tok[:, 2, :], -float(P), tok[:, 0, :], ALU.add, ALU.add)
            ct.link(dve.tensor_tensor(tok[:, 1, :], tok[:, 1, :], g.iota_slot[0:E1, :], ALU.mult))
            ct.link(dve.tensor_tensor(tok[:, 2, :], tok[:, 2, :], tok[:, 1, :], ALU.add))
            ct.end()
            dve.tensor_copy(tok[:, 1, :], tok[:, 2, :]).then_inc(tok_ready, 1)
            dve.wait_ge(tok_turned, 1)
            dve.tensor_copy(g.list_a[:, :], ps[:, TURN, 0:E1])
            dve.tensor_copy(g.list_b[:, :], ps[0:CAPX, TURN, E1:2 * E1])

        @block.scalar
        def _(act):
            root_of_variance(act, g, 3)

            def keep_yt(b, s):
                act.wait_ge(yt_turned, b + 1)
                if not (isinstance(b, int) and b < 2):
                    act.wait_ge(up_ready, KF * (b - 1))
                turned = ps[:, TURN, :].rearrange("p (k q) -> p k q", k=2)
                act.activation(yt[:, s, :, :], turned, ACT.Copy).then_inc(yt_ready, 1)
                act.activation(yt_hi[:, s, :, :], turned, ACT.Copy).then_inc(hi_ready, 1)

            def exps(b):
                act.wait_ge(neg_ready, b + 1)
                if not (isinstance(b, int) and b < 1):
                    act.wait_ge(wrow_ready, b)
                for k in range(QT):
                    act.activation(ex[:, k, :], lg[:, k, :], ACT.Exp, bias=neg[:, k:k + 1], accum_out=total[:, k:k + 1]
                                   ).then_inc(ex_ready, 1)

            def silu(b, f):
                act.wait_ge(up_ready, KF * b + f + 1)
                if not (isinstance(b, int) and b == 0 and f < 2):
                    act.wait_ge(gt_ready, KF * b + f - 1)
                act.activation(sil[:, f % 2, :], ps[:, UP + f % 2, 0:S], ACT.Silu).then_inc(sil_ready, 1)

            def round_hidden(b, s, f):
                act.wait_ge(gt_ready, KF * b + f + 1)
                if f == 0 and not (isinstance(b, int) and b < 2):
                    act.wait_ge(out_ready, b - 1)
                act.activation(gt_hi[:, s, f, :], gt[:, f % 2, :], ACT.Copy).then_inc(gt_hi_ready, 1)

            def places(b, k):
                if k == 0:
                    act.wait_ge(compared, b + 1)
                    apart(act)
                act.activation(aa[:, k, :, 0:RA], hot_a[:, k, :, :], ACT.Copy, scale=g.iota_p[:, 0:1])
                act.activation(aa[:, k, :, RA:2 * RA], hot_a[:, k, :, :], ACT.Copy, scale=g.iota_t[:, ds(2 * b + k, 1)]
                               ).then_inc(hot_ready, 1)

            act.wait_ge(zeroed, 4)
            keep_yt(0, 0)
            exps(0)

            def body(b, i, s):
                last = isinstance(b, int) and b == B - 1
                silu(b, 0)
                if not last:
                    keep_yt(b + 1, 1 - s)
                silu(b, 1)
                round_hidden(b, s, 0)
                places(b, 0)
                for f in range(2, KF):
                    silu(b, f)
                    round_hidden(b, s, f - 1)
                    if f == 2:
                        places(b, 1)
                round_hidden(b, s, KF - 1)
                if not last:
                    exps(b + 1)

            steps(act, B, body)

        @block.tensor
        def _(pe):
            pe.wait_ge(zeroed, 4)
            for n in range(2):
                pe.matmul(ps[:, LIST + n, :], g.ones_bf[:, :], zero[:, :], start=True, stop=False, skip_group_check=True)

            def turn(b, s):
                pe.wait_ge(y_ready, b + 1)
                if not (isinstance(b, int) and b == 0):
                    pe.wait_ge(hi_ready, b)
                for d in range(2):
                    for k in range(QT):
                        ins = pe.transpose(ps[:, TURN, d * S + k * P:d * S + (k + 1) * P], y[:, s, k, d * P:(d + 1) * P],
                                           g.ident[:, :])
                ins.then_inc(yt_turned, 1)

            def logits(b, s):
                pe.wait_ge(yt_ready, b + 1)
                if not (isinstance(b, int) and b == 0):
                    pe.wait_ge(neg_ready, b)
                for k in range(QT):
                    for d in range(2):
                        ins = pe.matmul(ps[:, LOGIT, k * E1:(k + 1) * E1], yt[:, s, d, k * P:(k + 1) * P], wg[:, d, :],
                                        start=(d == 0), stop=(d == 1))
                ins.then_inc(lg_ready, 1)

            def ranks(b, s):
                pe.wait_ge(maskb_ready, b + 1)
                if not (isinstance(b, int) and b == 0):
                    pe.wait_ge(hot_ready, 2 * b)
                for k in range(QT):
                    o = ps[:, RANK, k * E1:(k + 1) * E1]
                    pe.matmul(o, g.ones_bf[:, :], seen[:, s, :], start=True, stop=False)
                    if k == 1:
                        pe.matmul(o, g.ones_bf[:, :], maskb[:, 0, :], start=False, stop=False)
                    ins = pe.matmul(o, g.tri[:, :], maskb[:, k, :], start=False, stop=True)
                ins.then_inc(rank_ready, 1)

            def lists(b):
                pe.wait_ge(hot_ready, 2 * b + 2)
                for k in range(QT):
                    for q in range(E1 // 4):
                        ins = pe.matmul(ps[:, LIST + q // 8, (q % 8) * 4 * RB:(q % 8 + 1) * 4 * RB],
                                        aa[:, k, 4 * q:4 * q + 4, :], bb[:, k, 4 * q:4 * q + 4, :],
                                        start=False, stop=True, skip_group_check=True)
                ins.then_inc(hot_used, 1)

            def up(b, s, f):
                if f == 0:
                    pe.wait_ge(lo_ready, b + 1)
                if not (isinstance(b, int) and b == 0 and f < 2):
                    pe.wait_ge(gt_ready, KF * b + f - 1)
                for c, m in ((0, KF + f), (S, f)):
                    for d in range(2):
                        ins = split_matmul(pe, ps[:, UP + f % 2, c:c + S], [w[:, d, m * P:(m + 1) * P] for w in sw1],
                                           (yt_hi[:, s, d, :], yt_lo[:, s, d, :]), d == 0, d == 1)
                ins.then_inc(up_ready, 1)

            def down(b, s):
                pe.wait_ge(gt_lo_ready, KF * b + KF)
                if not (isinstance(b, int) and b == 0):
                    pe.wait_ge(base_ready, b)
                for k in range(QT):
                    for f in range(KF):
                        ins = split_matmul(pe, ps[:, OUT, k * D:(k + 1) * D],
                                           [g_[:, s, f, k * P:(k + 1) * P] for g_ in (gt_hi, gt_lo)],
                                           [w[:, f, :] for w in sw2], f == 0, f == KF - 1)
                ins.then_inc(out_ready, 1)

            turn(0, 0)
            logits(0, 0)
            ranks(0, 0)

            def body(b, i, s):
                last = isinstance(b, int) and b == B - 1
                up(b, s, 0)
                if not last:
                    turn(b + 1, 1 - s)
                up(b, s, 1)
                if not (isinstance(b, int) and b == 0):
                    down(b - 1, 1 - s)
                if not last:
                    logits(b + 1, 1 - s)
                up(b, s, 2)
                up(b, s, 3)
                lists(b)
                up(b, s, 4)
                if not last:
                    ranks(b + 1, 1 - s)
                up(b, s, 5)

            steps(pe, B, body)
            down(B - 1, (B - 1) % 2)
            pe.wait_ge(tok_ready, 1)
            pe.wait_ge(hi_ready, B)
            pe.transpose(ps[:, TURN, 0:E1], tok[:, 1, 0:P], g.ident[0:E1, 0:E1])
            pe.transpose(ps[0:CAPX, TURN, E1:2 * E1], tok[:, 1, P:CAP], g.ident[0:E1, 0:E1]).then_inc(tok_turned, 1)


def experts(nc, g, a):
    with ExitStack() as ctx:
        def sb(name, shape, dt=F32):
            return ctx.enter_context(nc.sbuf_tensor(name, shape, dt))

        def sem(name):
            return ctx.enter_context(nc.semaphore(name))

        W1 = 2 * 2 * FF
        HF = KF // 2
        w1 = [g.wring[:, s, 0:W1].rearrange("p (k f) -> p k f", k=2) for s in range(RING)]
        w2 = [g.wring[:, s, W1:WCOLS].rearrange("p (k d) -> p k d", k=KF) for s in range(RING)]
        rows_a = sb("rows_a", [P, RING], U32)
        rows_b = sb("rows_b", [CAPX, RING], U32)
        to_a = sb("to_a", [P, 2], U32)
        to_b = sb("to_b", [CAPX, 2], U32)
        xa = sb("xa", [P, RING, ROW])
        xb = sb("xb", [CAPX, RING, ROW])
        wa = sb("wa", [P, RING])
        wb = sb("wb", [CAPX, RING])
        xt = sb("xt", [P, 2, 2, CAP])
        sil = sb("sil3", [P, 2, HF, CAP])
        gt = sb("gt3", [P, 2, KF, CAP])
        zt = sb("zt", [P, 2, 2, CAP])
        za = sb("za", [P, 2, D])
        zb = sb("zb", [CAPX, 2, D])
        names = ("x_rows", "x_turned", "x_ready", "x_weights", "x_up", "x_sil", "x_gt", "x_down", "x_zt", "x_zturned",
                 "x_z", "x_added")
        (rows_ready, turned, xt_ready, weights_kept, up_ready, sil_ready, gt_ready, down_ready, zt_ready, z_turned,
         z_ready, added) = [sem(n) for n in names]
        gathered = [sem(f"gathered{s}") for s in range(RING)]
        to_ready = sem("x_to")
        AHEAD = 3
        ps = g.ps
        UP, DOWN, BACK, TURN = 0, 4, 5, 6
        block = ctx.enter_context(nc.Block())

        @block.sync
        def _(sp):
            def load(e, i, s):
                if isinstance(e, int) and e < RING:
                    if e == 2:
                        load_expert(sp, g, a, e)
                    return
                sp.wait_ge(down_ready, e - RING + 1)
                apart(sp)
                for c in range(PARTS):
                    if 1 <= c <= 2:
                        sp.wait_ge(up_ready, 2 * (e - RING + 2) + c)
                        apart(sp)
                    n = slice(c * WCOLS // PARTS, (c + 1) * WCOLS // PARTS)
                    sp.dma_start(g.wring[:, s, n], a["experts"][ds(e, 1), :, n].rearrange("o p n -> p (o n)")
                                 ).then_inc(g.w_loaded[s], 16)

            steps(sp, E1, load, RING)

        @block.gpsimd
        def _(pool):
            def gather(e, i, s):
                if not (isinstance(e, int) and e < RING):
                    pool.wait_ge(turned, e - RING + 1)
                    apart(pool)
                    pool.wait_ge(weights_kept, e - RING + 1)
                    apart(pool)
                nc.gpsimd.tensor_copy(rows_a[:, s:s + 1], g.list_a[:, ds(e, 1)]).then_inc(rows_ready, 1)
                nc.gpsimd.tensor_copy(rows_b[:, s:s + 1], g.list_b[:, ds(e, 1)]).then_inc(rows_ready, 1)
                pool.wait_ge(rows_ready, 2 * e + 2)
                apart(pool)
                pool.indirect_dma_start(xa[:, s, :], None, g.table,
                                        bass.IndirectOffsetOnAxis(ap=rows_a[:, s:s + 1], axis=0)).then_inc(gathered[s], 16)
                pool.indirect_dma_start(xb[:, s, :], None, g.table,
                                        bass.IndirectOffsetOnAxis(ap=rows_b[:, s:s + 1], axis=0)).then_inc(gathered[s], 16)

            def add(e, s):
                if not (isinstance(e, int) and e < 2):
                    pool.wait_ge(added, 32 * (e - 1))
                    apart(pool)
                nc.gpsimd.tensor_copy(to_a[:, s % 2:s % 2 + 1], g.list_a[:, ds(e, 1)]).then_inc(to_ready, 1)
                nc.gpsimd.tensor_copy(to_b[:, s % 2:s % 2 + 1], g.list_b[:, ds(e, 1)]).then_inc(to_ready, 1)
                pool.wait_ge(to_ready, 2 * e + 2)
                apart(pool)
                pool.wait_ge(z_ready, e + 1)
                apart(pool)
                if not (isinstance(e, int) and e == 0):
                    pool.wait_ge(added, 32 * e)
                    apart(pool)
                pool.indirect_dma_start(a["out"], bass.IndirectOffsetOnAxis(ap=to_a[:, s % 2:s % 2 + 1], axis=0),
                                        za[:, s % 2, :], None, compute_op=ALU.add).then_inc(added, 16)
                pool.indirect_dma_start(a["out"], bass.IndirectOffsetOnAxis(ap=to_b[:, s % 2:s % 2 + 1], axis=0),
                                        zb[:, s % 2, :], None, compute_op=ALU.add).then_inc(added, 16)

            for e in range(AHEAD):
                gather(e, 0, e)

            def body(e, i, s):
                if not (isinstance(e, int) and e >= E1 - AHEAD):
                    gather(e + AHEAD, i + (s + AHEAD) // RING, (s + AHEAD) % RING)
                if not (isinstance(e, int) and e < 2):
                    add(e - 2, (s - 2) % RING)

            steps(pool, E1, body, RING)
            add(E1 - 2, (E1 - 2) % RING)
            add(E1 - 1, (E1 - 1) % RING)
            pool.wait_ge(added, 32 * E1)

        @block.vector
        def _(dve):
            def keep_weights(e, i, s):
                dve.wait_ge(gathered[s], 32 * (i + 1))
                if not (isinstance(e, int) and e < RING):
                    dve.wait_ge(z_ready, e - RING + 1)
                apart(dve)
                dve.tensor_copy(wa[:, s:s + 1], xa[:, s, ds(e + D, 1)])
                dve.tensor_copy(wb[:, s:s + 1], xb[:, s, ds(e + D, 1)]).then_inc(weights_kept, 1)

            def hidden(e, s, h):
                dve.wait_ge(sil_ready, 2 * e + h + 1)
                if h == 0 and not (isinstance(e, int) and e < 2):
                    dve.wait_ge(down_ready, e - 1)
                dve.tensor_tensor(gt[:, s % 2, h * HF:(h + 1) * HF, :],
                                  ps[:, UP + 2 * h + 1, 0:HF * CAP].rearrange("p (f c) -> p f c", c=CAP),
                                  sil[:, h, :, :], ALU.mult).then_inc(gt_ready, 1)

            def scale(e, s):
                dve.wait_ge(z_turned, e + 1)
                dve.wait_ge(weights_kept, e + 1)
                if not (isinstance(e, int) and e < 2):
                    dve.wait_ge(added, 32 * (e - 1))
                dve.tensor_scalar(za[:, s % 2, :], ps[:, BACK, 0:D], wa[:, s:s + 1], None, ALU.mult)
                dve.tensor_scalar(zb[:, s % 2, :], ps[0:CAPX, BACK, D:2 * D], wb[:, s:s + 1], None, ALU.mult).then_inc(z_ready, 1)

            def body(e, i, s):
                keep_weights(e, i, s)
                hidden(e, s, 0)
                if not (isinstance(e, int) and e < 2):
                    scale(e - 2, (s - 2) % RING)
                hidden(e, s, 1)

            steps(dve, E1, body, RING)
            scale(E1 - 2, (E1 - 2) % RING)
            scale(E1 - 1, (E1 - 1) % RING)

        @block.scalar
        def _(act):
            def keep_xt(e, s):
                act.wait_ge(turned, e + 1)
                if not (isinstance(e, int) and e < 2):
                    act.wait_ge(up_ready, 2 * (e - 1))
                act.activation(xt[:, s % 2, :, :], ps[:, TURN, 0:2 * CAP].rearrange("p (k c) -> p k c", k=2), ACT.Copy
                               ).then_inc(xt_ready, 1)

            def silu(e, h):
                act.wait_ge(up_ready, 2 * e + h + 1)
                if not (isinstance(e, int) and e == 0):
                    act.wait_ge(gt_ready, 2 * e + h - 1)
                act.activation(sil[:, h, :, :], ps[:, UP + 2 * h, 0:HF * CAP].rearrange("p (f c) -> p f c", c=CAP), ACT.Silu
                               ).then_inc(sil_ready, 1)

            def keep_zt(e, s):
                act.wait_ge(down_ready, e + 1)
                if not (isinstance(e, int) and e < 2):
                    act.wait_ge(z_turned, e - 1)
                act.activation(zt[:, s % 2, :, :], ps[:, DOWN, 0:2 * CAP].rearrange("p (k c) -> p k c", k=2), ACT.Copy
                               ).then_inc(zt_ready, 1)

            keep_xt(0, 0)

            def body(e, i, s):
                silu(e, 0)
                if not (isinstance(e, int) and e == E1 - 1):
                    keep_xt(e + 1, (s + 1) % RING)
                silu(e, 1)
                if not (isinstance(e, int) and e == 0):
                    keep_zt(e - 1, (s - 1) % RING)

            steps(act, E1, body, RING)
            keep_zt(E1 - 1, (E1 - 1) % RING)

        @block.tensor
        def _(pe):
            def turn(e, i, s):
                pe.wait_ge(gathered[s], 32 * (i + 1))
                if not (isinstance(e, int) and e == 0):
                    pe.wait_ge(xt_ready, e)
                for k in range(2):
                    pe.transpose(ps[:, TURN, k * CAP:k * CAP + P], xa[:, s, k * P:(k + 1) * P], g.ident[:, :])
                    ins = pe.transpose(ps[:, TURN, k * CAP + P:(k + 1) * CAP], xb[:, s, k * P:(k + 1) * P],
                                       g.ident[0:CAPX, 0:CAPX])
                ins.then_inc(turned, 1)

            def up(e, i, s, h):
                if h == 0:
                    pe.wait_ge(xt_ready, e + 1)
                    pe.wait_ge(g.w_loaded[s], 16 * PARTS * (i + 1))
                if not (isinstance(e, int) and e == 0):
                    pe.wait_ge(gt_ready, 2 * e + h - 1)
                for n, m in ((0, KF), (1, 0)):
                    for f in range(HF):
                        c = (m + h * HF + f) * P
                        for d in range(2):
                            ins = pe.matmul(ps[:, UP + 2 * h + n, f * CAP:(f + 1) * CAP], w1[s][:, d, c:c + P],
                                            xt[:, s % 2, d, :], start=(d == 0), stop=(d == 1))
                ins.then_inc(up_ready, 1)

            def down(e, s):
                pe.wait_ge(gt_ready, 2 * e + 2)
                if not (isinstance(e, int) and e == 0):
                    pe.wait_ge(zt_ready, e)
                for d in range(2):
                    for f in range(KF):
                        ins = pe.matmul(ps[:, DOWN, d * CAP:(d + 1) * CAP], w2[s][:, f, d * P:(d + 1) * P],
                                        gt[:, s % 2, f, :], start=(f == 0), stop=(f == KF - 1))
                ins.then_inc(down_ready, 1)

            def turn_back(e, s):
                pe.wait_ge(zt_ready, e + 1)
                if not (isinstance(e, int) and e == 0):
                    pe.wait_ge(z_ready, e)
                for d in range(2):
                    pe.transpose(ps[:, BACK, d * P:(d + 1) * P], zt[:, s % 2, d, 0:P], g.ident[:, :])
                    ins = pe.transpose(ps[0:CAPX, BACK, D + d * P:D + (d + 1) * P], zt[:, s % 2, d, P:CAP], g.ident[:, :])
                ins.then_inc(z_turned, 1)

            turn(0, 0, 0)

            def body(e, i, s):
                up(e, i, s, 0)
                if not (isinstance(e, int) and e < 2):
                    turn_back(e - 2, (s - 2) % RING)
                if not (isinstance(e, int) and e == E1 - 1):
                    turn(e + 1, i + (s + 1) // RING, (s + 1) % RING)
                up(e, i, s, 1)
                if not (isinstance(e, int) and e == 0):
                    down(e - 1, (s - 1) % RING)

            steps(pe, E1, body, RING)
            turn_back(E1 - 2, (E1 - 2) % RING)
            down(E1 - 1, (E1 - 1) % RING)
            turn_back(E1 - 1, (E1 - 1) % RING)


def program(nc, a):
    with ExitStack() as ctx:
        def sb(name, shape, dt=F32):
            return ctx.enter_context(nc.sbuf_tensor(name, shape, dt))

        g = Shared()
        g.ps = ctx.enter_context(nc.psum_tensor("ps", [P, 8, 512], F32))
        g.x = sb("x_state", [P, T, D])
        g.st = sb("st", [P, T, 6])
        g.mv = sb("mv", [P, T, 2])
        g.rstd = sb("rstd", [P, T])
        g.ident = sb("ident", [P, P])
        g.tri = sb("tri", [P, P], BF16)
        g.ones_bf = sb("ones_bf", [P, P], BF16)
        g.ones_f = sb("ones_f", [1, P])
        g.iota8 = sb("iota8", [P, E0])
        g.iota_b = sb("iota_b", [P, RB])
        g.iota_p = sb("iota_p", [P, 1])
        g.iota_t = sb("iota_t", [P, T])
        g.iota_slot = sb("iota_slot", [P, CAP])
        g.maskcol = sb("maskcol", [P, QT, B])
        g.bm0 = sb("bm0", [P, QT, B])
        g.tg = sb("tg", [P, 4])
        g.wring = sb("wring", [P, RING, WCOLS])
        g.var_eps, g.rooted, g.scale_ready = [ctx.enter_context(nc.semaphore(n)) for n in ("var_eps", "rooted", "scale_ready")]
        g.w_loaded = [ctx.enter_context(nc.semaphore(f"w_loaded{k}")) for k in range(RING)]
        g.pen_dram = nc.dram_tensor("pen_dram", [B + 2, S], BF16).ap()
        g.k_dram = nc.dram_tensor("k_dram", [2, 3, D, S], BF16).ap()
        g.q_dram = nc.dram_tensor("q_dram", [2, 3, D, S], BF16).ap()
        g.bm_dram = nc.dram_tensor("bm_dram", [B, 2, 4, S], F32).ap()
        g.ew = g.wring[:, 0, 0:2 * E0 * D]
        g.w_tgt = g.wring[:, 1, 0:2 * D]
        g.w_src = g.wring[:, 1, 2 * D:10 * D]
        g.w_out = g.wring[:, 1, 10 * D:14 * D]
        g.sw = g.wring[:, 2, :]
        g.eb, g.rw, g.rb = sb("eb", [E0, D])[:, :], sb("rw", [P, 2 * E0])[:, :], sb("rb", [1, E0])[:, :]
        g.b_tgt, g.b_key = sb("b_tgt", [P, 2])[:, :], sb("b_key", [P, 2])[:, :]
        g.b_val, g.b_out, g.wg = sb("b_val", [P, D])[:, :], sb("b_out", [P, D])[:, :], sb("wg", [P, 2 * E1])[:, :]
        with ExitStack() as padded:
            g.qpad, g.kz, g.kzb, g.vraw, g.vaug = [padded.enter_context(nc.sbuf_tensor(*t)) for t in (
                ("qpad", [P, 2, QT, H0, 32], F32), ("kz", [P, 2, H0, S], F32), ("kzb", [P, 2, H0, S], BF16),
                ("vraw", [P, 2, QT, D], F32), ("vaug", [P, 2, QT, H0, 32], F32))]
            g.kv_loaded = [padded.enter_context(nc.semaphore(f"kv_loaded{s}")) for s in (0, 1)]
            g.kb_loaded = [padded.enter_context(nc.semaphore(f"kb_loaded{s}")) for s in (0, 1)]
            setup(nc, g, a)
            attn0(nc, g, a)
        g.sw_hi = sb("sw_hi", [P, WCOLS], F32R)[:, :]
        g.sw_lo = sb("sw_lo", [P, WCOLS], F32R)[:, :]
        ffn0(nc, g, a)
        attn1(nc, g, a)
        g.list_a = sb("list_a", [P, E1], U32)
        g.list_b = sb("list_b", [CAPX, E1], U32)
        g.table = nc.dram_tensor("table", [NT + CAP, ROW], F32).ap()
        g.lists = nc.dram_tensor("lists", [E1, 2, CAP], F32).ap()
        route(nc, g, a)
        experts(nc, g, a)

def lay_out(inputs):
    import numpy as np
    n = {k: np.asarray(v) for k, v in inputs.items()}
    E, F2, H = n["L1_ffn_expert_w1"].shape
    F = F2 // 2

    def rows(w):
        k = w.shape[-2] // 128
        return np.swapaxes(w.reshape(*w.shape[:-2], k, 128, w.shape[-1]), -3, -2).reshape(
            *w.shape[:-2], 128, k * w.shape[-1])

    def everywhere(v, shape):
        return np.broadcast_to(v, shape)

    out = {
        "x": n["x"].reshape(2048, 256),
        "ctx": n["ctx_2048"],
        "ctx_t": n["ctx_2048"].transpose(0, 2, 1),
        "seq": everywhere(n["itok_Bx1_68_817"].reshape(1, 8), (128, 8)),
        "b": n["L0_xattn_b"].reshape(2, 128).T,
        "gates": everywhere(np.stack([n["g_xattn"][0], n["g_ffn"][0], n["g_xattn"][1], n["g_ffn"][1]]).reshape(1, 4), (128, 4)),
        "maskcol": n["mask_BxS2_fk1"].reshape(8, 2, 128).transpose(2, 1, 0),
        "maskrow": n["mask_BxS2_fk1"].reshape(1, 2048),
        "router_w": rows(n["L0_ffn_router_w"]),
        "router_b": n["L0_ffn_router_b"].reshape(1, 8),
        "ew0": n["L0_ffn_expert_w"].reshape(8, 2, 128, 256).transpose(2, 1, 0, 3).reshape(128, 4096),
        "eb0": n["L0_ffn_expert_b"],
        "w_tgt": rows(n["L1_xattn_W_tgt"].T),
        "w_src": rows(n["L1_xattn_W_src"].T),
        "w_out": rows(n["L1_xattn_W_out"].T),
        "b_tgt": n["L1_xattn_b_tgt"].reshape(2, 128).T,
        "b_key": n["L1_xattn_b_src"][:256].reshape(2, 128).T,
        "b_val": everywhere(n["L1_xattn_b_src"][256:].reshape(1, 256), (128, 256)),
        "b_out": everywhere(n["L1_xattn_b_out"].reshape(1, 256), (128, 256)),
        "wg": rows(n["L1_ffn_wg"].T),
        "shared": np.concatenate([rows(n["L1_ffn_shared_w1"].T), rows(n["L1_ffn_shared_w2"].T)], axis=1),
        "experts": np.concatenate([rows(n["L1_ffn_expert_w1"].transpose(0, 2, 1)),
                                   rows(n["L1_ffn_expert_w2"].transpose(0, 2, 1))], axis=2),
    }
    return {k: np.ascontiguousarray(v) for k, v in out.items()}


def kernel(**inputs):
    import concourse.bacc as _bacc
    from concourse import mybir as _mybir
    from concourse.bass_utils import run_bass_kernel_spmd as _run

    nc = _bacc.Bacc("TRN2", target_bir_lowering=False, num_devices=1)
    arrays = lay_out(inputs)
    aps = {k: nc.dram_tensor("in_" + k, v.shape, _mybir.dt.from_np(v.dtype), kind="ExternalInput").ap()
           for k, v in arrays.items()}
    aps["out"] = nc.dram_tensor("out", (NT + CAP, D), F32, kind="ExternalOutput").ap()
    program(nc, aps)
    r = _run(nc, [{"in_" + k: v for k, v in arrays.items()}], core_ids=[0])
    return r.results[0]["out"][0:NT].reshape(B, S, D)
```
